# Optimizing a Trainium2 kernel written in Bass

```python
import numpy as np
import jax
import jax.numpy as jnp

def _softmax(x, axis=-1):
    return jax.nn.softmax(x, axis=axis)

def _gelu(x):
    return jax.nn.gelu(x, approximate=True)

def _silu(x):
    return jax.nn.silu(x)

def _sigmoid(x):
    return jax.nn.sigmoid(x)

def _layernorm(x, axis=-1, eps=1e-05):
    m = jnp.mean(x, axis=axis, keepdims=True)
    v = jnp.var(x, axis=axis, keepdims=True)
    return (x - m) / jnp.sqrt(v + eps)

def _scatter_add(tgt, idx, src, axis=0):
    return tgt.at[idx].add(src)

def _segment_sum(src, seg, n):
    return jax.ops.segment_sum(src, seg, n)
kernel_name = 'mk_decoder_postln_d1_seqx_r4_7a6ce6'

def setup_inputs(seed: int=0):
    np.random.seed(seed)
    _w = jnp.asarray

    def _rec_inputs():
        import jax
        import jax.numpy as jnp
        _rk = jax.random.key(seed)
        x = -0.0003929 + 0.9999 * jax.random.normal(jax.random.fold_in(_rk, 1), (4, 512, 256), jnp.float32)
        _lenS = 512 - jax.random.randint(jax.random.fold_in(_rk, 7), (4,), 0, max(1, 512 // 4) + 1, jnp.int32)
        _lenS2 = 512 - jax.random.randint(jax.random.fold_in(_rk, 8), (4,), 0, max(1, 512 // 4) + 1, jnp.int32)
        _ctx_1024P = jax.random.normal(jax.random.fold_in(_rk, 11), (4, 16, 256), jnp.float32)
        _ctx_1024c = jax.random.dirichlet(jax.random.fold_in(_rk, 511), 0.3 * jnp.ones((16,), jnp.float32), (4, 512))
        _ctx_1024t = jnp.einsum('bsk,bkd->bsd', _ctx_1024c, _ctx_1024P)
        _ctx_1024t = _ctx_1024t * jax.lax.rsqrt(jnp.mean(jnp.square(_ctx_1024t)) + 1e-12) * 0.953939
        ctx_1024 = 2.81802e-05 + 1.00001 * (_ctx_1024t + 0.3 * jax.random.normal(jax.random.fold_in(_rk, 611), (4, 512, 256), jnp.float32))
        return (x, ctx_1024)
    x, ctx_1024 = _rec_inputs()

    def _L0_attn_setup():
        import jax, jax.numpy as jnp
        import numpy as np
        D = 256
        B, S = (4, 512)
        key = jax.random.key(seed)
        ks = jax.random.split(key, 9)
        std = 1.0 / np.sqrt(D)
        x = jax.random.normal(ks[0], (B, S, D), dtype=jnp.float32)
        Wq = jax.random.normal(ks[1], (D, D), dtype=jnp.float32) * std
        bq = jax.random.normal(ks[2], (D,), dtype=jnp.float32) * std
        Wk = jax.random.normal(ks[3], (D, D), dtype=jnp.float32) * std
        bk = jax.random.normal(ks[4], (D,), dtype=jnp.float32) * std
        Wv = jax.random.normal(ks[5], (D, D), dtype=jnp.float32) * std
        bv = jax.random.normal(ks[6], (D,), dtype=jnp.float32) * std
        Wo = jax.random.normal(ks[7], (D, D), dtype=jnp.float32) * std
        bo = jax.random.normal(ks[8], (D,), dtype=jnp.float32) * std
        return {'x': x, 'Wq': Wq, 'bq': bq, 'Wk': Wk, 'bk': bk, 'Wv': Wv, 'bv': bv, 'Wo': Wo, 'bo': bo}
    _L0_attn_all = _L0_attn_setup()
    _L0_attn_in = {k: v for k, v in _L0_attn_all.items() if k in ('Wq', 'bq', 'Wk', 'bk', 'Wv', 'bv', 'Wo', 'bo')}
    del _L0_attn_all

    def _L0_xattn_setup():
        import jax, jax.numpy as jnp
        import numpy as np
        import math
        E = 256
        H = 16
        BS = 128
        G = 1
        D = E // H

        def _block_sparse_attn(Q, K, V):
            B, Hn, S, Dh = Q.shape
            nb = S // BS
            scale = 1.0 / math.sqrt(Dh)
            Qb = Q.reshape(B, Hn, nb, BS, Dh)
            Kb = K.reshape(B, Hn, nb, BS, Dh)
            Vb = V.reshape(B, Hn, nb, BS, Dh)
            loc_s = jnp.einsum('bhnqd,bhnkd->bhnqk', Qb, Kb) * scale
            loc_p = jax.nn.softmax(loc_s, axis=-1)
            out = jnp.einsum('bhnqk,bhnkd->bhnqd', loc_p, Vb)
            offs = jnp.arange(-G, G + 1)
            win = jnp.arange(nb)[:, None] + offs[None, :]
            valid = (win >= 0) & (win < nb)
            winc = jnp.clip(win, 0, nb - 1)
            W = 2 * G + 1
            Kw = Kb[:, :, winc].reshape(B, Hn, nb, W * BS, Dh)
            Vw = Vb[:, :, winc].reshape(B, Hn, nb, W * BS, Dh)
            cross_s = jnp.einsum('bhnqd,bhnkd->bhnqk', Qb, Kw) * scale
            kmask = jnp.repeat(valid, BS, axis=-1)
            cross_s = jnp.where(kmask[None, None, :, None, :], cross_s, -jnp.inf)
            cross_p = jax.nn.softmax(cross_s, axis=-1)
            out = out + jnp.einsum('bhnqk,bhnkd->bhnqd', cross_p, Vw)
            return out.reshape(B, Hn, S, Dh)
        key = jax.random.key(seed)
        ks = jax.random.split(key, 12)
        s = 1.0 / math.sqrt(E)
        inp = {'q': jax.random.normal(ks[0], (4, 1024, E), jnp.float32), 'k': jax.random.normal(ks[1], (4, 1024, E), jnp.float32), 'v': jax.random.normal(ks[2], (4, 1024, E), jnp.float32), 'Wq': jax.random.uniform(ks[3], (E, E), jnp.float32, -s, s), 'bq': jax.random.uniform(ks[4], (E,), jnp.float32, -s, s), 'Wk': jax.random.uniform(ks[5], (E, E), jnp.float32, -s, s), 'bk': jax.random.uniform(ks[6], (E,), jnp.float32, -s, s), 'Wv': jax.random.uniform(ks[7], (E, E), jnp.float32, -s, s), 'bv': jax.random.uniform(ks[8], (E,), jnp.float32, -s, s), 'Wo': jax.random.uniform(ks[9], (E, E), jnp.float32, -s, s), 'bo': jax.random.uniform(ks[10], (E,), jnp.float32, -s, s)}
        return inp
    _L0_xattn_all = _L0_xattn_setup()
    _L0_xattn_in = {k: v for k, v in _L0_xattn_all.items() if k in ('Wq', 'bq', 'Wk', 'bk', 'Wv', 'bv', 'Wo', 'bo')}
    del _L0_xattn_all

    def _L0_ffn_setup():
        import jax, jax.numpy as jnp
        import numpy as np
        B, S, DIM = (4, 512, 256)
        E, K, HID = (8, 2, 1024)
        key = jax.random.key(seed)
        ks = jax.random.split(key, 8)
        init = lambda k, sh: jax.random.normal(k, sh, jnp.float32) * 0.02
        return {'x': jax.random.normal(ks[0], (B, S, DIM), jnp.float32), 'gate_w': init(ks[1], (DIM, E)), 'gate_b': jnp.zeros((E,), jnp.float32), 'w1': init(ks[2], (E, DIM, HID)), 'b1': jnp.zeros((E, HID), jnp.float32), 'w2': init(ks[3], (E, HID, DIM)), 'b2': jnp.zeros((E, DIM), jnp.float32), 'ws1': init(ks[4], (DIM, HID)), 'bs1': jnp.zeros((HID,), jnp.float32), 'ws2': init(ks[5], (HID, DIM)), 'bs2': jnp.zeros((DIM,), jnp.float32)}
    _L0_ffn_all = _L0_ffn_setup()
    _L0_ffn_in = {k: v for k, v in _L0_ffn_all.items() if k in ('gate_w', 'gate_b', 'w1', 'b1', 'w2', 'b2', 'ws1', 'bs1', 'ws2', 'bs2')}
    del _L0_ffn_all
    return {'x': x, 'ctx_1024': ctx_1024, 'L0_attn_Wq': _L0_attn_in['Wq'], 'L0_attn_bq': _L0_attn_in['bq'], 'L0_attn_Wk': _L0_attn_in['Wk'], 'L0_attn_bk': _L0_attn_in['bk'], 'L0_attn_Wv': _L0_attn_in['Wv'], 'L0_attn_bv': _L0_attn_in['bv'], 'L0_attn_Wo': _L0_attn_in['Wo'], 'L0_attn_bo': _L0_attn_in['bo'], 'L0_xattn_Wq': _L0_xattn_in['Wq'], 'L0_xattn_bq': _L0_xattn_in['bq'], 'L0_xattn_Wk': _L0_xattn_in['Wk'], 'L0_xattn_bk': _L0_xattn_in['bk'], 'L0_xattn_Wv': _L0_xattn_in['Wv'], 'L0_xattn_bv': _L0_xattn_in['bv'], 'L0_xattn_Wo': _L0_xattn_in['Wo'], 'L0_xattn_bo': _L0_xattn_in['bo'], 'L0_ffn_gate_w': _L0_ffn_in['gate_w'], 'L0_ffn_gate_b': _L0_ffn_in['gate_b'], 'L0_ffn_w1': _L0_ffn_in['w1'], 'L0_ffn_b1': _L0_ffn_in['b1'], 'L0_ffn_w2': _L0_ffn_in['w2'], 'L0_ffn_b2': _L0_ffn_in['b2'], 'L0_ffn_ws1': _L0_ffn_in['ws1'], 'L0_ffn_bs1': _L0_ffn_in['bs1'], 'L0_ffn_ws2': _L0_ffn_in['ws2'], 'L0_ffn_bs2': _L0_ffn_in['bs2']}

def reference(x, ctx_1024, L0_attn_Wq, L0_attn_bq, L0_attn_Wk, L0_attn_bk, L0_attn_Wv, L0_attn_bv, L0_attn_Wo, L0_attn_bo, L0_xattn_Wq, L0_xattn_bq, L0_xattn_Wk, L0_xattn_bk, L0_xattn_Wv, L0_xattn_bv, L0_xattn_Wo, L0_xattn_bo, L0_ffn_gate_w, L0_ffn_gate_b, L0_ffn_w1, L0_ffn_b1, L0_ffn_w2, L0_ffn_b2, L0_ffn_ws1, L0_ffn_bs1, L0_ffn_ws2, L0_ffn_bs2):
    import jax
    import jax.numpy as jnp

    def _L0_attn_ref(x, Wq, bq, Wk, bk, Wv, bv, Wo, bo):
        import jax, jax.numpy as jnp
        import numpy as np
        D = 256
        B, S = (4, 512)
        d = x.shape[-1]
        q = x @ Wq + bq
        k = x @ Wk + bk
        v = x @ Wv + bv
        scale = 1.0 / jnp.sqrt(jnp.asarray(d, dtype=x.dtype))
        att = jnp.einsum('bqd,bkd->bqk', q, k) * scale
        sq, sk = (q.shape[1], k.shape[1])
        causal = jnp.triu(jnp.ones((sq, sk), dtype=bool), k=1)
        att = jnp.where(causal, -jnp.inf, att)
        att = jax.nn.softmax(att, axis=-1)
        out = jnp.einsum('bqk,bkd->bqd', att, v)
        return out @ Wo + bo

    def _L0_xattn_ref(q, k, v, Wq, bq, Wk, bk, Wv, bv, Wo, bo):
        import jax, jax.numpy as jnp
        import numpy as np
        import math
        E = 256
        H = 16
        BS = 128
        G = 1
        D = E // H

        def _block_sparse_attn(Q, K, V):
            B, Hn, S, Dh = Q.shape
            nb = S // BS
            scale = 1.0 / math.sqrt(Dh)
            Qb = Q.reshape(B, Hn, nb, BS, Dh)
            Kb = K.reshape(B, Hn, nb, BS, Dh)
            Vb = V.reshape(B, Hn, nb, BS, Dh)
            loc_s = jnp.einsum('bhnqd,bhnkd->bhnqk', Qb, Kb) * scale
            loc_p = jax.nn.softmax(loc_s, axis=-1)
            out = jnp.einsum('bhnqk,bhnkd->bhnqd', loc_p, Vb)
            offs = jnp.arange(-G, G + 1)
            win = jnp.arange(nb)[:, None] + offs[None, :]
            valid = (win >= 0) & (win < nb)
            winc = jnp.clip(win, 0, nb - 1)
            W = 2 * G + 1
            Kw = Kb[:, :, winc].reshape(B, Hn, nb, W * BS, Dh)
            Vw = Vb[:, :, winc].reshape(B, Hn, nb, W * BS, Dh)
            cross_s = jnp.einsum('bhnqd,bhnkd->bhnqk', Qb, Kw) * scale
            kmask = jnp.repeat(valid, BS, axis=-1)
            cross_s = jnp.where(kmask[None, None, :, None, :], cross_s, -jnp.inf)
            cross_p = jax.nn.softmax(cross_s, axis=-1)
            out = out + jnp.einsum('bhnqk,bhnkd->bhnqd', cross_p, Vw)
            return out.reshape(B, Hn, S, Dh)
        B, S, _ = q.shape

        def proj(x, Wm, bm):
            y = jnp.einsum('bse,fe->bsf', x, Wm) + bm
            return y.reshape(B, S, H, D).transpose(0, 2, 1, 3)
        Q = proj(q, Wq, bq)
        K = proj(k, Wk, bk)
        V = proj(v, Wv, bv)
        attn = _block_sparse_attn(Q, K, V)
        attn = attn.transpose(0, 2, 1, 3).reshape(B, S, E)
        return jnp.einsum('bse,fe->bsf', attn, Wo) + bo

    def _L0_ffn_ref(x, gate_w, gate_b, w1, b1, w2, b2, ws1, bs1, ws2, bs2):
        import jax, jax.numpy as jnp
        import numpy as np
        B, S, DIM = (4, 512, 256)
        E, K, HID = (8, 2, 1024)
        orig_shape = x.shape
        xf = x.reshape(-1, DIM)
        logits = xf @ gate_w + gate_b
        top_w, top_i = jax.lax.top_k(logits, K)
        gw = jax.nn.softmax(top_w, axis=-1).astype(xf.dtype)
        combine = (gw[:, :, None] * jax.nn.one_hot(top_i, E, dtype=xf.dtype)).sum(axis=1)
        out = jnp.zeros_like(xf)
        for e in range(E):
            h = jax.nn.gelu(xf @ w1[e] + b1[e], approximate=False)
            out = out + combine[:, e:e + 1] * (h @ w2[e] + b2[e])
        shared = jax.nn.gelu(xf @ ws1 + bs1, approximate=False) @ ws2 + bs2
        return (out + shared).reshape(orig_shape)
    x = _layernorm(x + _L0_attn_ref(x, L0_attn_Wq, L0_attn_bq, L0_attn_Wk, L0_attn_bk, L0_attn_Wv, L0_attn_bv, L0_attn_Wo, L0_attn_bo), axis=-1)
    x = _layernorm(x + _L0_xattn_ref(x, ctx_1024, ctx_1024, L0_xattn_Wq, L0_xattn_bq, L0_xattn_Wk, L0_xattn_bk, L0_xattn_Wv, L0_xattn_bv, L0_xattn_Wo, L0_xattn_bo), axis=-1)
    x = _layernorm(x + _L0_ffn_ref(x, L0_ffn_gate_w, L0_ffn_gate_b, L0_ffn_w1, L0_ffn_b1, L0_ffn_w2, L0_ffn_b2, L0_ffn_ws1, L0_ffn_bs1, L0_ffn_ws2, L0_ffn_bs2), axis=-1)
    return x

_drawn_inputs = setup_inputs


def setup_inputs(seed=0):
    import zlib

    import numpy as np

    out = dict(_drawn_inputs(seed))
    spreads = {'L0_ffn_gate_b': (0.0, 0.1),
     'L0_ffn_b1': (0.0, 0.311),
     'L0_ffn_b2': (0.0, 0.1),
     'L0_ffn_bs1': (0.0, 0.1),
     'L0_ffn_bs2': (0.0, 0.1)}
    factors = {'L0_attn_bq': 4.692, 'L0_attn_bk': 8.0, 'L0_xattn_bq': 8.0, 'L0_xattn_bk': 8.0}
    for name, (base, spread) in spreads.items():
        noise = np.random.default_rng([zlib.crc32(name.encode()), seed]).standard_normal(out[name].shape)
        drawn = base * np.exp(spread * noise) if base else spread * noise
        out[name] = jnp.asarray(drawn.astype(out[name].dtype))
    for name, factor in factors.items():
        out[name] = (out[name] * factor).astype(out[name].dtype)
    return out
```

```python
from contextlib import ExitStack

import concourse.bass as bass
from concourse import mybir

F = mybir.dt.float32
FR = mybir.dt.float32r
I32 = mybir.dt.int32
ACT = mybir.ActivationFunctionType
ALU = mybir.AluOpType
AX = mybir.AxisListType.X

P = 128
B, S, D = 4, 512, 256
T = B * S
NT = S // P
KD = D // P
E, HID = 8, 1024
NH = HID // P
HEADS, DH = 16, 16
HALF = HEADS // 2
UNITS = 16
SCALE1 = 1.0 / 16.0
SCALE2 = 0.25
NEG = -3.0e38
EPS = 1e-5
TILES = 2 * T // P + E
SLOTS = TILES * P
ROW = D + 2
PARTS = ((0, 0), (0, 1), (1, 0))
STACK_DMAS = HALF * 3 + HALF // 2 * 3


def side_blocks(i):
    return [n for n in (i - 1, i + 1) if 0 <= n < NT]


def build(nc, x_d, xT_d, cT_d, w_d, brow_d, bcol_d, gate_w_d, gate_b_d,
          w1_d, b1T_d, w2_d, b2_d, ws1_d, bs1T_d, ws2_d, bs2_d, out_d):
    ctx = ExitStack()
    with ctx:
        def sb(name, shape, dt=F, stack=ctx):
            return stack.enter_context(nc.sbuf_tensor(name, shape, dt))

        def sem(name):
            return ctx.enter_context(nc.semaphore(name))

        slot_rows = nc.dram_tensor("slot_rows", (SLOTS, ROW), F, kind="Internal").ap()
        pair_out = nc.dram_tensor("pair_out", (2 * T + SLOTS, D), F, kind="Internal").ap()
        shared_out = nc.dram_tensor("shared_out", (T, D), F, kind="Internal").ap()

        X = sb("X", [P, B * NT, D])
        ident = sb("ident", [P, P])
        causal = sb("causal", [P, P])
        brow = sb("brow", [P, 3, D])
        bcol = sb("bcol", [P, 5, KD])
        logits = sb("logits", [P, B * NT, E])
        half_pow = sb("half_pow", [P, NT])
        stats = sb("stats", [P, NT, 6])
        mv = sb("mv", [P, NT, 2])
        rstd = sb("rstd", [P, NT])
        var_eps = sb("var_eps", [P, NT])
        gate_w = sb("gate_w", [P, KD, E])
        gate_b = sb("gate_b", [E, 1])
        pad_no = sb("pad_no", [P, TILES], I32)
        pad_end = sb("pad_end", [P, TILES, 2])

        att = ExitStack()
        W_s = [sb("w1_s", [P, 4, 2, KD, D], FR, att)]
        q_stack = sb("q_stack", [P, HEADS, S], FR, att)
        W_s.append(sb("w2_s", [P, 4, 2, KD, D], FR, att))
        k_stack = sb("k_stack", [P, HEADS // 2, S], FR, att)
        a_s = sb("a_s", [P, 2, KD, S], FR, att)
        c_s = sb("c_s", [P, 2, KD, S], FR, att)
        q_s = sb("q_s", [P, KD, 2, S], FR, att)
        k_s = sb("k_s", [P, KD, 2, S], FR, att)
        v_s = sb("v_s", [P, 2, NT, D], FR, att)
        attnT_s = v_s[:, :, :, :].rearrange("p l n d -> p (l n d)").rearrange(
            "p (l k t) -> p l k t", l=2, k=KD)
        pT_s = sb("pT_s", [P, 2, NT, S], FR, att)
        aug = sb("aug", [P, NT, 4, HALF], FR, att)
        augT = sb("augT", [4 * HALF, S], FR, att)
        x_raw = sb("x_raw", [P, KD, S], F, att)
        c_raw = sb("c_raw", [P, KD, S], F, att)
        res = sb("res", [P, NT, D], F, att)
        v_aug = sb("v_aug", [P, NT, HEADS, 32], F, att)
        pT = sb("pT", [P, 2, 2, 768], F, att)
        probs = pT[:, :, :, :].rearrange("p a b c -> p (a b c)")[:, 0:NT * S].rearrange(
            "p (n k) -> p n k", n=NT)
        oT = sb("oT", [P, 2, 2, S], F, att)
        oT_flat = oT[:, :, :, :].rearrange("p a b c -> p (a b c)")
        x2T = oT_flat[:, 0:KD * S].rearrange("p (k t) -> p k t", k=KD)
        lgT = oT_flat[0:E, KD * S:KD * S + S]
        raw1 = oT_flat[:, 0:4 * KD * D].rearrange("p (w k n) -> p w k n", w=4, k=KD)
        raw2 = v_aug[:, :, :, :].rearrange("p a b c -> p (a b c)").rearrange(
            "p (w k n) -> p w k n", w=4, k=KD)
        attn = sb("attn", [P, NT, D], F, att)
        mx = sb("mx", [P, NT, HALF, 3], F, att)
        ncross = sb("ncross", [P, NT, HALF], F, att)
        dloc = sb("dloc", [P, 2, NT, HALF], F, att)
        wloc = sb("wloc", [P, NT, HALF], F, att)
        cw = sb("cw", [P, 4, NT, HALF], F, att)
        cmb = sb("cmb", [P, NT, HALF, DH], F, att)
        nmax = sb("nmax", [P, 2, NT], F, att)
        den = sb("den", [P, 2, NT], F, att)
        att.close()

        mo = ExitStack()
        ws = sb("ws", [P, 1, 4096], F, mo)
        we = sb("we", [P, E, 4096], F, mo)
        b1T = sb("b1T", [P, (E + 1) * NH], F, mo)
        b2b = sb("b2b", [P, E + 1, D], F, mo)
        xs = sb("xs", [P, 2, D], F, mo)
        meta = sb("meta", [P, TILES, 2], F, mo)
        xT = sb("xT", [P, 2, KD, P], F, mo)
        hp = sb("hp", [P, HID], F, mo)
        hT = sb("hT", [P, NH, P], F, mo)
        ysum = sb("ysum", [P, 2, D], F, mo)
        yw = sb("yw", [P, 2, D], F, mo)
        stage = sb("stage", [P, 2, ROW], F, mo)
        yidx = sb("yidx", [P, 2, 1], I32, mo)
        sidx = sb("sidx", [P, 2, 1], I32, mo)
        upper = sb("upper", [P, P], F, mo)
        ones = sb("ones", [P, P], F, mo)
        desc8 = sb("desc8", [P, E], F, mo)
        step128 = sb("step128", [P, 16], F, mo)
        tile_no = sb("tile_no", [P, TILES], F, mo)
        ids = sb("ids", [P, 2, B * NT], F, mo)
        R = {n: sb("r_" + n, [P, B * NT, E], F, mo) for n in
             ("t0", "oh1", "oh2", "lg2", "mask", "c0", "c1", "pos")}
        r1 = {n: sb("r1_" + n, [P, B * NT], F, mo) for n in ("m1", "i1", "m2", "i2", "e2", "g1", "g2", "s1", "s2")}
        cmp = sb("cmp", [P, E, 16], F, mo)
        cmpt = sb("cmpt", [P, TILES, E], F, mo)
        nt_e = sb("nt_e", [P, E], F, mo)
        end_e = sb("end_e", [P, E], F, mo)
        beg_e = sb("beg_e", [P, E], F, mo)
        one_e = sb("one_e", [P, E], F, mo)
        tab_f = sb("tab_f", [P, TILES], F, mo)
        table = sb("table", [P, TILES], I32, mo)
        mo.close()
        fin = ExitStack()
        yl = sb("yl", [P, B, NT, 3, D], F, fin)
        fo = sb("fo", [P, B, NT, D], F, fin)
        fin.close()

        ps = ctx.enter_context(nc.psum_tensor("ps", [P, 8, 512], F))

        names = """x_in w1_in w2_in w1_hi w1_lo b_in x_raw_in c_raw_in wsplit wsplit_hi consts consts2 masks xbo pad_set pad_out
          xa_hi xa_lo qk1_ps qk1_hi qk1_lo v1_ps v1_hi v1_lo s1_ps s1_step s1_max s1_exp p1_step p1_norm
          pt_ps pt_hi pt_lo o1_ps o1_hi o1_lo w1_ps ln_step ln_pow ln_out x_kept
          x1_ps x1_hi x1_lo ctx_hi ctx_lo qk2_ps qk2_hi qk2_lo stacked aug_in
          a_ps a_red aug_step aug_ready augT_ps augT_out b_ps b_exp pv_done oc_out os_out
          cb_ps w_exp cb_step cb_out v2_ps v2_out at_ps at_hi at_lo w2_ps
          g_ps g_out lg_ps lg_out lgT_ps lgT_out
          ws_in we_in eb_in r_step r_exp r_exp_in r_ps table_ready slots_ready st_step st_out
          xT_ps xT_out meta_in h_ps h_out hT_ps hT_out y_ps y_sum y_out y_idx
          f_step f_pow f_out o_sent
          """.split()
        s = {n: sem("s_" + n) for n in names}
        xs_in, yw_sent, shared_sent = ([sem(f"s_{n}{q}") for q in range(2)] for n in ("xs_in", "yw_sent", "shared_sent"))
        yl_in = [sem(f"s_yl_in{b}") for b in range(B)]

        block = ctx.enter_context(nc.Block())

        def mm3(pe, out, lhs, rhs, first=True, last=True, check=False):
            for n, (a, b) in enumerate(PARTS):
                m = nc.tensor.matmul(out, lhs(a), rhs(b), start=first and n == 0,
                                     stop=last and n == 2, skip_group_check=check)
            return m

        @block.sync
        def _(sp):
            for i in range(4):
                sp.dma_start(raw1[:, i, :, :], w_d[i].rearrange("(k p) n -> p k n", p=P)).then_inc(s["w1_in"], 16)
            sp.dma_start(x_raw[:, :, :], xT_d[:, 0:S].rearrange("(k p) t -> p k t", p=P)).then_inc(s["x_raw_in"], 16)
            sp.dma_start(bcol[:, :, :].rearrange("p i k -> p (i k)"), bcol_d).then_inc(s["b_in"], 16)
            sp.dma_start(brow[:, :, :], brow_d.partition_broadcast(P)).then_inc(s["b_in"], 16)
            sp.dma_start(gate_w[:, :, :], gate_w_d.rearrange("(k p) e -> p k e", p=P)).then_inc(s["b_in"], 16)
            sp.dma_start(gate_b[:, :], gate_b_d.rearrange("(e o) -> e o", o=1)).then_inc(s["b_in"], 16)
            for i in range(4):
                sp.dma_start(raw2[:, i, :, :], w_d[4 + i].rearrange("(k p) n -> p k n", p=P)).then_inc(s["w2_in"], 16)
            for b in range(B):
                sp.dma_start(X[:, NT * b:NT * b + NT, :],
                             x_d[b * S:(b + 1) * S, :].rearrange("(n p) d -> p n d", p=P)).then_inc(s["x_in"], 16)
            sp.dma_start(c_raw[:, :, :], cT_d[:, 0:S].rearrange("(k p) t -> p k t", p=P)).then_inc(s["c_raw_in"], 16)

            sp.wait_ge(s["pad_set"], 4)
            sp.dma_start(slot_rows[:, 0:D].rearrange("(i p) d -> p i d", p=P),
                         attn[:, 0:1, :].broadcast_to([P, TILES, D])).then_inc(s["pad_out"], 16)
            sp.dma_start(slot_rows[:, D:].rearrange("(i p) d -> p i d", p=P), pad_end[:, :, :]).then_inc(s["pad_out"], 16)

            def stack(h):
                for g in range(HALF // 2):
                    for sec, part in enumerate((0, 1, 0)):
                        sp.dma_start(k_stack[32 * sec:32 * sec + 32, h * (HALF // 2) + g, :].bitcast(F),
                                     k_s[32 * g:32 * g + 32, h, part, :].bitcast(F)).then_inc(s["stacked"], 16)
                for g in range(HALF):
                    for sec, part in enumerate((0, 0, 1)):
                        r = 32 * sec + 16 * (g % 2)
                        sp.dma_start(q_stack[r:r + 16, h * HALF + g, :].bitcast(F),
                                     q_s[16 * g:16 * g + 16, h, part, :].bitcast(F)).then_inc(s["stacked"], 16)

            def aug_rows(b, h):
                sp.wait_ge(s["augT_out"], 2 * b + h + 1)
                for r in range(4):
                    sp.dma_start(q_stack[96 + r:97 + r, h * HALF:(h + 1) * HALF, :].bitcast(F),
                                 augT[r * HALF:(r + 1) * HALF, :].bitcast(F)).then_inc(s["aug_in"], 16)

            def body(b, first):
                sp.wait_ge(s["qk2_lo"], 4 * b + 4)
                if first:
                    sp.wait_ge(s["masks"], 2)
                else:
                    sp.wait_ge(s["b_ps"], UNITS * (2 * b - 1))
                stack(0)
                aug_rows(b, 0)
                if not first:
                    sp.wait_ge(s["b_ps"], UNITS * (2 * b))
                stack(1)
                nb = (b + 1) % B
                sp.wait_ge(s["xa_lo"], b + 1)
                sp.dma_start(x_raw[:, :, :], xT_d[:, bass.ts(nb, S)].rearrange("(k p) t -> p k t", p=P))\
                    .then_inc(s["x_raw_in"], 16)
                sp.wait_ge(s["ctx_lo"], b + 1)
                sp.dma_start(c_raw[:, :, :], cT_d[:, bass.ts(nb, S)].rearrange("(k p) t -> p k t", p=P))\
                    .then_inc(s["c_raw_in"], 16)
                aug_rows(b, 1)

            body(0, True)
            with sp.Fori(1, B) as b:
                body(b, False)

            sp.wait_ge(s["x_raw_in"], 16 * (B + 1))
            sp.wait_ge(s["c_raw_in"], 16 * (B + 1))
            sp.wait_ge(s["lgT_out"], B)
            sp.wait_ge(s["x_kept"], 2 * B)
            sp.wait_ge(s["pad_out"], 32)
            for q in range(2):
                sp.dma_start(xs[:, q, :], X[:, q, :]).then_inc(xs_in[q], 16)
            sp.dma_start(ws[:, 0, 0:KD * HID].rearrange("p (k n) -> p k n", k=KD),
                         ws1_d.rearrange("(k p) n -> p k n", p=P)).then_inc(s["ws_in"], 16)
            sp.dma_start(ws[:, 0, KD * HID:].rearrange("p (k n) -> p k n", k=NH),
                         ws2_d.rearrange("(k p) n -> p k n", p=P)).then_inc(s["ws_in"], 16)
            sp.dma_start(b1T[:, 0:NH], bs1T_d).then_inc(s["eb_in"], 16)
            sp.dma_start(b1T[:, NH:], b1T_d).then_inc(s["eb_in"], 16)
            sp.dma_start(b2b[:, 0, :], bs2_d.partition_broadcast(P)).then_inc(s["eb_in"], 16)
            sp.dma_start(b2b[:, 1:, :], b2_d.partition_broadcast(P)).then_inc(s["eb_in"], 16)
            for e in range(E):
                sp.dma_start(we[:, e, 0:KD * HID].rearrange("p (k n) -> p k n", k=KD),
                             w1_d[e].rearrange("(k p) n -> p k n", p=P)).then_inc(s["we_in"], 16)
                sp.dma_start(we[:, e, KD * HID:].rearrange("p (k n) -> p k n", k=NH),
                             w2_d[e].rearrange("(k p) n -> p k n", p=P)).then_inc(s["we_in"], 16)
            def shared_tile(t, q, last):
                if not last:
                    sp.wait_ge(s["xT_ps"], t + 1)
                    sp.dma_start(xs[:, q, :], X[:, bass.ds(t + 2, 1), :].rearrange("p o d -> p (o d)"))\
                        .then_inc(xs_in[q], 16)
                sp.wait_ge(s["y_sum"], t + 1)
                sp.dma_start(shared_out[bass.ts(t, P), :], ysum[:, q, :]).then_inc(shared_sent[q], 16)

            with sp.Fori(0, T // P // 2 - 1) as i:
                for q in range(2):
                    shared_tile(2 * i + q, q, False)
            for q in range(2):
                shared_tile(T // P - 2 + q, q, True)
            sp.wait_ge(s["st_out"], 16 * 2 * T // P)
            for q in range(2):
                sp.dma_start(xs[:, q, :], slot_rows[q * P:(q + 1) * P, 0:D]).then_inc(xs_in[q], 16)
            sp.dma_start(meta[:, :, :], slot_rows[:, D:].rearrange("(i p) m -> p i m", p=P)).then_inc(s["meta_in"], 16)
            with sp.Fori(0, TILES // 2 - 1) as i:
                for q in range(2):
                    t = 2 * i + q
                    sp.wait_ge(s["xT_ps"], T // P + t + 1)
                    sp.dma_start(xs[:, q, :], slot_rows[bass.ts(t + 2, P), 0:D]).then_inc(xs_in[q], 16)
            for q in range(2):
                sp.wait_ge(yw_sent[q], 16 * TILES // 2)
                sp.wait_ge(shared_sent[q], 16 * T // P // 2)
            sp.wait_ge(s["y_ps"], T // P + TILES)
            for b in range(B):
                sp.dma_start(yl[:, b, :, 0:2, :],
                             pair_out[2 * b * S:2 * (b + 1) * S, :].rearrange("(n p k) d -> p n k d", p=P, k=2))\
                    .then_inc(yl_in[b], 16)
                sp.dma_start(yl[:, b, :, 2, :],
                             shared_out[b * S:(b + 1) * S, :].rearrange("(n p) d -> p n d", p=P))\
                    .then_inc(yl_in[b], 16)
            for b in range(B):
                sp.wait_ge(s["f_out"], b + 1)
                sp.dma_start(out_d[b * S:(b + 1) * S, :].rearrange("(n p) d -> p n d", p=P),
                             fo[:, b, :, :]).then_inc(s["o_sent"], 16)
            sp.wait_ge(s["o_sent"], 16 * B)

        @block.gpsimd
        def _(pool):
            nc.gpsimd.memset(ident[:, :], 0.0).then_inc(s["consts"], 1)
            nc.gpsimd.memset(causal[:, :], 0.0).then_inc(s["consts"], 1)
            nc.gpsimd.memset(half_pow[:, :], -0.5).then_inc(s["consts"], 1)
            pool.wait_ge(s["consts"], 3)
            nc.gpsimd.affine_select(out=ident[:, :], in_=ident[:, :], compare_op=ALU.not_equal, fill=1.0,
                                    base=0, pattern=[[-1, P]], channel_multiplier=1).then_inc(s["consts"], 1)
            nc.gpsimd.affine_select(out=causal[:, :], in_=causal[:, :], compare_op=ALU.is_ge, fill=NEG,
                                    base=0, pattern=[[-1, P]], channel_multiplier=1).then_inc(s["consts"], 1)
            nc.gpsimd.memset(attn[:, 0, :], 0.0).then_inc(s["pad_set"], 1)
            nc.gpsimd.memset(pad_end[:, :, :], 0.0).then_inc(s["pad_set"], 1)
            nc.gpsimd.iota(pad_no[:, :], pattern=[[P, TILES]], base=2 * T, channel_multiplier=1).then_inc(s["pad_set"], 1)
            pool.wait_ge(s["pad_set"], 3)
            nc.gpsimd.tensor_copy(pad_end[:, :, 0], pad_no[:, :]).then_inc(s["pad_set"], 1)
            pool.wait_ge(s["w2_in"], 16 * 4)
            for i in range(4):
                nc.gpsimd.tensor_copy(W_s[1][:, i, 0, :, :], raw2[:, i, :, :]).then_inc(s["wsplit_hi"], 1)
            for i in range(4):
                pool.wait_ge(s["wsplit_hi"], i + 1)
                nc.gpsimd.tensor_tensor(W_s[1][:, i, 1, :, :], raw2[:, i, :, :],
                                        W_s[1][:, i, 0, :, :].bitcast(F), ALU.subtract).then_inc(s["wsplit"], 1)
            nc.gpsimd.memset(q_stack[:, :, :].bitcast(F), 0.0).then_inc(s["masks"], 1)
            pool.wait_ge(s["masks"], 1)
            nc.gpsimd.memset(k_stack[96:P, :, :].bitcast(F), 1.0).then_inc(s["masks"], 1)
            pool.wait_ge(s["masks"], 2)
            nc.gpsimd.memset(pT_s[:, :, :, :].bitcast(F), 0.0).then_inc(s["masks"], 1)
            nc.gpsimd.memset(mx[:, :, :, :], -NEG).then_inc(s["masks"], 1)
            pool.wait_ge(s["wsplit"], 4)
            nc.gpsimd.memset(v_aug[:, :, :, :], 0.0).then_inc(s["masks"], 1)
            pool.wait_ge(s["masks"], 5)
            nc.gpsimd.memset(v_aug[:, :, :, DH:DH + 1], 1.0).then_inc(s["masks"], 1)
            pool.wait_ge(s["b_in"], 64)
            pool.wait_ge(s["x_in"], 16 * B)
            for b in range(B):
                Xb = X[:, NT * b:NT * b + NT, :]
                nc.gpsimd.tensor_tensor(Xb, Xb, brow[:, 0:1, :].broadcast_to([P, NT, D]), ALU.add)\
                    .then_inc(s["xbo"], 1)

            def norm_pow(c):
                pool.wait_ge(s["ln_step"], 4 * c + 4)
                nc.gpsimd.tensor_tensor(rstd[:, :], var_eps[:, :], half_pow[:, :], ALU.pow).then_inc(s["ln_pow"], 1)

            def keep(b, c, bias):
                pool.wait_ge(s["ln_out"], c + 1)
                Xb = X[:, bass.ts(b, NT), :]
                if bias:
                    nc.gpsimd.tensor_tensor(Xb, res[:, :, :], brow[:, 2:3, :].broadcast_to([P, NT, D]), ALU.add)\
                        .then_inc(s["x_kept"], 1)
                else:
                    nc.gpsimd.tensor_copy(Xb, res[:, :, :]).then_inc(s["x_kept"], 1)

            norm_pow(0)
            keep(0, 0, True)
            with pool.Fori(1, B) as b:
                norm_pow(2 * b - 1)
                keep(b, 2 * b - 1, True)
                norm_pow(2 * b)
                keep(b - 1, 2 * b, False)
            norm_pow(2 * B - 1)
            keep(B - 1, 2 * B - 1, False)

            pool.wait_ge(s["lgT_out"], B)
            pool.wait_ge(s["x_kept"], 2 * B)
            nc.gpsimd.memset(upper[:, :], 1.0).then_inc(s["consts2"], 1)
            nc.gpsimd.memset(ones[:, :], 1.0).then_inc(s["consts2"], 1)
            nc.gpsimd.memset(one_e[:, :], 1.0).then_inc(s["consts2"], 1)
            nc.gpsimd.iota(R["t0"][:, 0:1, :].bitcast(I32), pattern=[[0, 1], [-1, E]], base=E, channel_multiplier=0)\
                .then_inc(s["consts2"], 1)
            nc.gpsimd.iota(R["lg2"][:, 0:2, :].bitcast(I32), pattern=[[P * E, 2], [P, E]], base=0, channel_multiplier=0)\
                .then_inc(s["consts2"], 1)
            nc.gpsimd.iota(table[:, :], pattern=[[1, TILES]], base=0, channel_multiplier=0).then_inc(s["consts2"], 1)
            nc.gpsimd.iota(R["mask"][:, 0:4, :].bitcast(I32).rearrange("p (k a) e -> p k (a e)", k=2),
                           pattern=[[1, 2], [2 * P, B * NT]], base=0, channel_multiplier=2).then_inc(s["consts2"], 1)
            pool.wait_ge(s["consts2"], 7)
            nc.gpsimd.affine_select(out=upper[:, :], in_=upper[:, :], compare_op=ALU.is_ge, fill=0.0,
                                    base=-1, pattern=[[1, P]], channel_multiplier=-1).then_inc(s["consts2"], 1)
            nc.gpsimd.tensor_copy(desc8[:, :], R["t0"][:, 0, :].bitcast(I32)).then_inc(s["consts2"], 1)
            nc.gpsimd.tensor_copy(step128[:, :].rearrange("p (a b) -> p a b", a=2), R["lg2"][:, 0:2, :].bitcast(I32))\
                .then_inc(s["consts2"], 1)
            nc.gpsimd.tensor_copy(tile_no[:, :], table[:, :]).then_inc(s["consts2"], 1)
            nc.gpsimd.tensor_copy(ids[:, :, :].rearrange("p k t -> p (k t)"),
                                  R["mask"][:, 0:4, :].bitcast(I32).rearrange("p a e -> p (a e)"))\
                .then_inc(s["consts2"], 1)

            pool.wait_ge(s["consts2"], 12)
            pool.wait_ge(s["pad_out"], 32)
            pool.wait_ge(s["slots_ready"], 1)
            with pool.Fori(1, T // P + 1) as u:
                t = u - 1
                for k, (g, sl) in enumerate((("g1", "s1"), ("g2", "s2"))):
                    st = stage[:, k, :]
                    nc.gpsimd.tensor_copy(st[:, 0:D], X[:, bass.ds(t, 1), :].rearrange("p o d -> p (o d)"))
                    nc.gpsimd.tensor_copy(st[:, D:D + 1], ids[:, k, bass.ds(t, 1)])
                    nc.gpsimd.tensor_copy(st[:, D + 1:D + 2], r1[g][:, bass.ds(t, 1)])
                    last = nc.gpsimd.tensor_copy(sidx[:, k, :], r1[sl][:, bass.ds(t, 1)])
                last.then_inc(s["st_step"], 1)
                pool.wait_ge(s["slots_ready"], 1)
                pool.wait_ge(s["st_step"], u)
                for k in range(2):
                    pool.indirect_dma_start(
                        out=slot_rows, out_offset=bass.IndirectOffsetOnAxis(ap=sidx[:, k, :], axis=0),
                        in_=stage[:, k, :], in_offset=None).then_inc(s["st_out"], 16)
                pool.wait_ge(s["st_out"], 32 * u)

            pool.wait_ge(s["meta_in"], 16)
            with pool.Fori(0, TILES // 2) as i:
                for q in range(2):
                    t = 2 * i + q
                    pool.wait_ge(s["y_out"], t + 1)
                    nc.gpsimd.tensor_copy(yidx[:, q, :], meta[:, bass.ds(t, 1), 0]).then_inc(s["y_idx"], 1)
                    pool.wait_ge(s["meta_in"], 16)
                    pool.wait_ge(s["y_idx"], t + 1)
                    pool.indirect_dma_start(
                        out=pair_out, out_offset=bass.IndirectOffsetOnAxis(ap=yidx[:, q, :], axis=0),
                        in_=yw[:, q, :], in_offset=None).then_inc(yw_sent[q], 16)
            for b in range(B):
                pool.wait_ge(s["f_step"], 6 * b + 6)
                nc.gpsimd.tensor_tensor(rstd[:, :], var_eps[:, :], half_pow[:, :], ALU.pow).then_inc(s["f_pow"], 1)

        @block.scalar
        def _(act):
            def copy(out, in_, name):
                nc.scalar.activation(out, in_, ACT.Copy).then_inc(s[name], 1)

            def copy_bias(out, in_, bias, name):
                nc.scalar.activation(out, in_, ACT.Identity, bias=bias).then_inc(s[name], 1)

            def attention1(b, first):
                act.wait_ge(s["x_raw_in"], 16 * b + 16)
                copy(a_s[:, 0, :, :], x_raw[:, :, :], "xa_hi")
                if first:
                    act.wait_ge(s["b_in"], 64)
                else:
                    act.wait_ge(s["stacked"], 16 * STACK_DMAS * 2 * b)
                for j in range(4):
                    act.wait_ge(s["qk1_ps"], 4 * b + j + 1)
                    copy_bias((q_s, k_s)[j // 2][:, j % 2, 0, :], ps[:, j, :], bcol[:, j // 2, j % 2:j % 2 + 1], "qk1_hi")
                for j in range(2):
                    act.wait_ge(s["v1_ps"], 2 * b + j + 1)
                    copy(v_s[:, 0, 2 * j:2 * j + 2, :], ps[:, 4 + j, :].rearrange("p (n d) -> p n d", n=2), "v1_hi")

                def expo(n):
                    act.wait_ge(s["s1_max"], NT * b + n + 1)
                    w = (n + 1) * P
                    nc.scalar.activation(probs[:, n, 0:w], ps[:, n, 0:w], ACT.Exp, bias=nmax[:, 1, n:n + 1],
                                         scale=SCALE1, accum_out=den[:, 0, n:n + 1]).then_inc(s["s1_exp"], 1)

                def turned(n):
                    act.wait_ge(s["pt_ps"], NT * b + n + 1)
                    copy(pT_s[:, 0, 0:n + 1, n * P:(n + 1) * P],
                         ps[:, 4 + n, 0:(n + 1) * P].rearrange("p (j q) -> p j q", q=P), "pt_hi")

                if first:
                    act.wait_ge(s["masks"], 3)
                expo(0)
                expo(1)
                turned(0)
                expo(2)
                turned(1)
                expo(3)
                turned(2)
                turned(3)
                for j in range(2):
                    act.wait_ge(s["o1_ps"], 2 * b + j + 1)
                    copy_bias(c_s[:, 0, j, :], ps[:, j, :], bcol[:, 2, j:j + 1], "o1_hi")

            def project2(b):
                act.wait_ge(s["w1_ps"], NT * b + NT)
                act.wait_ge(s["c_raw_in"], 16 * b + 16)
                copy(c_s[:, 0, :, :], c_raw[:, :, :], "ctx_hi")
                act.wait_ge(s["x1_ps"], b + 1)
                copy(a_s[:, 0, :, :], ps[:, 4:6, :], "x1_hi")
                for j, (dst, blk) in enumerate(((q_s, 0), (k_s, 0), (q_s, 1), (k_s, 1))):
                    act.wait_ge(s["qk2_ps"], 4 * b + j + 1)
                    copy_bias(dst[:, blk, 0, :], ps[:, j, :], bcol[:, 3 + j % 2, blk:blk + 1], "qk2_hi")

            def half(a, c, free):
                if c is not None:
                    for u in range(UNITS):
                        m, i = u // 2, (u // 2) % NT
                        w = 2 * P * (1 + len(side_blocks(i)))
                        act.wait_ge(s["b_ps"], UNITS * c + u + 1)
                        if m >= 2:
                            act.wait_ge(s["pv_done"], 8 * c + m - 1)
                        nc.scalar.activation(pT[:, m % 2, u % 2, 0:w],
                                             ps[:, 4:6, :].rearrange("p a c -> p (a c)")[:, 256:256 + w],
                                             ACT.Exp, scale=SCALE2).then_inc(s["b_exp"], 1)
                        if u == 9:
                            out_local(c, 0)
                    out_local(c, 1)
                if a is not None:
                    if free:
                        act.wait_ge(s["aug_in"], 64 * a)
                    act.wait_ge(s["augT_ps"], a + 1)
                    copy(augT[:, :], ps[0:4 * HALF, 2, :], "augT_out")

            def out_local(c, g):
                act.wait_ge(s["pv_done"], 8 * c + 4 * g + 4)
                copy(oT[:, g, 0, :], ps[:, 6, :], "oc_out")

            def local_weight(c, h):
                nc.scalar.activation(wloc[:, :, :], dloc[:, h, :, :], ACT.Exp, scale=-SCALE2).then_inc(s["w_exp"], 1)

            def output2(b):
                act.wait_ge(s["at_ps"], b + 1)
                copy(attnT_s[:, 0, :, :], ps[:, 6:8, :], "at_hi")
                act.wait_ge(s["g_ps"], b + 1)
                copy(x2T, ps[:, 4:6, :], "g_out")

            def body(b, first):
                attention1(b, first)
                project2(b)
                half(2 * b, None if first else 2 * b - 1, not first)
                if not first:
                    act.wait_ge(s["cb_out"], 2 * b - 1)
                    local_weight(2 * b - 1, 1)
                    output2(b - 1)
                half(2 * b + 1, 2 * b, True)
                if not first:
                    act.wait_ge(s["cb_out"], 2 * b)
                local_weight(2 * b, 0)

            body(0, True)
            with act.Fori(1, B) as b:
                body(b, False)
            half(None, 2 * B - 1, True)
            act.wait_ge(s["cb_out"], 2 * B - 1)
            local_weight(2 * B - 1, 1)
            output2(B - 1)

            act.wait_ge(s["r_exp_in"], 1)
            nc.scalar.activation(r1["e2"][:, :], r1["e2"][:, :], ACT.Exp).then_inc(s["r_exp"], 1)

            def expert_tiles(base, n, table_expert, weigh):
                def x_out(t, q, reused=True):
                    if base or reused:
                        act.wait_ge(s["h_ps"], base + t - 1)
                    act.wait_ge(s["xT_ps"], base + t + 1)
                    copy(xT[:, q, :, :], ps[:, 7 * q, 0:KD * P].rearrange("p (k t) -> p k t", k=KD), "xT_out")

                def gelu(t, q):
                    e = table_expert(t)
                    act.wait_ge(s["hT_ps"], base + t + 1)
                    for c in range(NH):
                        last = nc.scalar.activation(hT[:, c, :], ps[:, 4 + c // 4, (c % 4) * P:(c % 4 + 1) * P],
                                                    ACT.Gelu, bias=b1T[:, bass.ds(e * NH + c, 1)])
                    last.then_inc(s["hT_out"], 1)

                def weight(t, q):
                    act.wait_ge(s["meta_in"], 16)
                    act.wait_ge(s["y_sum"], base + t + 1)
                    if not (isinstance(t, int) and t < 2):
                        act.wait_ge(yw_sent[q], 8 * (t - q))
                    nc.scalar.activation(yw[:, q, :], ysum[:, q, :], ACT.Copy, scale=meta[:, bass.ds(t, 1), 1])\
                        .then_inc(s["y_out"], 1)

                def step(t, q, end=False):
                    if not (end and q >= 0):
                        x_out(t + 2, q)
                    if not (end and q == 1):
                        gelu(t + 1, 1 - q)
                    if weigh:
                        weight(t, q)

                x_out(0, 0, False)
                x_out(1, 1, False)
                gelu(0, 0)
                step(0, 0)
                step(1, 1)
                with act.Fori(1, n // 2 - 1) as i:
                    step(2 * i, 0)
                    step(2 * i + 1, 1)
                step(n - 2, 0, True)
                step(n - 1, 1, True)

            act.wait_ge(s["eb_in"], 64)
            expert_tiles(0, T // P, lambda t: 0, False)
            act.wait_ge(s["table_ready"], 1)
            expert_tiles(T // P, TILES,
                         lambda t: act.value_load(table[0:1, bass.ds(t, 1)], min_val=0, max_val=E - 1) + 1, True)

        @block.vector
        def _(dve):
            def lo_of(out, full, hi, name):
                nc.vector.tensor_tensor(out, full, hi.bitcast(F), ALU.subtract).then_inc(s[name], 1)

            def lo_of_bias(out, full, bias, hi, name):
                nc.vector.scalar_tensor_tensor(out=out, in0=full, scalar=bias, in1=hi.bitcast(F),
                                               op0=ALU.add, op1=ALU.subtract).then_inc(s[name], 1)

            dve.wait_ge(s["w1_in"], 64)
            nc.vector.tensor_copy(W_s[0][:, :, 0, :, :].rearrange("p w k n -> p w (k n)"),
                                  raw1[:, :, :, :].rearrange("p w k n -> p w (k n)")).then_inc(s["w1_hi"], 1)
            dve.wait_ge(s["w1_hi"], 1)
            nc.vector.tensor_tensor(W_s[0][:, :, 1, :, :].rearrange("p w k n -> p w (k n)"),
                                    raw1[:, :, :, :].rearrange("p w k n -> p w (k n)"),
                                    W_s[0][:, :, 0, :, :].rearrange("p w k n -> p w (k n)").bitcast(F),
                                    ALU.subtract).then_inc(s["w1_lo"], 1)

            def norm(c, step="ln_step", pow_="ln_pow", out="ln_out", src=None, dst=None, first_steps=0, per=4):
                src = res if src is None else src
                dst = res if dst is None else dst
                at = per * c + first_steps
                dve.wait_ge(s[step], at + 1)
                for n in range(NT):
                    last = nc.vector.bn_stats(stats[:, n, :], src[:, n, :])
                last.then_inc(s[step], 1)
                dve.wait_ge(s[step], at + 2)
                nc.vector.memset(var_eps[:, :], 0.0)
                for n in range(NT):
                    last = nc.vector.bn_aggr(mv[:, n, :], stats[:, n, :])
                last.then_inc(s[step], 1)
                dve.wait_ge(s[step], at + 3)
                nc.vector.tensor_scalar(var_eps[:, :], mv[:, :, 1], EPS, None, ALU.add).then_inc(s[step], 1)
                dve.wait_ge(s[pow_], c + 1)
                for n in range(NT):
                    last = nc.vector.tensor_scalar(dst[:, n, :], src[:, n, :], mv[:, n, 0:1], rstd[:, n:n + 1],
                                                   ALU.subtract, ALU.mult)
                last.then_inc(s[out], 1)

            def attention1(b, first):
                dve.wait_ge(s["xa_hi"], b + 1)
                lo_of(a_s[:, 1, :, :], x_raw[:, :, :], a_s[:, 0, :, :], "xa_lo")
                for j in range(4):
                    dve.wait_ge(s["qk1_hi"], 4 * b + j + 1)
                    t = (q_s, k_s)[j // 2]
                    lo_of_bias(t[:, j % 2, 1, :], ps[:, j, :], bcol[:, j // 2, j % 2:j % 2 + 1], t[:, j % 2, 0, :], "qk1_lo")
                for j in range(2):
                    dve.wait_ge(s["v1_hi"], 2 * b + j + 1)
                    lo_of(v_s[:, 1, 2 * j:2 * j + 2, :], ps[:, 4 + j, :].rearrange("p (n d) -> p n d", n=2),
                          v_s[:, 0, 2 * j:2 * j + 2, :], "v1_lo")

                def maximum(n):
                    dve.wait_ge(s["s1_ps"], NT * b + n + 1)
                    diag = ps[:, n, n * P:(n + 1) * P]
                    nc.vector.tensor_tensor(diag, diag, causal[:, :], ALU.add).then_inc(s["s1_step"], 1)
                    dve.wait_ge(s["s1_step"], 2 * (NT * b + n) + 1)
                    nc.vector.tensor_reduce(nmax[:, 0, n:n + 1], ps[:, n, 0:(n + 1) * P], AX, ALU.max, negate=True)\
                        .then_inc(s["s1_step"], 1)
                    dve.wait_ge(s["s1_step"], 2 * (NT * b + n) + 2)
                    nc.vector.tensor_scalar(nmax[:, 1, n:n + 1], nmax[:, 0, n:n + 1], SCALE1, None, ALU.mult)\
                        .then_inc(s["s1_max"], 1)

                def normalise(n):
                    dve.wait_ge(s["s1_exp"], NT * b + n + 1)
                    nc.vector.reciprocal(den[:, 1, n:n + 1], den[:, 0, n:n + 1]).then_inc(s["p1_step"], 1)
                    dve.wait_ge(s["p1_step"], NT * b + n + 1)
                    w = (n + 1) * P
                    nc.vector.tensor_scalar(probs[:, n, 0:w], probs[:, n, 0:w], den[:, 1, n:n + 1], None, ALU.mult)\
                        .then_inc(s["p1_norm"], 1)

                def turned(n):
                    dve.wait_ge(s["pt_hi"], NT * b + n + 1)
                    lo_of(pT_s[:, 1, 0:n + 1, n * P:(n + 1) * P],
                          ps[:, 4 + n, 0:(n + 1) * P].rearrange("p (j q) -> p j q", q=P),
                          pT_s[:, 0, 0:n + 1, n * P:(n + 1) * P], "pt_lo")

                if first:
                    dve.wait_ge(s["consts"], 5)
                maximum(0)
                maximum(1)
                normalise(0)
                maximum(2)
                normalise(1)
                turned(0)
                maximum(3)
                normalise(2)
                turned(1)
                normalise(3)
                turned(2)
                turned(3)
                for j in range(2):
                    dve.wait_ge(s["o1_hi"], 2 * b + j + 1)
                    lo_of_bias(c_s[:, 1, j, :], ps[:, j, :], bcol[:, 2, j:j + 1], c_s[:, 0, j, :], "o1_lo")
                if first:
                    dve.wait_ge(s["xbo"], B)
                else:
                    dve.wait_ge(s["x_kept"], 2 * b - 1)
                for n in range(NT):
                    dve.wait_ge(s["w1_ps"], NT * b + n + 1)
                    last = nc.vector.tensor_tensor(res[:, n, :], ps[:, 2 + n, 0:D],
                                                   X[:, bass.ds(NT * b + n, 1), :].rearrange("p o d -> p (o d)"), ALU.add)
                last.then_inc(s["ln_step"], 1)

            def project2(b):
                dve.wait_ge(s["ctx_hi"], b + 1)
                lo_of(c_s[:, 1, :, :], c_raw[:, :, :], c_s[:, 0, :, :], "ctx_lo")
                dve.wait_ge(s["x1_hi"], b + 1)
                lo_of(a_s[:, 1, :, :], ps[:, 4:6, :], a_s[:, 0, :, :], "x1_lo")
                for j, (t, blk) in enumerate(((q_s, 0), (k_s, 0), (q_s, 1), (k_s, 1))):
                    dve.wait_ge(s["qk2_hi"], 4 * b + j + 1)
                    lo_of_bias(t[:, blk, 1, :], ps[:, j, :], bcol[:, 3 + j % 2, blk:blk + 1], t[:, blk, 0, :], "qk2_lo")

            def out_cross(c, g):
                dve.wait_ge(s["pv_done"], 8 * c + 4 * g + 4)
                nc.vector.tensor_copy(oT[:, g, 1, :], ps[:, 7, :]).then_inc(s["os_out"], 1)

            def half(a, c, h):
                if a is not None:
                    for u in range(UNITS):
                        n, p = u // 4, u % 4
                        k0, nb = max(n - 1, 0), 3 if 0 < n < NT - 1 else 2
                        r0 = k0 - n + 1
                        dve.wait_ge(s["a_ps"], UNITS * a + u + 1)
                        nc.vector.tensor_reduce(mx[:, n, 2 * p:2 * p + 2, r0:r0 + nb],
                                                ps[:, 2:4, 0:nb * P].rearrange("p h (b k) -> p h b k", k=P),
                                                AX, ALU.max, negate=True).then_inc(s["a_red"], 1)
                        if u == 9 and c is not None:
                            out_cross(c, 0)
                    at = 3 * a
                    dve.wait_ge(s["a_red"], UNITS * a + UNITS)
                    nc.vector.tensor_reduce(ncross[:, :, :], mx[:, :, :, :], AX, ALU.min).then_inc(s["aug_step"], 1)
                    dve.wait_ge(s["aug_step"], at + 1)
                    nc.vector.tensor_tensor(dloc[:, h, :, :], mx[:, :, :, 1], ncross[:, :, :], ALU.subtract)
                    nc.vector.tensor_copy(aug[:, :, 0, :], ncross[:, :, :]).then_inc(s["aug_step"], 1)
                    dve.wait_ge(s["aug_step"], at + 2)
                    nc.vector.tensor_tensor(aug[:, :, 1, :], ncross[:, :, :], aug[:, :, 0, :].bitcast(F), ALU.subtract)
                    nc.vector.tensor_copy(aug[:, :, 2, :], dloc[:, h, :, :]).then_inc(s["aug_step"], 1)
                    dve.wait_ge(s["aug_step"], at + 3)
                    nc.vector.tensor_tensor(aug[:, :, 3, :], dloc[:, h, :, :], aug[:, :, 2, :].bitcast(F), ALU.subtract)\
                        .then_inc(s["aug_ready"], 1)
                elif c is not None:
                    out_cross(c, 0)
                if c is not None:
                    out_cross(c, 1)

            def combine(c, h):
                def part(k, lo, hi):
                    x = ps[:, 0:NT, :].rearrange("p n (c g j d) -> p n c (g j) d", c=2, g=2, j=4)
                    return x[:, :, k, :, lo:hi]

                l_loc = part(0, DH, DH + 1).rearrange("p n j o -> p n (j o)")
                l_side = part(1, DH, DH + 1).rearrange("p n j o -> p n (j o)")
                at = 6 * c
                k = [0]

                def link(ins):
                    k[0] += 1
                    ins.then_inc(s["cb_step"], 1)
                    dve.wait_ge(s["cb_step"], at + k[0])

                dve.wait_ge(s["w_exp"], c + 1)
                dve.wait_ge(s["cb_ps"], c + 1)
                nc.vector.reciprocal(cw[:, 3, :, :], l_loc)
                link(nc.vector.tensor_tensor(cw[:, 0, :, :], wloc[:, :, :], l_loc, ALU.mult))
                link(nc.vector.tensor_tensor(cw[:, 1, :, :], cw[:, 0, :, :], l_side, ALU.add))
                link(nc.vector.reciprocal(cw[:, 2, :, :], cw[:, 1, :, :]))
                link(nc.vector.tensor_tensor(cw[:, 0, :, :], wloc[:, :, :], cw[:, 2, :, :], ALU.mult))
                nc.vector.tensor_tensor(cmb[:, :, :, :], part(1, 0, DH),
                                        cw[:, 2, :, :].unsqueeze(3).broadcast_to([P, NT, HALF, DH]), ALU.mult)
                link(nc.vector.tensor_tensor(cw[:, 1, :, :], cw[:, 0, :, :], cw[:, 3, :, :], ALU.add))
                av = attn[:, :, h * P:(h + 1) * P].rearrange("p n (j d) -> p n j d", d=DH)
                link(nc.vector.tensor_tensor(av, part(0, 0, DH),
                                             cw[:, 1, :, :].unsqueeze(3).broadcast_to([P, NT, HALF, DH]), ALU.mult))
                nc.vector.tensor_tensor(av, av, cmb[:, :, :, :], ALU.add).then_inc(s["cb_out"], 1)

            def values2(b):
                for j in range(2):
                    dve.wait_ge(s["v2_ps"], 2 * b + j + 1)
                    nc.vector.tensor_tensor(v_aug[:, 2 * j:2 * j + 2, :, 0:DH],
                                            ps[:, 4 + j, :].rearrange("p (n h d) -> p n h d", n=2, d=DH),
                                            brow[:, 1:2, :].rearrange("p o (h d) -> p o h d", d=DH)
                                            .broadcast_to([P, 2, HEADS, DH]), ALU.add).then_inc(s["v2_out"], 1)

            def output2(b, c):
                dve.wait_ge(s["at_hi"], b + 1)
                lo_of(attnT_s[:, 1, :, :], ps[:, 6:8, :], attnT_s[:, 0, :, :], "at_lo")
                dve.wait_ge(s["x_kept"], 2 * b + 2 if c is None else c)
                for n in range(NT):
                    dve.wait_ge(s["w2_ps"], NT * b + n + 1)
                    last = nc.vector.tensor_tensor(res[:, n, :], ps[:, n, 0:D],
                                                   X[:, bass.ds(NT * b + n, 1), :].rearrange("p o d -> p (o d)"), ALU.add)
                last.then_inc(s["ln_step"], 1)

            def gates(b):
                dve.wait_ge(s["lg_ps"], b + 1)
                nc.vector.tensor_scalar(lgT, ps[0:E, 6, :], gate_b[:, 0:1], None, ALU.add).then_inc(s["lg_out"], 1)
                dve.wait_ge(s["lgT_ps"], b + 1)
                nc.vector.tensor_copy(logits[:, bass.ts(b, NT), :],
                                      ps[:, 7, 0:NT * E].rearrange("p (n e) -> p n e", e=E)).then_inc(s["lgT_out"], 1)

            def body(b, first):
                attention1(b, first)
                norm(0 if first else 2 * b - 1)
                project2(b)
                half(2 * b, None if first else 2 * b - 1, 0)
                if not first:
                    combine(2 * b - 1, 1)
                if first:
                    dve.wait_ge(s["masks"], 6)
                values2(b)
                if not first:
                    output2(b - 1, 2 * b)
                    norm(2 * b)
                    gates(b - 1)
                half(2 * b + 1, 2 * b, 1)
                combine(2 * b, 0)

            dve.wait_ge(s["masks"], 4)
            body(0, True)
            with dve.Fori(1, B) as b:
                body(b, False)
            half(None, 2 * B - 1, 1)
            combine(2 * B - 1, 1)
            output2(B - 1, 2 * B - 1)
            norm(2 * B - 1)
            gates(B - 1)

            k = [0]

            def link(ins):
                k[0] += 1
                ins.then_inc(s["r_step"], 1)
                dve.wait_ge(s["r_step"], k[0])

            def bc(x):
                return x[:, :].unsqueeze(2).broadcast_to([P, B * NT, E])

            def tt(out, a, b_, op):
                return nc.vector.tensor_tensor(out, a, b_, op)

            desc = desc8[:, :].unsqueeze(1).broadcast_to([P, B * NT, E])
            dve.wait_ge(s["consts2"], 12)
            dve.wait_ge(s["lgT_out"], B)
            for src, m, i, oh in ((logits, "m1", "i1", "oh1"), (R["lg2"], "m2", "i2", "oh2")):
                link(nc.vector.tensor_reduce(r1[m][:, :], src[:, :, :], AX, ALU.max))
                link(tt(R["t0"][:, :, :], src[:, :, :], bc(r1[m]), ALU.is_equal))
                link(tt(R["t0"][:, :, :], R["t0"][:, :, :], desc, ALU.mult))
                link(nc.vector.tensor_reduce(r1[i][:, :], R["t0"][:, :, :], AX, ALU.max))
                link(tt(R[oh][:, :, :], desc, bc(r1[i]), ALU.is_equal))
                if m == "m1":
                    link(nc.vector.scalar_tensor_tensor(out=R["lg2"][:, :, :], in0=R["oh1"][:, :, :], scalar=NEG,
                                                        in1=logits[:, :, :], op0=ALU.mult, op1=ALU.add))
            tt(r1["e2"][:, :], r1["m2"][:, :], r1["m1"][:, :], ALU.subtract).then_inc(s["r_exp_in"], 1)
            tt(R["mask"][:, :, :], R["oh1"][:, :, :], R["oh2"][:, :, :], ALU.add).then_inc(s["r_exp_in"], 1)
            dve.wait_ge(s["r_ps"], 2)
            link(nc.vector.tensor_copy(R["c0"][:, :, :], ps[:, 1, 128:256].rearrange("p (t e) -> p t e", e=E)))
            a, b_ = R["c0"], R["c1"]
            for sh in (1, 2, 4, 8):
                nc.vector.tensor_copy(b_[:, 0:sh, :], a[:, 0:sh, :])
                link(tt(b_[:, sh:, :], a[:, sh:, :], a[:, 0:B * NT - sh, :], ALU.add))
                a, b_ = b_, a
            link(tt(cmp[:, :, :], a[:, B * NT - 1, :].unsqueeze(2).broadcast_to([P, E, 16]),
                    step128[:, :].unsqueeze(1).broadcast_to([P, E, 16]), ALU.is_gt))
            link(nc.vector.tensor_reduce(nt_e[:, :], cmp[:, :, :], AX, ALU.add))
            link(nc.vector.tensor_tensor_scan(end_e[:, :], one_e[:, :], nt_e[:, :], 0.0, ALU.mult, ALU.add))
            link(tt(beg_e[:, :], end_e[:, :], nt_e[:, :], ALU.subtract))
            link(nc.vector.tensor_scalar(beg_e[:, :], beg_e[:, :], float(P), None, ALU.mult))
            link(tt(R["pos"][:, :, :], a[:, :, :], ps[:, 1, 128:256].rearrange("p (t e) -> p t e", e=E), ALU.subtract))
            link(tt(R["pos"][:, :, :], R["pos"][:, :, :], ps[:, 1, 0:128].rearrange("p (t e) -> p t e", e=E), ALU.add))
            link(tt(R["pos"][:, :, :], R["pos"][:, :, :], beg_e[:, :].unsqueeze(1).broadcast_to([P, B * NT, E]), ALU.add))
            for oh, sl in (("oh1", "s1"), ("oh2", "s2")):
                link(tt(R["t0"][:, :, :], R[oh][:, :, :], R["pos"][:, :, :], ALU.mult))
                link(nc.vector.tensor_reduce(r1[sl][:, :], R["t0"][:, :, :], AX, ALU.add))
            link(tt(cmpt[:, :, :], tile_no[:, :].unsqueeze(2).broadcast_to([P, TILES, E]),
                    end_e[:, :].unsqueeze(1).broadcast_to([P, TILES, E]), ALU.is_ge))
            link(nc.vector.tensor_reduce(tab_f[:, :], cmpt[:, :, :], AX, ALU.add))
            link(nc.vector.tensor_scalar(table[:, :], tab_f[:, :], float(E - 1), None, ALU.min))
            dve.wait_ge(s["r_exp"], 1)
            link(nc.vector.tensor_scalar(r1["m1"][:, :], r1["e2"][:, :], 1.0, None, ALU.add))
            link(nc.vector.reciprocal(r1["g1"][:, :], r1["m1"][:, :]))
            link(tt(r1["g2"][:, :], r1["e2"][:, :], r1["g1"][:, :], ALU.mult))
            nc.vector.tensor_copy(r1["m2"][:, :], r1["g1"][:, :]).then_inc(s["slots_ready"], 1)
            nc.vector.tensor_copy(r1["i2"][:, :], r1["g1"][:, :]).then_inc(s["table_ready"], 1)

            def expert_tiles(base, n, table_expert):
                def h_out(t):
                    dve.wait_ge(s["h_ps"], base + t + 1)
                    if base or not (isinstance(t, int) and t == 0):
                        dve.wait_ge(s["hT_ps"], base + t)
                    for c in range(2):
                        last = nc.vector.tensor_copy(hp[:, c * 512:(c + 1) * 512], ps[:, 2 + c, :])
                    last.then_inc(s["h_out"], 1)

                def y_sum(t, q, free):
                    e = table_expert(t)
                    dve.wait_ge(s["y_ps"], base + t + 1)
                    if free and base:
                        dve.wait_ge(s["y_out"], t - 1)
                    elif free:
                        dve.wait_ge(shared_sent[q], 8 * (t - q))
                    nc.vector.tensor_tensor(ysum[:, q, :], ps[:, 6, 0:D],
                                            b2b[:, bass.ds(e, 1), :].rearrange("p o d -> p (o d)"), ALU.add)\
                        .then_inc(s["y_sum"], 1)

                h_out(0)
                for t in range(2):
                    h_out(t + 1)
                    y_sum(t, t, False)
                with dve.Fori(1, n // 2 - 1) as i:
                    for q in range(2):
                        h_out(2 * i + q + 1)
                        y_sum(2 * i + q, q, True)
                h_out(n - 1)
                y_sum(n - 2, 0, True)
                y_sum(n - 1, 1, True)

            dve.wait_ge(s["eb_in"], 64)
            expert_tiles(0, T // P, lambda t: 0)
            for q in range(2):
                dve.wait_ge(shared_sent[q], 16 * T // P // 2)
            expert_tiles(T // P, TILES,
                         lambda t: dve.value_load(table[0:1, bass.ds(t, 1)], min_val=0, max_val=E - 1) + 1)

            for b in range(B):
                q = b
                dve.wait_ge(yl_in[b], 32)
                at = 6 * b
                nc.vector.tensor_tensor(fo[:, q, :, :], yl[:, q, :, 0, :], yl[:, q, :, 1, :], ALU.add).then_inc(s["f_step"], 1)
                nc.vector.tensor_tensor(yl[:, q, :, 2, :], yl[:, q, :, 2, :], X[:, NT * b:NT * b + NT, :], ALU.add)\
                    .then_inc(s["f_step"], 1)
                dve.wait_ge(s["f_step"], at + 2)
                nc.vector.tensor_tensor(fo[:, q, :, :], fo[:, q, :, :], yl[:, q, :, 2, :], ALU.add).then_inc(s["f_step"], 1)
                norm(b, "f_step", "f_pow", "f_out", fo[:, q, :, :], fo[:, q, :, :], 2, 6)

        @block.tensor
        def _(pe):
            def attention1(b, first):
                pe.wait_ge(s["xa_lo"], b + 1)
                if first:
                    pe.wait_ge(s["w1_lo"], 1)
                else:
                    pe.wait_ge(s["cb_out"], 2 * b - 1)
                w = W_s[0]
                for j in range(4):
                    for k in range(KD):
                        m = mm3(pe, ps[:, j, :], lambda l: w[:, j // 2, l, k, (j % 2) * P:(j % 2 + 1) * P],
                                lambda l: a_s[:, l, k, :], k == 0, k == KD - 1)
                    m.then_inc(s["qk1_ps"], 1)
                for n in range(NT):
                    for k in range(KD):
                        m = mm3(pe, ps[:, 4 + n // 2, (n % 2) * D:(n % 2 + 1) * D],
                                lambda l: a_s[:, l, k, n * P:(n + 1) * P], lambda l: w[:, 2, l, k, :],
                                k == 0, k == KD - 1)
                    if n % 2:
                        m.then_inc(s["v1_ps"], 1)
                pe.wait_ge(s["qk1_lo"], 4 * b + 4)
                for n in range(NT):
                    wd = max(n + 1, 2) * P
                    for k in range(KD):
                        m = mm3(pe, ps[:, n, 0:wd], lambda l: q_s[:, k, l, n * P:(n + 1) * P],
                                lambda l: k_s[:, k, l, 0:wd], k == 0, k == KD - 1)
                    m.then_inc(s["s1_ps"], 1)
                if first:
                    pe.wait_ge(s["consts"], 5)
                pe.wait_ge(s["v1_lo"], 2 * b + 2)
                for n in range(NT):
                    pe.wait_ge(s["p1_norm"], NT * b + n + 1)
                    for j in range(n + 1):
                        m = nc.tensor.transpose(ps[:, 4 + n, j * P:(j + 1) * P], probs[:, n, j * P:(j + 1) * P], ident[:, :])
                    m.then_inc(s["pt_ps"], 1)
                pe.wait_ge(s["pt_lo"], NT * b + NT)
                for d in range(KD):
                    for j in range(NT):
                        q0 = min(j, NT - 2) * P
                        m = mm3(pe, ps[:, d, q0:S], lambda l: v_s[:, l, j, d * P:(d + 1) * P],
                                lambda l: pT_s[:, l, j, q0:S], j == 0, j == NT - 1, True)
                    m.then_inc(s["o1_ps"], 1)
                pe.wait_ge(s["o1_lo"], 2 * b + 2)
                for n in range(NT):
                    for k in range(KD):
                        m = mm3(pe, ps[:, 2 + n, 0:D], lambda l: c_s[:, l, k, n * P:(n + 1) * P],
                                lambda l: w[:, 3, l, k, :], k == 0, k == KD - 1)
                    m.then_inc(s["w1_ps"], 1)

            def turn_res(bank, name):
                for n in range(NT):
                    for k in range(KD):
                        m = nc.tensor.transpose(ps[:, bank + k, n * P:(n + 1) * P], res[:, n, k * P:(k + 1) * P], ident[:, :])
                m.then_inc(s[name], 1)

            def project2(b, c, first):
                pe.wait_ge(s["ln_out"], c + 1)
                turn_res(4, "x1_ps")
                w = W_s[1]
                if first:
                    pe.wait_ge(s["wsplit"], 4)
                for j, blk in enumerate((0, 0, 1, 1)):
                    if j == 0:
                        pe.wait_ge(s["x1_lo"], b + 1)
                    if j == 1:
                        pe.wait_ge(s["ctx_lo"], b + 1)
                    src = (a_s, c_s)[j % 2]
                    for k in range(KD):
                        m = mm3(pe, ps[:, j, :], lambda l: w[:, j % 2, l, k, blk * P:(blk + 1) * P],
                                lambda l: src[:, l, k, :], k == 0, k == KD - 1)
                    m.then_inc(s["qk2_ps"], 1)

            def half(a, c, ha, hc, full):
                def pv(m):
                    g, i = m // NT, m % NT
                    sides = side_blocks(i)
                    pe.wait_ge(s["b_exp"], UNITS * c + 2 * m + 2)
                    if i == 0 and (full or g):
                        pe.wait_ge(s["oc_out"], 2 * c + g)
                        pe.wait_ge(s["os_out"], 2 * c + g)
                    v = [v_aug[:, i, hc * HALF + 4 * g + j, :] for j in range(4)]
                    for j in range(4):
                        nc.tensor.matmul(ps[32 * j:32 * j + 32, 6, i * P:(i + 1) * P], v[j],
                                         pT[:, m % 2, j // 2, (j % 2) * P:(j % 2 + 1) * P],
                                         start=True, stop=True, skip_group_check=True)
                    w = len(sides) * P
                    for j in range(4):
                        out = ps[32 * j:32 * j + 32, 7, :].rearrange("p (n q) -> p n q", q=P)[:, sides[0]:sides[-1] + 1:2, :]
                        last = nc.tensor.matmul(
                            out, v[j],
                            pT[:, m % 2, j // 2, 2 * P + (j % 2) * w:2 * P + (j % 2 + 1) * w].rearrange("p (n q) -> p n q", q=P),
                            start=i == 0, stop=True, skip_group_check=True)
                    last.then_inc(s["pv_done"], 1)

                if a is not None:
                    pe.wait_ge(s["stacked"], 16 * STACK_DMAS * (a + 1))
                    if full or c is not None:
                        pe.wait_ge(s["augT_out"], a)
                if c is not None:
                    pe.wait_ge(s["aug_in"], 64 * (c + 1))
                for u in range(UNITS):
                    if a is not None:
                        n, p = u // 4, u % 4
                        k0, nb = max(n - 1, 0), 3 if 0 < n < NT - 1 else 2
                        if u:
                            pe.wait_ge(s["a_red"], UNITS * a + u)
                        for j in range(2):
                            m = nc.tensor.matmul(ps[:, 2 + j, 0:nb * P],
                                                 q_stack[0:96, ha * HALF + 2 * p + j, n * P:(n + 1) * P],
                                                 k_stack[0:96, ha * (HALF // 2) + p, k0 * P:(k0 + nb) * P],
                                                 start=True, stop=True)
                        m.then_inc(s["a_ps"], 1)
                    if c is not None:
                        g, i, p = u // 8, (u // 2) % NT, hc * (HALF // 2) + 2 * (u // 8) + u % 2
                        if full or u:
                            pe.wait_ge(s["b_exp"], UNITS * c + u)
                        sides = side_blocks(i)
                        qv = q_stack[:, 2 * p:2 * p + 2, :]
                        nc.tensor.matmul(ps[:, 4, 256:512].rearrange("p (h q) -> p h q", h=2),
                                         k_stack[0:100, p, i * P:(i + 1) * P], qv[0:100, :, i * P:(i + 1) * P],
                                         start=True, stop=True)
                        w = 2 * len(sides) * P
                        nc.tensor.matmul(ps[:, 5, 0:w].rearrange("p (h n q) -> p h n q", h=2, q=P),
                                         k_stack[0:98, p, i * P:(i + 1) * P],
                                         qv[0:98, :, :].rearrange("p h (n q) -> p h n q", q=P)[:, :, sides[0]:sides[-1] + 1:2, :],
                                         start=True, stop=True).then_inc(s["b_ps"], 1)
                        if u % 2 == 0 and u >= 2:
                            pv(u // 2 - 1)
                if c is not None:
                    pv(7)
                if a is not None:
                    pe.wait_ge(s["aug_ready"], a + 1)
                    for n in range(NT):
                        m = nc.tensor.transpose(ps[0:4 * HALF, 2, n * P:(n + 1) * P],
                                                aug[:, n, :, :].rearrange("p r h -> p (r h)").bitcast(F), ident[:, :])
                    m.then_inc(s["augT_ps"], 1)

            def turn_out(c):
                pe.wait_ge(s["oc_out"], 2 * c + 2)
                pe.wait_ge(s["os_out"], 2 * c + 2)
                for n in range(NT):
                    for k in range(2):
                        for g in range(2):
                            m = nc.tensor.transpose(ps[:, n, (2 * k + g) * P:(2 * k + g + 1) * P],
                                                    oT[:, g, k, n * P:(n + 1) * P], ident[:, :])
                m.then_inc(s["cb_ps"], 1)

            def values2(b):
                for n in range(NT):
                    for k in range(KD):
                        m = mm3(pe, ps[:, 4 + n // 2, (n % 2) * D:(n % 2 + 1) * D],
                                lambda l: c_s[:, l, k, n * P:(n + 1) * P], lambda l: W_s[1][:, 2, l, k, :],
                                k == 0, k == KD - 1)
                    if n % 2:
                        m.then_inc(s["v2_ps"], 1)

            def output2(b, c_ln):
                pe.wait_ge(s["cb_out"], 2 * b + 2)
                for n in range(NT):
                    for k in range(KD):
                        m = nc.tensor.transpose(ps[:, 6 + k, n * P:(n + 1) * P], attn[:, n, k * P:(k + 1) * P], ident[:, :])
                m.then_inc(s["at_ps"], 1)
                pe.wait_ge(s["at_lo"], b + 1)
                for n in range(NT):
                    for k in range(KD):
                        m = mm3(pe, ps[:, n, 0:D], lambda l: attnT_s[:, l, k, n * P:(n + 1) * P],
                                lambda l: W_s[1][:, 3, l, k, :], k == 0, k == KD - 1)
                    m.then_inc(s["w2_ps"], 1)
                pe.wait_ge(s["ln_out"], c_ln + 1)
                turn_res(4, "g_ps")
                pe.wait_ge(s["g_out"], b + 1)
                for k in range(KD):
                    m = nc.tensor.matmul(ps[0:E, 6, :], gate_w[:, k, :], x2T[:, k, :], start=k == 0, stop=k == KD - 1)
                m.then_inc(s["lg_ps"], 1)
                pe.wait_ge(s["consts"], 5)
                pe.wait_ge(s["lg_out"], b + 1)
                for n in range(NT):
                    m = nc.tensor.transpose(ps[:, 7, n * E:(n + 1) * E], lgT[:, n * P:(n + 1) * P], ident[0:E, 0:E])
                m.then_inc(s["lgT_ps"], 1)

            def body(b, first):
                attention1(b, first)
                project2(b, 0 if first else 2 * b - 1, first)
                half(2 * b, None if first else 2 * b - 1, 0, 1, not first)
                if not first:
                    pe.wait_ge(s["augT_out"], 2 * b + 1)
                    turn_out(2 * b - 1)
                values2(b)
                if not first:
                    pe.wait_ge(s["v2_out"], 2 * b + 2)
                    output2(b - 1, 2 * b)
                    pe.wait_ge(s["lgT_out"], b)
                pe.wait_ge(s["v2_out"], 2 * b + 2)
                half(2 * b + 1, 2 * b, 1, 0, not first)
                pe.wait_ge(s["augT_out"], 2 * b + 2)
                turn_out(2 * b)

            body(0, True)
            with pe.Fori(1, B) as b:
                body(b, False)
            half(None, 2 * B - 1, 0, 1, True)
            pe.wait_ge(s["cb_out"], 2 * B - 1)
            turn_out(2 * B - 1)
            output2(B - 1, 2 * B - 1)

            pe.wait_ge(s["consts2"], 12)
            pe.wait_ge(s["r_exp_in"], 2)
            mask = R["mask"][:, :, :].rearrange("p t e -> p (t e)")
            nc.tensor.matmul(ps[:, 1, 0:128], upper[:, :], mask, start=True, stop=True).then_inc(s["r_ps"], 1)
            nc.tensor.matmul(ps[:, 1, 128:256], ones[:, :], mask, start=True, stop=True).then_inc(s["r_ps"], 1)

            def expert_tiles(base, n, table_expert, w):
                def turn_x(t, q):
                    pe.wait_ge(xs_in[q], 8 * (base + t - q) + 16)
                    if base or not (isinstance(t, int) and t < 2):
                        pe.wait_ge(s["xT_out"], base + t - 1)
                    for k in range(KD):
                        m = nc.tensor.transpose(ps[:, 7 * q, k * P:(k + 1) * P],
                                                xs[:, q, k * P:(k + 1) * P], ident[:, :])
                    m.then_inc(s["xT_ps"], 1)

                def hidden(t, q):
                    e = table_expert(t)
                    pe.wait_ge(s["xT_out"], base + t + 1)
                    if base or not (isinstance(t, int) and t == 0):
                        pe.wait_ge(s["h_out"], base + t)
                    for c in range(2):
                        for k in range(KD):
                            m = nc.tensor.matmul(
                                ps[:, 2 + c, :], xT[:, q, k, :],
                                w[:, bass.ds(e, 1), k * HID + c * 512:k * HID + (c + 1) * 512].rearrange("p o n -> p (o n)"),
                                start=k == 0, stop=k == KD - 1)
                    m.then_inc(s["h_ps"], 1)

                def turn_h(t):
                    pe.wait_ge(s["h_out"], base + t + 1)
                    if base or not (isinstance(t, int) and t == 0):
                        pe.wait_ge(s["hT_out"], base + t)
                    for c in range(NH):
                        m = nc.tensor.transpose(ps[:, 4 + c // 4, (c % 4) * P:(c % 4 + 1) * P],
                                                hp[:, c * P:(c + 1) * P], ident[:, :])
                    m.then_inc(s["hT_ps"], 1)

                def output(t):
                    e = table_expert(t)
                    pe.wait_ge(s["hT_out"], base + t + 1)
                    if base or not (isinstance(t, int) and t == 0):
                        pe.wait_ge(s["y_sum"], base + t)
                    for c in range(NH):
                        m = nc.tensor.matmul(
                            ps[:, 6, 0:D], hT[:, c, :],
                            w[:, bass.ds(e, 1), KD * HID + c * D:KD * HID + (c + 1) * D].rearrange("p o n -> p (o n)"),
                            start=c == 0, stop=c == NH - 1)
                    m.then_inc(s["y_ps"], 1)

                turn_x(0, 0)
                turn_x(1, 1)
                hidden(0, 0)
                turn_h(0)
                hidden(1, 1)
                output(0)
                turn_x(2, 0)
                turn_h(1)
                hidden(2, 0)
                output(1)
                turn_x(3, 1)
                turn_h(2)
                with pe.Fori(1, n // 2 - 1) as i:
                    t = 2 * i
                    hidden(t + 1, 1)
                    output(t)
                    turn_x(t + 2, 0)
                    turn_h(t + 1)
                    hidden(t + 2, 0)
                    output(t + 1)
                    turn_x(t + 3, 1)
                    turn_h(t + 2)
                hidden(n - 1, 1)
                output(n - 2)
                turn_h(n - 1)
                output(n - 1)

            pe.wait_ge(s["ws_in"], 32)
            expert_tiles(0, T // P, lambda t: 0, ws)
            pe.wait_ge(s["we_in"], 32 * E)
            pe.wait_ge(s["table_ready"], 1)
            expert_tiles(T // P, TILES,
                         lambda t: pe.value_load(table[0:1, bass.ds(t, 1)], min_val=0, max_val=E - 1), we)


_WEIGHTS = ["L0_attn_Wq", "L0_attn_Wk", "L0_attn_Wv", "L0_attn_Wo",
            "L0_xattn_Wq", "L0_xattn_Wk", "L0_xattn_Wv", "L0_xattn_Wo"]


def kernel(**inputs):
    import numpy as np
    import concourse.bacc as bacc
    from concourse.bass_utils import run_bass_kernel_spmd

    a = {n: np.asarray(v) for n, v in inputs.items()}
    lay = {"x": a["x"].reshape(T, D), "xT": a["x"].reshape(T, D).T, "cT": a["ctx_1024"].reshape(T, D).T}
    for n in _WEIGHTS:
        lay[n] = a[n].T if "xattn" in n else a[n]
    lay["brow"] = np.stack([a["L0_attn_bo"], a["L0_xattn_bv"], a["L0_xattn_bo"]])
    lay["bcol"] = np.stack([a[n] for n in ("L0_attn_bq", "L0_attn_bk", "L0_attn_bv", "L0_xattn_bq", "L0_xattn_bk")])
    lay["bcol"] = lay["bcol"].reshape(5 * KD, P).T
    lay["gate_w"], lay["gate_b"] = a["L0_ffn_gate_w"], a["L0_ffn_gate_b"]
    lay["w1"], lay["w2"], lay["b2"] = a["L0_ffn_w1"], a["L0_ffn_w2"], a["L0_ffn_b2"]
    lay["b1T"] = a["L0_ffn_b1"].reshape(E * NH, P).T
    lay["ws1"], lay["ws2"], lay["bs2"] = a["L0_ffn_ws1"], a["L0_ffn_ws2"], a["L0_ffn_bs2"]
    lay["bs1T"] = a["L0_ffn_bs1"].reshape(NH, P).T
    arrays = {f"in_{n}": np.ascontiguousarray(v) for n, v in lay.items()}

    nc = bacc.Bacc("TRN2", target_bir_lowering=False, num_devices=1)
    t = {n: nc.dram_tensor(f"in_{n}", arrays[f"in_{n}"].shape, F, kind="ExternalInput").ap() for n in lay}
    out = nc.dram_tensor("out", (T, D), F, kind="ExternalOutput").ap()
    build(nc, t["x"], t["xT"], t["cT"], [t[n] for n in _WEIGHTS], t["brow"], t["bcol"], t["gate_w"], t["gate_b"],
          t["w1"], t["b1T"], t["w2"], t["b2"], t["ws1"], t["bs1T"], t["ws2"], t["bs2"], out)
    r = run_bass_kernel_spmd(nc, [arrays], core_ids=[0])
    return r.results[0]["out"].reshape(B, S, D)
```

```python
from contextlib import ExitStack

import concourse.bass as bass
from concourse import mybir

F = mybir.dt.float32
FR = mybir.dt.float32r
I32 = mybir.dt.int32
ACT = mybir.ActivationFunctionType
ALU = mybir.AluOpType
AX = mybir.AxisListType.X

P = 128
B, S, D = 4, 512, 256
T = B * S
NT = S // P
KD = D // P
E, HID = 8, 1024
NH = HID // P
HEADS, DH = 16, 16
HALF = HEADS // 2
PT_BANK = (0, 1, 4, 5)
UNITS = 16
SCALE1 = 1.0 / 16.0
SCALE2 = 0.25
NEG = -3.0e38
EPS = 1e-5
TILES = 2 * T // P + E
SLOTS = TILES * P
ROW = D + 2
PARTS = ((0, 0), (0, 1), (1, 0))
PAIRS = HALF // 2
PAIR_DMAS = 3 + 2 * 3


def side_blocks(i):
    return [n for n in (i - 1, i + 1) if 0 <= n < NT]


def build(nc, x_d, xT_d, cT_d, w_d, brow_d, bcol_d, gate_w_d, gate_b_d,
          w1_d, b1T_d, w2_d, b2_d, ws1_d, bs1T_d, ws2_d, bs2_d, out_d):
    ctx = ExitStack()
    with ctx:
        def sb(name, shape, dt=F, stack=ctx):
            return stack.enter_context(nc.sbuf_tensor(name, shape, dt))

        def sem(name):
            return ctx.enter_context(nc.semaphore(name))

        slot_rows = nc.dram_tensor("slot_rows", (SLOTS, ROW), F, kind="Internal").ap()
        pair_out = nc.dram_tensor("pair_out", (2 * T + SLOTS, D), F, kind="Internal").ap()
        shared_out = nc.dram_tensor("shared_out", (T, D), F, kind="Internal").ap()

        X = sb("X", [P, B * NT, D])
        ident = sb("ident", [P, P])
        zero = sb("zero", [P, 1, 1])
        causal = sb("causal", [P, P])
        brow = sb("brow", [P, 3, D])
        bcol = sb("bcol", [P, 5, KD])
        logits = sb("logits", [P, B * NT, E])
        half_pow = sb("half_pow", [P, NT])
        stats = sb("stats", [P, NT, 6])
        mv = sb("mv", [P, NT, 2])
        rstd = sb("rstd", [P, NT])
        var_eps = sb("var_eps", [P, NT])
        gate_w = sb("gate_w", [P, KD, E])
        gate_b = sb("gate_b", [E, 1])
        pad_no = sb("pad_no", [P, TILES], I32)
        pad_end = sb("pad_end", [P, TILES, 2])

        att = ExitStack()
        W_s = [sb("w1_s", [P, 4, 2, KD, D], FR, att)]
        q_stack = sb("q_stack", [P, HEADS, S], FR, att)
        W_s.append(sb("w2_s", [P, 4, 2, KD, D], FR, att))
        k_stack = sb("k_stack", [P, HEADS // 2, S], FR, att)
        a_s = sb("a_s", [P, 2, KD, S], FR, att)
        c_s = sb("c_s", [P, 2, KD, S], FR, att)
        q_s = sb("q_s", [P, KD, 2, S], FR, att)
        k_s = sb("k_s", [P, KD, 2, S], FR, att)
        v_s = sb("v_s", [P, 2, NT, D], FR, att)
        pT_s = sb("pT_s", [P, 2, NT, S], FR, att)
        aug = sb("aug", [P, NT, 4, HALF], FR, att)
        augT = sb("augT", [4 * HALF, S], FR, att)
        x_raw = sb("x_raw", [P, KD, S], F, att)
        c_raw = sb("c_raw", [P, KD, S], F, att)
        v_wait = c_raw[:, :, :].rearrange("p k t -> p (k t)").rearrange("p (n d) -> p n d", n=NT)
        res = sb("res", [P, NT, D], F, att)
        v_aug = sb("v_aug", [P, NT, HEADS, 32], F, att)
        pT = sb("pT", [P, 2, 2, 768], F, att)
        probs = pT[:, :, :, :].rearrange("p a b c -> p (a b c)")[:, 0:NT * S].rearrange(
            "p (n k) -> p n k", n=NT)
        raw2 = v_aug[:, :, :, :].rearrange("p a b c -> p (a b c)").rearrange(
            "p (w k n) -> p w k n", w=4, k=KD)
        attn = sb("attn", [P, NT, D], F, att)
        lgT = attn[:, :, :].rearrange("p n d -> p (n d)")[0:E, 0:S]
        mx = sb("mx", [P, NT, HALF, 3], F, att)
        ncross = sb("ncross", [P, NT, HALF], F, att)
        dloc = sb("dloc", [P, 2, NT, HALF], F, att)
        wloc = sb("wloc", [P, NT, HALF], F, att)
        cw = sb("cw", [P, 4, NT, HALF], F, att)
        cmb = sb("cmb", [P, NT, HALF, DH], F, att)
        nmax = sb("nmax", [P, 2, NT], F, att)
        den = sb("den", [P, 2, NT], F, att)
        turned = ExitStack()
        oT = sb("oT", [P, 2, 2, S], F, turned)
        oT_flat = oT[:, :, :, :].rearrange("p a b c -> p (a b c)")
        x2T = oT_flat[:, 0:KD * S].rearrange("p (k t) -> p k t", k=KD)
        raw1 = oT_flat[:, 0:4 * KD * D].rearrange("p (w k n) -> p w k n", w=4, k=KD)
        turned.close()
        q1_s = sb("q1_s", [P, 2, KD, S], FR, att)
        att.close()

        mo = ExitStack()
        ws = sb("ws", [P, 1, 4096], F, mo)
        we = sb("we", [P, E, 4096], F, mo)
        b1T = sb("b1T", [P, (E + 1) * NH], F, mo)
        b2b = sb("b2b", [P, E + 1, D], F, mo)
        xs = sb("xs", [P, 2, D], F, mo)
        meta = sb("meta", [P, TILES, 2], F, mo)
        xT = sb("xT", [P, 2, KD, P], F, mo)
        hp = sb("hp", [P, HID], F, mo)
        hT = sb("hT", [P, NH, P], F, mo)
        ysum = sb("ysum", [P, 2, D], F, mo)
        yw = sb("yw", [P, 2, D], F, mo)
        stage = sb("stage", [P, 2, ROW], F, mo)
        yidx = sb("yidx", [P, 2, 1], I32, mo)
        sidx = sb("sidx", [P, 2, 1], I32, mo)
        upper = sb("upper", [P, P], F, mo)
        ones = sb("ones", [P, P], F, mo)
        desc8 = sb("desc8", [P, E], F, mo)
        step128 = sb("step128", [P, 16], F, mo)
        tile_no = sb("tile_no", [P, TILES], F, mo)
        ids = sb("ids", [P, 2, B * NT], F, mo)
        R = {n: sb("r_" + n, [P, B * NT, E], F, mo) for n in
             ("t0", "oh1", "oh2", "lg2", "mask", "c0", "c1", "pos")}
        r1 = {n: sb("r1_" + n, [P, B * NT], F, mo) for n in ("m1", "i1", "m2", "i2", "e2", "g1", "g2", "s1", "s2")}
        cmp = sb("cmp", [P, E, 16], F, mo)
        cmpt = sb("cmpt", [P, TILES, E], F, mo)
        nt_e = sb("nt_e", [P, E], F, mo)
        end_e = sb("end_e", [P, E], F, mo)
        beg_e = sb("beg_e", [P, E], F, mo)
        one_e = sb("one_e", [P, E], F, mo)
        tab_f = sb("tab_f", [P, TILES], F, mo)
        table = sb("table", [P, TILES], I32, mo)
        mo.close()
        fin = ExitStack()
        yl = sb("yl", [P, B, NT, 3, D], F, fin)
        fo = sb("fo", [P, B, NT, D], F, fin)
        fin.close()

        ps = ctx.enter_context(nc.psum_tensor("ps", [P, 8, 512], F))

        names = """x_in w1_in w2_in w1_hi w1_lo b_in x_raw_in c_raw_in wsplit wsplit_hi consts consts2 masks xbo pad_set pad_out
          xa_hi xa_lo qk1_ps qk1_hi qk1_lo v1_ps v1_hi v1_lo s1_ps s1_step s1_max s1_exp p1_step p1_norm
          pt_ps pt_hi pt_lo o1_ps o1_hi o1_lo w1_ps ln_step ln_pow ln_out x_kept zeroed
          x1_ps x1_hi x1_lo ctx_hi ctx_lo qk2_ps qk2_hi qk2_lo aug_in v_set
          a_ps a_red aug_step aug_ready augT_ps augT_out b_ps b_exp pv_done oc_out os_out
          cb_ps w_exp cb_step cb_out v2_ps v2_out at_ps at_hi at_lo w2_ps
          g_ps g_out lg_ps lg_out lgT_ps lgT_out
          ws_in we_in eb_in r_step r_exp r_exp_in r_ps table_ready slots_ready st_step st_out
          xT_ps xT_out meta_in h_ps h_out hT_ps hT_out y_ps y_sum y_out y_idx
          f_step f_pow f_out o_sent
          """.split()
        s = {n: sem("s_" + n) for n in names}
        xs_in, yw_sent, shared_sent = ([sem(f"s_{n}{q}") for q in range(2)] for n in ("xs_in", "yw_sent", "shared_sent"))
        stacked = [sem(f"s_stacked{p}") for p in range(PAIRS)]
        yl_in = [sem(f"s_yl_in{b}") for b in range(B)]

        block = ctx.enter_context(nc.Block())

        def mm3(pe, out, lhs, rhs, first=True, last=True, check=False):
            for n, (a, b) in enumerate(PARTS):
                m = nc.tensor.matmul(out, lhs(a), rhs(b), start=first and n == 0,
                                     stop=last and n == 2, skip_group_check=check)
            return m

        @block.sync
        def _(sp):
            for i in range(4):
                sp.dma_start(raw1[:, i, :, :], w_d[i].rearrange("(k p) n -> p k n", p=P)).then_inc(s["w1_in"], 16)
            sp.dma_start(x_raw[:, :, :], xT_d[:, 0:S].rearrange("(k p) t -> p k t", p=P)).then_inc(s["x_raw_in"], 16)
            sp.dma_start(bcol[:, :, :].rearrange("p i k -> p (i k)"), bcol_d).then_inc(s["b_in"], 16)
            sp.dma_start(brow[:, :, :], brow_d.partition_broadcast(P)).then_inc(s["b_in"], 16)
            sp.dma_start(gate_w[:, :, :], gate_w_d.rearrange("(k p) e -> p k e", p=P)).then_inc(s["b_in"], 16)
            sp.dma_start(gate_b[:, :], gate_b_d.rearrange("(e o) -> e o", o=1)).then_inc(s["b_in"], 16)
            for i in range(4):
                sp.dma_start(raw2[:, i, :, :], w_d[4 + i].rearrange("(k p) n -> p k n", p=P)).then_inc(s["w2_in"], 16)
            for b in range(B):
                sp.dma_start(X[:, NT * b:NT * b + NT, :],
                             x_d[b * S:(b + 1) * S, :].rearrange("(n p) d -> p n d", p=P)).then_inc(s["x_in"], 16)
            sp.dma_start(c_raw[:, :, :], cT_d[:, 0:S].rearrange("(k p) t -> p k t", p=P)).then_inc(s["c_raw_in"], 16)

            sp.wait_ge(s["pad_set"], 4)
            sp.dma_start(slot_rows[:, 0:D].rearrange("(i p) d -> p i d", p=P),
                         attn[:, 0:1, :].broadcast_to([P, TILES, D])).then_inc(s["pad_out"], 16)
            sp.dma_start(slot_rows[:, D:].rearrange("(i p) d -> p i d", p=P), pad_end[:, :, :]).then_inc(s["pad_out"], 16)

            def stack(h):
                for g in range(PAIRS):
                    for sec, part in enumerate((0, 1, 0)):
                        sp.dma_start(k_stack[32 * sec:32 * sec + 32, h * PAIRS + g, :].bitcast(F),
                                     k_s[32 * g:32 * g + 32, h, part, :].bitcast(F)).then_inc(stacked[g], 16)
                    for head in (2 * g, 2 * g + 1):
                        for sec, part in enumerate((0, 0, 1)):
                            r = 32 * sec + 16 * (head % 2)
                            sp.dma_start(q_stack[r:r + 16, h * HALF + head, :].bitcast(F),
                                         q_s[16 * head:16 * head + 16, h, part, :].bitcast(F)).then_inc(stacked[g], 16)

            def aug_rows(b, h):
                sp.wait_ge(s["augT_out"], 2 * b + h + 1)
                for r in range(4):
                    sp.dma_start(q_stack[96 + r:97 + r, h * HALF:(h + 1) * HALF, :].bitcast(F),
                                 augT[r * HALF:(r + 1) * HALF, :].bitcast(F)).then_inc(s["aug_in"], 16)

            def body(b, first, last):
                nb = (b + 1) % B
                sp.wait_ge(s["qk2_lo"], 4 * b + 2)
                if first:
                    sp.wait_ge(s["masks"], 2)
                else:
                    sp.wait_ge(s["b_ps"], UNITS * (2 * b - 1))
                stack(0)
                if not last:
                    sp.wait_ge(s["xa_lo"], b + 1)
                    sp.dma_start(x_raw[:, :, :], xT_d[:, bass.ts(nb, S)].rearrange("(k p) t -> p k t", p=P))\
                        .then_inc(s["x_raw_in"], 16)
                aug_rows(b, 0)
                if not first:
                    sp.wait_ge(s["b_ps"], UNITS * (2 * b))
                stack(1)
                if not last:
                    sp.wait_ge(s["v_set"], b + 1)
                    sp.dma_start(c_raw[:, :, :], cT_d[:, bass.ts(nb, S)].rearrange("(k p) t -> p k t", p=P))\
                        .then_inc(s["c_raw_in"], 16)
                aug_rows(b, 1)

            body(0, True, False)
            with sp.Fori(1, B - 1) as b:
                body(b, False, False)
            sp.wait_ge(s["w1_ps"], 2 * B)
            sp.dma_start(ws[:, 0, 0:KD * HID].rearrange("p (k n) -> p k n", k=KD),
                         ws1_d.rearrange("(k p) n -> p k n", p=P)).then_inc(s["ws_in"], 16)
            sp.dma_start(ws[:, 0, KD * HID:].rearrange("p (k n) -> p k n", k=NH),
                         ws2_d.rearrange("(k p) n -> p k n", p=P)).then_inc(s["ws_in"], 16)
            body(B - 1, False, True)

            sp.wait_ge(s["lgT_out"], B)
            sp.wait_ge(s["x_kept"], 2 * B)
            sp.wait_ge(s["pad_out"], 32)
            for q in range(2):
                sp.dma_start(xs[:, q, :], X[:, q, :]).then_inc(xs_in[q], 16)
            sp.dma_start(b1T[:, 0:NH], bs1T_d).then_inc(s["eb_in"], 16)
            sp.dma_start(b1T[:, NH:], b1T_d).then_inc(s["eb_in"], 16)
            sp.dma_start(b2b[:, 0, :], bs2_d.partition_broadcast(P)).then_inc(s["eb_in"], 16)
            sp.dma_start(b2b[:, 1:, :], b2_d.partition_broadcast(P)).then_inc(s["eb_in"], 16)
            def shared_tile(t, q, last):
                if not last:
                    sp.wait_ge(s["xT_ps"], t + 1)
                    sp.dma_start(xs[:, q, :], X[:, bass.ds(t + 2, 1), :].rearrange("p o d -> p (o d)"))\
                        .then_inc(xs_in[q], 16)
                sp.wait_ge(s["y_sum"], t + 1)
                sp.dma_start(shared_out[bass.ts(t, P), :], ysum[:, q, :]).then_inc(shared_sent[q], 16)

            def load_expert(e):
                sp.dma_start(we[:, bass.ds(e, 1), 0:KD * HID].rearrange("p o (k n) -> p (o k) n", k=KD),
                             w1_d[bass.ds(e, 1)].rearrange("o (k p) n -> p (o k) n", p=P)).then_inc(s["we_in"], 16)
                sp.dma_start(we[:, bass.ds(e, 1), KD * HID:].rearrange("p o (k n) -> p (o k) n", k=NH),
                             w2_d[bass.ds(e, 1)].rearrange("o (k p) n -> p (o k) n", p=P)).then_inc(s["we_in"], 16)

            with sp.Fori(0, T // P // 2 - 1) as i:
                load_expert(i)
                for q in range(2):
                    shared_tile(2 * i + q, q, False)
            load_expert(E - 1)
            for q in range(2):
                shared_tile(T // P - 2 + q, q, True)
            sp.wait_ge(s["st_out"], 16 * 2 * T // P)
            for q in range(2):
                sp.dma_start(xs[:, q, :], slot_rows[q * P:(q + 1) * P, 0:D]).then_inc(xs_in[q], 16)
            sp.dma_start(meta[:, :, :], slot_rows[:, D:].rearrange("(i p) m -> p i m", p=P)).then_inc(s["meta_in"], 16)
            with sp.Fori(0, TILES // 2 - 1) as i:
                for q in range(2):
                    t = 2 * i + q
                    sp.wait_ge(s["xT_ps"], T // P + t + 1)
                    sp.dma_start(xs[:, q, :], slot_rows[bass.ts(t + 2, P), 0:D]).then_inc(xs_in[q], 16)
            for q in range(2):
                sp.wait_ge(yw_sent[q], 16 * TILES // 2)
                sp.wait_ge(shared_sent[q], 16 * T // P // 2)
            sp.wait_ge(s["y_ps"], T // P + TILES)
            for b in range(B):
                sp.dma_start(yl[:, b, :, 0:2, :],
                             pair_out[2 * b * S:2 * (b + 1) * S, :].rearrange("(n p k) d -> p n k d", p=P, k=2))\
                    .then_inc(yl_in[b], 16)
                sp.dma_start(yl[:, b, :, 2, :],
                             shared_out[b * S:(b + 1) * S, :].rearrange("(n p) d -> p n d", p=P))\
                    .then_inc(yl_in[b], 16)
            for b in range(B):
                sp.wait_ge(s["f_out"], b + 1)
                sp.dma_start(out_d[b * S:(b + 1) * S, :].rearrange("(n p) d -> p n d", p=P),
                             fo[:, b, :, :]).then_inc(s["o_sent"], 16)
            sp.wait_ge(s["o_sent"], 16 * B)

        @block.gpsimd
        def _(pool):
            def split(dst, src, free, hi, lo, n):
                for sem_, value in free:
                    pool.wait_ge(s[sem_], value)
                nc.gpsimd.tensor_tensor(dst[:, 0, :, :], src[:, :, :], zero[:, :, :].broadcast_to([P, KD, S]), ALU.add)\
                    .then_inc(s[hi], 1)
                pool.wait_ge(s[hi], n + 1)
                nc.gpsimd.tensor_tensor(dst[:, 1, :, :], src[:, :, :], dst[:, 0, :, :].bitcast(F), ALU.subtract)\
                    .then_inc(s[lo], 1)

            nc.gpsimd.memset(zero[:, :, :], 0.0).then_inc(s["zeroed"], 1)
            pool.wait_ge(s["zeroed"], 1)
            split(a_s, x_raw, (("x_raw_in", 16),), "xa_hi", "xa_lo", 0)
            nc.gpsimd.memset(ident[:, :], 0.0).then_inc(s["consts"], 1)
            nc.gpsimd.memset(causal[:, :], 0.0).then_inc(s["consts"], 1)
            nc.gpsimd.memset(half_pow[:, :], -0.5).then_inc(s["consts"], 1)
            pool.wait_ge(s["consts"], 3)
            nc.gpsimd.affine_select(out=ident[:, :], in_=ident[:, :], compare_op=ALU.not_equal, fill=1.0,
                                    base=0, pattern=[[-1, P]], channel_multiplier=1).then_inc(s["consts"], 1)
            nc.gpsimd.affine_select(out=causal[:, :], in_=causal[:, :], compare_op=ALU.is_ge, fill=NEG,
                                    base=0, pattern=[[-1, P]], channel_multiplier=1).then_inc(s["consts"], 1)
            nc.gpsimd.memset(attn[:, 0, :], 0.0).then_inc(s["pad_set"], 1)
            nc.gpsimd.memset(pad_end[:, :, :], 0.0).then_inc(s["pad_set"], 1)
            nc.gpsimd.iota(pad_no[:, :], pattern=[[P, TILES]], base=2 * T, channel_multiplier=1).then_inc(s["pad_set"], 1)
            pool.wait_ge(s["pad_set"], 3)
            nc.gpsimd.tensor_copy(pad_end[:, :, 0], pad_no[:, :]).then_inc(s["pad_set"], 1)
            pool.wait_ge(s["w2_in"], 16 * 4)
            for i in range(4):
                nc.gpsimd.tensor_copy(W_s[1][:, i, 0, :, :], raw2[:, i, :, :]).then_inc(s["wsplit_hi"], 1)
            for i in range(4):
                pool.wait_ge(s["wsplit_hi"], i + 1)
                nc.gpsimd.tensor_tensor(W_s[1][:, i, 1, :, :], raw2[:, i, :, :],
                                        W_s[1][:, i, 0, :, :].bitcast(F), ALU.subtract).then_inc(s["wsplit"], 1)
            nc.gpsimd.memset(q_stack[:, :, :].bitcast(F), 0.0).then_inc(s["masks"], 1)
            pool.wait_ge(s["masks"], 1)
            nc.gpsimd.memset(k_stack[96:P, :, :].bitcast(F), 1.0).then_inc(s["masks"], 1)
            pool.wait_ge(s["masks"], 2)
            nc.gpsimd.memset(pT_s[:, :, :, :].bitcast(F), 0.0).then_inc(s["masks"], 1)
            nc.gpsimd.memset(mx[:, :, :, :], -NEG).then_inc(s["masks"], 1)
            pool.wait_ge(s["wsplit"], 4)
            nc.gpsimd.memset(v_aug[:, :, :, :], 0.0).then_inc(s["masks"], 1)
            pool.wait_ge(s["masks"], 5)
            nc.gpsimd.memset(v_aug[:, :, :, DH:DH + 1], 1.0).then_inc(s["masks"], 1)
            pool.wait_ge(s["b_in"], 64)
            pool.wait_ge(s["x_in"], 16 * B)
            for b in range(B):
                Xb = X[:, NT * b:NT * b + NT, :]
                nc.gpsimd.tensor_tensor(Xb, Xb, brow[:, 0:1, :].broadcast_to([P, NT, D]), ALU.add)\
                    .then_inc(s["xbo"], 1)

            def norm_pow(c):
                pool.wait_ge(s["ln_step"], 4 * c + 4)
                nc.gpsimd.tensor_tensor(rstd[:, :], var_eps[:, :], half_pow[:, :], ALU.pow).then_inc(s["ln_pow"], 1)

            def keep(b, c, bias):
                pool.wait_ge(s["ln_out"], c + 1)
                Xb = X[:, bass.ts(b, NT), :]
                if bias:
                    nc.gpsimd.tensor_tensor(Xb, res[:, :, :], brow[:, 2:3, :].broadcast_to([P, NT, D]), ALU.add)\
                        .then_inc(s["x_kept"], 1)
                else:
                    nc.gpsimd.tensor_copy(Xb, res[:, :, :]).then_inc(s["x_kept"], 1)

            def body(b, first, last):
                if not last:
                    split(a_s, x_raw, (("x_raw_in", 16 * b + 32), ("qk2_ps", 4 * b + 4)), "xa_hi", "xa_lo", b + 1)
                if not first:
                    pool.wait_ge(s["pv_done"], 8 * 2 * b)
                pool.wait_ge(s["v2_out"], 2 * b + 2)
                nc.gpsimd.tensor_tensor(v_aug[:, :, :, 0:DH], v_wait.rearrange("p n (h d) -> p n h d", d=DH),
                                        brow[:, 1:2, :].rearrange("p o (h d) -> p o h d", d=DH)
                                        .broadcast_to([P, NT, HEADS, DH]), ALU.add)\
                    .then_inc(s["v_set"], 1)
                if not first:
                    norm_pow(2 * b)
                    keep(b - 1, 2 * b, False)
                if not last:
                    norm_pow(2 * b + 1)
                    keep(b + 1, 2 * b + 1, True)
                    split(c_s, c_raw, (("w1_ps", 2 * b + 4), ("c_raw_in", 16 * b + 32)), "ctx_hi", "ctx_lo", b + 1)

            norm_pow(0)
            keep(0, 0, True)
            split(c_s, c_raw, (("w1_ps", 2), ("c_raw_in", 16)), "ctx_hi", "ctx_lo", 0)
            pool.wait_ge(s["masks"], 6)
            body(0, True, False)
            with pool.Fori(1, B - 1) as b:
                body(b, False, False)
            body(B - 1, False, True)
            norm_pow(2 * B - 1)
            keep(B - 1, 2 * B - 1, False)

            pool.wait_ge(s["lgT_out"], B)
            pool.wait_ge(s["x_kept"], 2 * B)
            nc.gpsimd.memset(upper[:, :], 1.0).then_inc(s["consts2"], 1)
            nc.gpsimd.memset(ones[:, :], 1.0).then_inc(s["consts2"], 1)
            nc.gpsimd.memset(one_e[:, :], 1.0).then_inc(s["consts2"], 1)
            nc.gpsimd.iota(R["t0"][:, 0:1, :].bitcast(I32), pattern=[[0, 1], [-1, E]], base=E, channel_multiplier=0)\
                .then_inc(s["consts2"], 1)
            nc.gpsimd.iota(R["lg2"][:, 0:2, :].bitcast(I32), pattern=[[P * E, 2], [P, E]], base=0, channel_multiplier=0)\
                .then_inc(s["consts2"], 1)
            nc.gpsimd.iota(table[:, :], pattern=[[1, TILES]], base=0, channel_multiplier=0).then_inc(s["consts2"], 1)
            nc.gpsimd.iota(R["mask"][:, 0:4, :].bitcast(I32).rearrange("p (k a) e -> p k (a e)", k=2),
                           pattern=[[1, 2], [2 * P, B * NT]], base=0, channel_multiplier=2).then_inc(s["consts2"], 1)
            pool.wait_ge(s["consts2"], 7)
            nc.gpsimd.affine_select(out=upper[:, :], in_=upper[:, :], compare_op=ALU.is_ge, fill=0.0,
                                    base=-1, pattern=[[1, P]], channel_multiplier=-1).then_inc(s["consts2"], 1)
            nc.gpsimd.tensor_copy(desc8[:, :], R["t0"][:, 0, :].bitcast(I32)).then_inc(s["consts2"], 1)
            nc.gpsimd.tensor_copy(step128[:, :].rearrange("p (a b) -> p a b", a=2), R["lg2"][:, 0:2, :].bitcast(I32))\
                .then_inc(s["consts2"], 1)
            nc.gpsimd.tensor_copy(tile_no[:, :], table[:, :]).then_inc(s["consts2"], 1)
            nc.gpsimd.tensor_copy(ids[:, :, :].rearrange("p k t -> p (k t)"),
                                  R["mask"][:, 0:4, :].bitcast(I32).rearrange("p a e -> p (a e)"))\
                .then_inc(s["consts2"], 1)

            pool.wait_ge(s["consts2"], 12)
            pool.wait_ge(s["pad_out"], 32)
            pool.wait_ge(s["slots_ready"], 1)
            with pool.Fori(1, T // P + 1) as u:
                t = u - 1
                for k, (g, sl) in enumerate((("g1", "s1"), ("g2", "s2"))):
                    st = stage[:, k, :]
                    nc.gpsimd.tensor_copy(st[:, 0:D], X[:, bass.ds(t, 1), :].rearrange("p o d -> p (o d)"))
                    nc.gpsimd.tensor_copy(st[:, D:D + 1], ids[:, k, bass.ds(t, 1)])
                    nc.gpsimd.tensor_copy(st[:, D + 1:D + 2], r1[g][:, bass.ds(t, 1)])
                    last = nc.gpsimd.tensor_copy(sidx[:, k, :], r1[sl][:, bass.ds(t, 1)])
                last.then_inc(s["st_step"], 1)
                pool.wait_ge(s["slots_ready"], 1)
                pool.wait_ge(s["st_step"], u)
                for k in range(2):
                    pool.indirect_dma_start(
                        out=slot_rows, out_offset=bass.IndirectOffsetOnAxis(ap=sidx[:, k, :], axis=0),
                        in_=stage[:, k, :], in_offset=None).then_inc(s["st_out"], 16)
                pool.wait_ge(s["st_out"], 32 * u)

            pool.wait_ge(s["meta_in"], 16)
            with pool.Fori(0, TILES // 2) as i:
                for q in range(2):
                    t = 2 * i + q
                    pool.wait_ge(s["y_out"], t + 1)
                    nc.gpsimd.tensor_copy(yidx[:, q, :], meta[:, bass.ds(t, 1), 0]).then_inc(s["y_idx"], 1)
                    pool.wait_ge(s["meta_in"], 16)
                    pool.wait_ge(s["y_idx"], t + 1)
                    pool.indirect_dma_start(
                        out=pair_out, out_offset=bass.IndirectOffsetOnAxis(ap=yidx[:, q, :], axis=0),
                        in_=yw[:, q, :], in_offset=None).then_inc(yw_sent[q], 16)
            for b in range(B):
                pool.wait_ge(s["f_step"], 6 * b + 6)
                nc.gpsimd.tensor_tensor(rstd[:, :], var_eps[:, :], half_pow[:, :], ALU.pow).then_inc(s["f_pow"], 1)

        @block.scalar
        def _(act):
            def copy(out, in_, name):
                nc.scalar.activation(out, in_, ACT.Copy).then_inc(s[name], 1)

            def copy_bias(out, in_, bias, name):
                nc.scalar.activation(out, in_, ACT.Identity, bias=bias).then_inc(s[name], 1)

            def glue_and_attention1(g, n):
                if g is not None:
                    act.wait_ge(s["cb_out"], 2 * g + 1)
                    local_weight(2 * g + 1, 1)
                if n is not None:
                    for j in range(4):
                        act.wait_ge(s["qk1_ps"], 4 * n + j + 1)
                        copy_bias((q1_s, c_s)[j // 2][:, 0, j % 2, :], ps[:, 4 + j, :],
                                  bcol[:, j // 2, j % 2:j % 2 + 1], "qk1_hi")
                    for j in range(2):
                        act.wait_ge(s["v1_ps"], 2 * n + j + 1)
                        copy(v_s[:, 0, 2 * j:2 * j + 2, :], ps[:, j, :].rearrange("p (n d) -> p n d", n=2), "v1_hi")
                if g is not None:
                    act.wait_ge(s["at_ps"], g + 1)
                    copy(a_s[:, 0, :, :], ps[:, 2:4, :], "at_hi")

                def expo(i):
                    act.wait_ge(s["s1_max"], NT * n + i + 1)
                    w = (i + 1) * P
                    nc.scalar.activation(probs[:, i, 0:w], ps[:, 4 + i, 0:w], ACT.Exp, bias=nmax[:, 1, i:i + 1],
                                         scale=SCALE1, accum_out=den[:, 0, i:i + 1]).then_inc(s["s1_exp"], 1)

                def turned(i):
                    act.wait_ge(s["pt_ps"], NT * n + i + 1)
                    copy(pT_s[:, 0, 0:i + 1, i * P:(i + 1) * P],
                         ps[:, PT_BANK[i], 0:(i + 1) * P].rearrange("p (j q) -> p j q", q=P), "pt_hi")

                if n is not None:
                    if isinstance(n, int) and n == 0:
                        act.wait_ge(s["masks"], 3)
                    expo(0)
                    expo(1)
                    turned(0)
                    expo(2)
                    turned(1)
                    expo(3)
                    turned(2)
                    turned(3)
                    for j in range(2):
                        act.wait_ge(s["o1_ps"], 2 * n + j + 1)
                        copy_bias(c_s[:, 0, j, :], ps[:, 6 + j, :], bcol[:, 2, j:j + 1], "o1_hi")
                if g is not None:
                    act.wait_ge(s["g_ps"], g + 1)
                    copy(x2T, ps[:, 2:4, :], "g_out")

            def project2(b, first):
                act.wait_ge(s["x1_ps"], b + 1)
                copy(a_s[:, 0, :, :], ps[:, 0:2, :], "x1_hi")
                if not first:
                    for p in range(PAIRS):
                        act.wait_ge(stacked[p], 16 * PAIR_DMAS * 2 * b)
                for j, (dst, blk) in enumerate(((k_s, 0), (q_s, 0), (k_s, 1), (q_s, 1))):
                    act.wait_ge(s["qk2_ps"], 4 * b + j + 1)
                    copy_bias(dst[:, blk, 0, :], ps[:, 4 + j, :], bcol[:, 4 - j % 2, blk:blk + 1], "qk2_hi")

            def half(a, c, free):
                if c is not None:
                    for u in range(UNITS):
                        m, i = u // 2, (u // 2) % NT
                        w = 2 * P * (1 + len(side_blocks(i)))
                        act.wait_ge(s["b_ps"], UNITS * c + u + 1)
                        if m >= 2:
                            act.wait_ge(s["pv_done"], 8 * c + m - 1)
                        nc.scalar.activation(pT[:, m % 2, u % 2, 0:w],
                                             ps[:, 4:6, :].rearrange("p a c -> p (a c)")[:, 256:256 + w],
                                             ACT.Exp, scale=SCALE2).then_inc(s["b_exp"], 1)
                        if u == 9:
                            out_local(c, 0)
                    out_local(c, 1)
                if a is not None:
                    if free:
                        act.wait_ge(s["aug_in"], 64 * a)
                    act.wait_ge(s["augT_ps"], a + 1)
                    copy(augT[:, :], ps[0:4 * HALF, 2, :], "augT_out")

            def out_local(c, g):
                act.wait_ge(s["pv_done"], 8 * c + 4 * g + 4)
                copy(oT[:, g, 0, :], ps[:, 6, :], "oc_out")

            def local_weight(c, h):
                nc.scalar.activation(wloc[:, :, :], dloc[:, h, :, :], ACT.Exp, scale=-SCALE2).then_inc(s["w_exp"], 1)

            def body(b, first, last):
                half(2 * b, None if first else 2 * b - 1, not first)
                glue_and_attention1(None if first else b - 1, None if last else b + 1)
                half(2 * b + 1, 2 * b, True)
                if not last:
                    project2(b + 1, False)
                if not first:
                    act.wait_ge(s["cb_out"], 2 * b)
                local_weight(2 * b, 0)

            act.wait_ge(s["b_in"], 64)
            glue_and_attention1(None, 0)
            project2(0, True)
            body(0, True, False)
            with act.Fori(1, B - 1) as b:
                body(b, False, False)
            body(B - 1, False, True)
            half(None, 2 * B - 1, True)
            glue_and_attention1(B - 1, None)

            act.wait_ge(s["r_exp_in"], 1)
            nc.scalar.activation(r1["e2"][:, :], r1["e2"][:, :], ACT.Exp).then_inc(s["r_exp"], 1)

            def expert_tiles(base, n, table_expert, weigh):
                def x_out(t, q, reused=True):
                    if base or reused:
                        act.wait_ge(s["h_ps"], base + t - 1)
                    act.wait_ge(s["xT_ps"], base + t + 1)
                    copy(xT[:, q, :, :], ps[:, 7 * q, 0:KD * P].rearrange("p (k t) -> p k t", k=KD), "xT_out")

                def gelu(t, q):
                    e = table_expert(t)
                    act.wait_ge(s["hT_ps"], base + t + 1)
                    for c in range(NH):
                        last = nc.scalar.activation(hT[:, c, :], ps[:, 4 + c // 4, (c % 4) * P:(c % 4 + 1) * P],
                                                    ACT.Gelu, bias=b1T[:, bass.ds(e * NH + c, 1)])
                    last.then_inc(s["hT_out"], 1)

                def weight(t, q):
                    act.wait_ge(s["meta_in"], 16)
                    act.wait_ge(s["y_sum"], base + t + 1)
                    if not (isinstance(t, int) and t < 2):
                        act.wait_ge(yw_sent[q], 8 * (t - q))
                    nc.scalar.activation(yw[:, q, :], ysum[:, q, :], ACT.Copy, scale=meta[:, bass.ds(t, 1), 1])\
                        .then_inc(s["y_out"], 1)

                def step(t, q, end=False):
                    if not (end and q >= 0):
                        x_out(t + 2, q)
                    if not (end and q == 1):
                        gelu(t + 1, 1 - q)
                    if weigh:
                        weight(t, q)

                x_out(0, 0, False)
                x_out(1, 1, False)
                gelu(0, 0)
                step(0, 0)
                step(1, 1)
                with act.Fori(1, n // 2 - 1) as i:
                    step(2 * i, 0)
                    step(2 * i + 1, 1)
                step(n - 2, 0, True)
                step(n - 1, 1, True)

            act.wait_ge(s["eb_in"], 64)
            expert_tiles(0, T // P, lambda t: 0, False)
            act.wait_ge(s["table_ready"], 1)
            expert_tiles(T // P, TILES,
                         lambda t: act.value_load(table[0:1, bass.ds(t, 1)], min_val=0, max_val=E - 1) + 1, True)

        @block.vector
        def _(dve):
            def lo_of(out, full, hi, name):
                nc.vector.tensor_tensor(out, full, hi.bitcast(F), ALU.subtract).then_inc(s[name], 1)

            def lo_of_bias(out, full, bias, hi, name):
                nc.vector.scalar_tensor_tensor(out=out, in0=full, scalar=bias, in1=hi.bitcast(F),
                                               op0=ALU.add, op1=ALU.subtract).then_inc(s[name], 1)

            dve.wait_ge(s["w1_in"], 64)
            nc.vector.tensor_copy(W_s[0][:, :, 0, :, :].rearrange("p w k n -> p w (k n)"),
                                  raw1[:, :, :, :].rearrange("p w k n -> p w (k n)")).then_inc(s["w1_hi"], 1)
            dve.wait_ge(s["w1_hi"], 1)
            nc.vector.tensor_tensor(W_s[0][:, :, 1, :, :].rearrange("p w k n -> p w (k n)"),
                                    raw1[:, :, :, :].rearrange("p w k n -> p w (k n)"),
                                    W_s[0][:, :, 0, :, :].rearrange("p w k n -> p w (k n)").bitcast(F),
                                    ALU.subtract).then_inc(s["w1_lo"], 1)

            def norm_stats(c, step="ln_step", src=None, first_steps=0, per=4):
                src = res if src is None else src
                at = per * c + first_steps
                dve.wait_ge(s[step], at + 1)
                for n in range(NT):
                    last = nc.vector.bn_stats(stats[:, n, :], src[:, n, :])
                last.then_inc(s[step], 1)
                dve.wait_ge(s[step], at + 2)
                nc.vector.memset(var_eps[:, :], 0.0)
                for n in range(NT):
                    last = nc.vector.bn_aggr(mv[:, n, :], stats[:, n, :])
                last.then_inc(s[step], 1)
                dve.wait_ge(s[step], at + 3)
                nc.vector.tensor_scalar(var_eps[:, :], mv[:, :, 1], EPS, None, ALU.add).then_inc(s[step], 1)

            def norm_apply(c, pow_="ln_pow", out="ln_out", rows=None):
                rows = res if rows is None else rows
                dve.wait_ge(s[pow_], c + 1)
                for n in range(NT):
                    last = nc.vector.tensor_scalar(rows[:, n, :], rows[:, n, :], mv[:, n, 0:1], rstd[:, n:n + 1],
                                                   ALU.subtract, ALU.mult)
                last.then_inc(s[out], 1)

            def residual(b, banks, name):
                for j in range(2):
                    dve.wait_ge(s[name], 2 * b + j + 1)
                    last = nc.vector.tensor_tensor(res[:, 2 * j:2 * j + 2, :],
                                                   ps[:, banks + j, :].rearrange("p (n d) -> p n d", n=2),
                                                   X[:, bass.ds(NT * b + 2 * j, 2), :], ALU.add)
                last.then_inc(s["ln_step"], 1)

            def glue_and_attention1(g, n, cg, cn):
                first = isinstance(n, int) and n == 0
                if g is not None:
                    combine(2 * g + 1, 1)
                if n is not None:
                    for j in range(4):
                        dve.wait_ge(s["qk1_hi"], 4 * n + j + 1)
                        t = (q1_s, c_s)[j // 2]
                        lo_of_bias(t[:, 1, j % 2, :], ps[:, 4 + j, :], bcol[:, j // 2, j % 2:j % 2 + 1],
                                   t[:, 0, j % 2, :], "qk1_lo")
                    for j in range(2):
                        dve.wait_ge(s["v1_hi"], 2 * n + j + 1)
                        lo_of(v_s[:, 1, 2 * j:2 * j + 2, :], ps[:, j, :].rearrange("p (n d) -> p n d", n=2),
                              v_s[:, 0, 2 * j:2 * j + 2, :], "v1_lo")
                if g is not None:
                    dve.wait_ge(s["at_hi"], g + 1)
                    lo_of(a_s[:, 1, :, :], ps[:, 2:4, :], a_s[:, 0, :, :], "at_lo")

                def maximum(i):
                    dve.wait_ge(s["s1_ps"], NT * n + i + 1)
                    diag = ps[:, 4 + i, i * P:(i + 1) * P]
                    nc.vector.tensor_tensor(diag, diag, causal[:, :], ALU.add).then_inc(s["s1_step"], 1)
                    dve.wait_ge(s["s1_step"], 2 * (NT * n + i) + 1)
                    nc.vector.tensor_reduce(nmax[:, 0, i:i + 1], ps[:, 4 + i, 0:(i + 1) * P], AX, ALU.max, negate=True)\
                        .then_inc(s["s1_step"], 1)
                    dve.wait_ge(s["s1_step"], 2 * (NT * n + i) + 2)
                    nc.vector.tensor_scalar(nmax[:, 1, i:i + 1], nmax[:, 0, i:i + 1], SCALE1, None, ALU.mult)\
                        .then_inc(s["s1_max"], 1)

                def normalise(i):
                    dve.wait_ge(s["s1_exp"], NT * n + i + 1)
                    nc.vector.reciprocal(den[:, 1, i:i + 1], den[:, 0, i:i + 1]).then_inc(s["p1_step"], 1)
                    dve.wait_ge(s["p1_step"], NT * n + i + 1)
                    w = (i + 1) * P
                    nc.vector.tensor_scalar(probs[:, i, 0:w], probs[:, i, 0:w], den[:, 1, i:i + 1], None, ALU.mult)\
                        .then_inc(s["p1_norm"], 1)

                def turned(i):
                    dve.wait_ge(s["pt_hi"], NT * n + i + 1)
                    lo_of(pT_s[:, 1, 0:i + 1, i * P:(i + 1) * P],
                          ps[:, PT_BANK[i], 0:(i + 1) * P].rearrange("p (j q) -> p j q", q=P),
                          pT_s[:, 0, 0:i + 1, i * P:(i + 1) * P], "pt_lo")

                if n is not None:
                    if first:
                        dve.wait_ge(s["consts"], 5)
                    maximum(0)
                    maximum(1)
                    normalise(0)
                    maximum(2)
                    normalise(1)
                    turned(0)
                    maximum(3)
                    normalise(2)
                    turned(1)
                    normalise(3)
                    turned(2)
                    turned(3)
                if g is not None:
                    dve.wait_ge(s["x_kept"], cg)
                    residual(g, 2, "w2_ps")
                    norm_stats(cg)
                    norm_apply(cg)
                if n is not None:
                    for j in range(2):
                        dve.wait_ge(s["o1_hi"], 2 * n + j + 1)
                        lo_of_bias(c_s[:, 1, j, :], ps[:, 6 + j, :], bcol[:, 2, j:j + 1], c_s[:, 0, j, :], "o1_lo")
                    if first:
                        dve.wait_ge(s["xbo"], B)
                    else:
                        dve.wait_ge(s["x_kept"], cn)
                    if g is not None:
                        dve.wait_ge(s["g_ps"], g + 1)
                    residual(n, 0, "w1_ps")
                if g is not None:
                    dve.wait_ge(s["lg_ps"], g + 1)
                    nc.vector.tensor_scalar(lgT, ps[0:E, 4, :], gate_b[:, 0:1], None, ALU.add).then_inc(s["lg_out"], 1)

            def gates(b):
                dve.wait_ge(s["lgT_ps"], b + 1)
                nc.vector.tensor_copy(logits[:, bass.ts(b, NT), :],
                                      ps[:, 4, 0:NT * E].rearrange("p (n e) -> p n e", e=E)).then_inc(s["lgT_out"], 1)

            def project2(b):
                dve.wait_ge(s["x1_hi"], b + 1)
                lo_of(a_s[:, 1, :, :], ps[:, 0:2, :], a_s[:, 0, :, :], "x1_lo")
                for j, (t, blk) in enumerate(((k_s, 0), (q_s, 0), (k_s, 1), (q_s, 1))):
                    dve.wait_ge(s["qk2_hi"], 4 * b + j + 1)
                    lo_of_bias(t[:, blk, 1, :], ps[:, 4 + j, :], bcol[:, 4 - j % 2, blk:blk + 1], t[:, blk, 0, :], "qk2_lo")
                    if j == 0:
                        dve.wait_ge(s["ctx_lo"], b + 1)
                        for i in range(2):
                            dve.wait_ge(s["v2_ps"], 2 * b + i + 1)
                            nc.vector.tensor_copy(v_wait[:, 2 * i:2 * i + 2, :],
                                                  ps[:, 2 + i, :].rearrange("p (n d) -> p n d", n=2)).then_inc(s["v2_out"], 1)

            def out_cross(c, g):
                dve.wait_ge(s["pv_done"], 8 * c + 4 * g + 4)
                nc.vector.tensor_copy(oT[:, g, 1, :], ps[:, 7, :]).then_inc(s["os_out"], 1)

            def half(a, c, h, norm=None):
                if a is not None:
                    for u in range(UNITS):
                        p, n = u // NT, u % NT
                        k0, nb = max(n - 1, 0), 3 if 0 < n < NT - 1 else 2
                        r0 = k0 - n + 1
                        dve.wait_ge(s["a_ps"], UNITS * a + u + 1)
                        nc.vector.tensor_reduce(mx[:, n, 2 * p:2 * p + 2, r0:r0 + nb],
                                                ps[:, 2 * (u % 2):2 * (u % 2) + 2, 0:nb * P].rearrange("p h (b k) -> p h b k", k=P),
                                                AX, ALU.max, negate=True).then_inc(s["a_red"], 1)
                        if u == 1 and norm is not None:
                            norm_stats(norm)
                        if u == 3 and norm is not None:
                            norm_apply(norm)
                        if u == 9 and c is not None:
                            out_cross(c, 0)
                    at = 3 * a
                    dve.wait_ge(s["a_red"], UNITS * a + UNITS)
                    nc.vector.tensor_reduce(ncross[:, :, :], mx[:, :, :, :], AX, ALU.min).then_inc(s["aug_step"], 1)
                    dve.wait_ge(s["aug_step"], at + 1)
                    nc.vector.tensor_tensor(dloc[:, h, :, :], mx[:, :, :, 1], ncross[:, :, :], ALU.subtract)
                    nc.vector.tensor_copy(aug[:, :, 0, :], ncross[:, :, :]).then_inc(s["aug_step"], 1)
                    dve.wait_ge(s["aug_step"], at + 2)
                    nc.vector.tensor_tensor(aug[:, :, 1, :], ncross[:, :, :], aug[:, :, 0, :].bitcast(F), ALU.subtract)
                    nc.vector.tensor_copy(aug[:, :, 2, :], dloc[:, h, :, :]).then_inc(s["aug_step"], 1)
                    dve.wait_ge(s["aug_step"], at + 3)
                    nc.vector.tensor_tensor(aug[:, :, 3, :], dloc[:, h, :, :], aug[:, :, 2, :].bitcast(F), ALU.subtract)\
                        .then_inc(s["aug_ready"], 1)
                elif c is not None:
                    out_cross(c, 0)
                if c is not None:
                    out_cross(c, 1)

            def combine(c, h):
                def part(k, lo, hi):
                    x = ps[:, 0:NT, :].rearrange("p n (c g j d) -> p n c (g j) d", c=2, g=2, j=4)
                    return x[:, :, k, :, lo:hi]

                l_loc = part(0, DH, DH + 1).rearrange("p n j o -> p n (j o)")
                l_side = part(1, DH, DH + 1).rearrange("p n j o -> p n (j o)")
                at = 6 * c
                k = [0]

                def link(ins):
                    k[0] += 1
                    ins.then_inc(s["cb_step"], 1)
                    dve.wait_ge(s["cb_step"], at + k[0])

                dve.wait_ge(s["w_exp"], c + 1)
                dve.wait_ge(s["cb_ps"], c + 1)
                nc.vector.reciprocal(cw[:, 3, :, :], l_loc)
                link(nc.vector.tensor_tensor(cw[:, 0, :, :], wloc[:, :, :], l_loc, ALU.mult))
                link(nc.vector.tensor_tensor(cw[:, 1, :, :], cw[:, 0, :, :], l_side, ALU.add))
                link(nc.vector.reciprocal(cw[:, 2, :, :], cw[:, 1, :, :]))
                link(nc.vector.tensor_tensor(cw[:, 0, :, :], wloc[:, :, :], cw[:, 2, :, :], ALU.mult))
                nc.vector.tensor_tensor(cmb[:, :, :, :], part(1, 0, DH),
                                        cw[:, 2, :, :].unsqueeze(3).broadcast_to([P, NT, HALF, DH]), ALU.mult)
                link(nc.vector.tensor_tensor(cw[:, 1, :, :], cw[:, 0, :, :], cw[:, 3, :, :], ALU.add))
                av = attn[:, :, h * P:(h + 1) * P].rearrange("p n (j d) -> p n j d", d=DH)
                link(nc.vector.tensor_tensor(av, part(0, 0, DH),
                                             cw[:, 1, :, :].unsqueeze(3).broadcast_to([P, NT, HALF, DH]), ALU.mult))
                nc.vector.tensor_tensor(av, av, cmb[:, :, :, :], ALU.add).then_inc(s["cb_out"], 1)

            def body(b, first, last):
                half(2 * b, None if first else 2 * b - 1, 0)
                glue_and_attention1(None if first else b - 1, None if last else b + 1, 2 * b, 2 * b + 1)
                half(2 * b + 1, 2 * b, 1, None if last else 2 * b + 1)
                if not last:
                    project2(b + 1)
                if first:
                    dve.wait_ge(s["pad_out"], 32)
                else:
                    gates(b - 1)
                combine(2 * b, 0)

            dve.wait_ge(s["masks"], 4)
            glue_and_attention1(None, 0, None, 0)
            norm_stats(0)
            norm_apply(0)
            project2(0)
            body(0, True, False)
            with dve.Fori(1, B - 1) as b:
                body(b, False, False)
            body(B - 1, False, True)
            half(None, 2 * B - 1, 1)
            glue_and_attention1(B - 1, None, 2 * B - 1, None)
            gates(B - 1)

            k = [0]

            def link(ins):
                k[0] += 1
                ins.then_inc(s["r_step"], 1)
                dve.wait_ge(s["r_step"], k[0])

            def bc(x):
                return x[:, :].unsqueeze(2).broadcast_to([P, B * NT, E])

            def tt(out, a, b_, op):
                return nc.vector.tensor_tensor(out, a, b_, op)

            desc = desc8[:, :].unsqueeze(1).broadcast_to([P, B * NT, E])
            dve.wait_ge(s["consts2"], 12)
            dve.wait_ge(s["lgT_out"], B)
            for src, m, i, oh in ((logits, "m1", "i1", "oh1"), (R["lg2"], "m2", "i2", "oh2")):
                link(nc.vector.tensor_reduce(r1[m][:, :], src[:, :, :], AX, ALU.max))
                link(tt(R["t0"][:, :, :], src[:, :, :], bc(r1[m]), ALU.is_equal))
                link(tt(R["t0"][:, :, :], R["t0"][:, :, :], desc, ALU.mult))
                link(nc.vector.tensor_reduce(r1[i][:, :], R["t0"][:, :, :], AX, ALU.max))
                link(tt(R[oh][:, :, :], desc, bc(r1[i]), ALU.is_equal))
                if m == "m1":
                    link(nc.vector.scalar_tensor_tensor(out=R["lg2"][:, :, :], in0=R["oh1"][:, :, :], scalar=NEG,
                                                        in1=logits[:, :, :], op0=ALU.mult, op1=ALU.add))
            tt(r1["e2"][:, :], r1["m2"][:, :], r1["m1"][:, :], ALU.subtract).then_inc(s["r_exp_in"], 1)
            tt(R["mask"][:, :, :], R["oh1"][:, :, :], R["oh2"][:, :, :], ALU.add).then_inc(s["r_exp_in"], 1)
            dve.wait_ge(s["r_ps"], 2)
            link(nc.vector.tensor_copy(R["c0"][:, :, :], ps[:, 1, 128:256].rearrange("p (t e) -> p t e", e=E)))
            a, b_ = R["c0"], R["c1"]
            for sh in (1, 2, 4, 8):
                nc.vector.tensor_copy(b_[:, 0:sh, :], a[:, 0:sh, :])
                link(tt(b_[:, sh:, :], a[:, sh:, :], a[:, 0:B * NT - sh, :], ALU.add))
                a, b_ = b_, a
            link(tt(cmp[:, :, :], a[:, B * NT - 1, :].unsqueeze(2).broadcast_to([P, E, 16]),
                    step128[:, :].unsqueeze(1).broadcast_to([P, E, 16]), ALU.is_gt))
            link(nc.vector.tensor_reduce(nt_e[:, :], cmp[:, :, :], AX, ALU.add))
            link(nc.vector.tensor_tensor_scan(end_e[:, :], one_e[:, :], nt_e[:, :], 0.0, ALU.mult, ALU.add))
            link(tt(beg_e[:, :], end_e[:, :], nt_e[:, :], ALU.subtract))
            link(nc.vector.tensor_scalar(beg_e[:, :], beg_e[:, :], float(P), None, ALU.mult))
            link(tt(R["pos"][:, :, :], a[:, :, :], ps[:, 1, 128:256].rearrange("p (t e) -> p t e", e=E), ALU.subtract))
            link(tt(R["pos"][:, :, :], R["pos"][:, :, :], ps[:, 1, 0:128].rearrange("p (t e) -> p t e", e=E), ALU.add))
            link(tt(R["pos"][:, :, :], R["pos"][:, :, :], beg_e[:, :].unsqueeze(1).broadcast_to([P, B * NT, E]), ALU.add))
            for oh, sl in (("oh1", "s1"), ("oh2", "s2")):
                link(tt(R["t0"][:, :, :], R[oh][:, :, :], R["pos"][:, :, :], ALU.mult))
                link(nc.vector.tensor_reduce(r1[sl][:, :], R["t0"][:, :, :], AX, ALU.add))
            link(tt(cmpt[:, :, :], tile_no[:, :].unsqueeze(2).broadcast_to([P, TILES, E]),
                    end_e[:, :].unsqueeze(1).broadcast_to([P, TILES, E]), ALU.is_ge))
            link(nc.vector.tensor_reduce(tab_f[:, :], cmpt[:, :, :], AX, ALU.add))
            link(nc.vector.tensor_scalar(table[:, :], tab_f[:, :], float(E - 1), None, ALU.min))
            dve.wait_ge(s["r_exp"], 1)
            link(nc.vector.tensor_scalar(r1["m1"][:, :], r1["e2"][:, :], 1.0, None, ALU.add))
            link(nc.vector.reciprocal(r1["g1"][:, :], r1["m1"][:, :]))
            link(tt(r1["g2"][:, :], r1["e2"][:, :], r1["g1"][:, :], ALU.mult))
            nc.vector.tensor_copy(r1["m2"][:, :], r1["g1"][:, :]).then_inc(s["slots_ready"], 1)
            nc.vector.tensor_copy(r1["i2"][:, :], r1["g1"][:, :]).then_inc(s["table_ready"], 1)

            def expert_tiles(base, n, table_expert):
                def h_out(t):
                    dve.wait_ge(s["h_ps"], base + t + 1)
                    if base or not (isinstance(t, int) and t == 0):
                        dve.wait_ge(s["hT_ps"], base + t)
                    for c in range(2):
                        last = nc.vector.tensor_copy(hp[:, c * 512:(c + 1) * 512], ps[:, 2 + c, :])
                    last.then_inc(s["h_out"], 1)

                def y_sum(t, q, free):
                    e = table_expert(t)
                    dve.wait_ge(s["y_ps"], base + t + 1)
                    if free and base:
                        dve.wait_ge(s["y_out"], t - 1)
                    elif free:
                        dve.wait_ge(shared_sent[q], 8 * (t - q))
                    nc.vector.tensor_tensor(ysum[:, q, :], ps[:, 6, 0:D],
                                            b2b[:, bass.ds(e, 1), :].rearrange("p o d -> p (o d)"), ALU.add)\
                        .then_inc(s["y_sum"], 1)

                h_out(0)
                for t in range(2):
                    h_out(t + 1)
                    y_sum(t, t, False)
                with dve.Fori(1, n // 2 - 1) as i:
                    for q in range(2):
                        h_out(2 * i + q + 1)
                        y_sum(2 * i + q, q, True)
                h_out(n - 1)
                y_sum(n - 2, 0, True)
                y_sum(n - 1, 1, True)

            dve.wait_ge(s["eb_in"], 64)
            expert_tiles(0, T // P, lambda t: 0)
            for q in range(2):
                dve.wait_ge(shared_sent[q], 16 * T // P // 2)
            expert_tiles(T // P, TILES,
                         lambda t: dve.value_load(table[0:1, bass.ds(t, 1)], min_val=0, max_val=E - 1) + 1)

            for b in range(B):
                q = b
                dve.wait_ge(yl_in[b], 32)
                at = 6 * b
                nc.vector.tensor_tensor(fo[:, q, :, :], yl[:, q, :, 0, :], yl[:, q, :, 1, :], ALU.add).then_inc(s["f_step"], 1)
                nc.vector.tensor_tensor(yl[:, q, :, 2, :], yl[:, q, :, 2, :], X[:, NT * b:NT * b + NT, :], ALU.add)\
                    .then_inc(s["f_step"], 1)
                dve.wait_ge(s["f_step"], at + 2)
                nc.vector.tensor_tensor(fo[:, q, :, :], fo[:, q, :, :], yl[:, q, :, 2, :], ALU.add).then_inc(s["f_step"], 1)
                norm_stats(b, "f_step", fo[:, q, :, :], 2, 6)
                norm_apply(b, "f_pow", "f_out", fo[:, q, :, :])

        @block.tensor
        def _(pe):
            def turn(bank, src, name):
                for n in range(NT):
                    for k in range(KD):
                        m = nc.tensor.transpose(ps[:, bank + k, n * P:(n + 1) * P], src[:, n, k * P:(k + 1) * P], ident[:, :])
                m.then_inc(s[name], 1)

            def rows_of(bank, src, w, i, name):
                for n in range(NT):
                    for k in range(KD):
                        m = mm3(pe, ps[:, bank + n // 2, (n % 2) * D:(n % 2 + 1) * D],
                                lambda l: src[:, l, k, n * P:(n + 1) * P], lambda l: w[:, i, l, k, :],
                                k == 0, k == KD - 1)
                    if n % 2:
                        m.then_inc(s[name], 1)

            def glue_and_attention1(g, n, cg, cn):
                w = W_s[0]
                if g is not None:
                    turn_out(2 * g + 1)
                if n is not None:
                    pe.wait_ge(s["xa_lo"], n + 1)
                    if isinstance(n, int) and n == 0:
                        pe.wait_ge(s["w1_lo"], 1)
                    for j in range(4):
                        for k in range(KD):
                            m = mm3(pe, ps[:, 4 + j, :], lambda l: w[:, j // 2, l, k, (j % 2) * P:(j % 2 + 1) * P],
                                    lambda l: a_s[:, l, k, :], k == 0, k == KD - 1)
                        m.then_inc(s["qk1_ps"], 1)
                if g is not None:
                    pe.wait_ge(s["cb_out"], 2 * g + 2)
                if n is not None:
                    rows_of(0, a_s, w, 2, "v1_ps")
                if g is not None:
                    turn(2, attn, "at_ps")
                if n is not None:
                    pe.wait_ge(s["qk1_lo"], 4 * n + 4)
                    for i in range(NT):
                        wd = max(i + 1, 2) * P
                        for k in range(KD):
                            m = mm3(pe, ps[:, 4 + i, 0:wd], lambda l: q1_s[:, l, k, i * P:(i + 1) * P],
                                    lambda l: c_s[:, l, k, 0:wd], k == 0, k == KD - 1)
                        m.then_inc(s["s1_ps"], 1)
                if g is not None:
                    pe.wait_ge(s["at_lo"], g + 1)
                    rows_of(2, a_s, W_s[1], 3, "w2_ps")
                if n is not None:
                    if isinstance(n, int) and n == 0:
                        pe.wait_ge(s["consts"], 5)
                    pe.wait_ge(s["v1_lo"], 2 * n + 2)
                    for i in range(NT):
                        pe.wait_ge(s["p1_norm"], NT * n + i + 1)
                        for j in range(i + 1):
                            m = nc.tensor.transpose(ps[:, PT_BANK[i], j * P:(j + 1) * P], probs[:, i, j * P:(j + 1) * P],
                                                    ident[:, :])
                        m.then_inc(s["pt_ps"], 1)
                    pe.wait_ge(s["pt_lo"], NT * n + NT)
                    for d in range(KD):
                        for j in range(NT):
                            q0 = min(j, NT - 2) * P
                            m = mm3(pe, ps[:, 6 + d, q0:S], lambda l: v_s[:, l, j, d * P:(d + 1) * P],
                                    lambda l: pT_s[:, l, j, q0:S], j == 0, j == NT - 1, True)
                        m.then_inc(s["o1_ps"], 1)
                if g is not None:
                    pe.wait_ge(s["ln_out"], cg + 1)
                    turn(2, res, "g_ps")
                if n is not None:
                    pe.wait_ge(s["o1_lo"], 2 * n + 2)
                    rows_of(0, c_s, w, 3, "w1_ps")
                if g is not None:
                    pe.wait_ge(s["g_out"], g + 1)
                    for k in range(KD):
                        m = nc.tensor.matmul(ps[0:E, 4, :], gate_w[:, k, :], x2T[:, k, :], start=k == 0, stop=k == KD - 1)
                    m.then_inc(s["lg_ps"], 1)
                if n is not None:
                    pe.wait_ge(s["ln_step"], 4 * cn + 1)
                if g is not None:
                    pe.wait_ge(s["lg_out"], g + 1)

            def gates(b):
                for i in range(NT):
                    m = nc.tensor.transpose(ps[:, 4, i * E:(i + 1) * E], lgT[:, i * P:(i + 1) * P], ident[0:E, 0:E])
                m.then_inc(s["lgT_ps"], 1)

            def project2(b, cn, c, g):
                w = W_s[1]
                pe.wait_ge(s["ln_out"], cn + 1)
                turn(0, res, "x1_ps")
                if c is None:
                    pe.wait_ge(s["wsplit"], 4)
                for j, blk in enumerate((0, 0, 1, 1)):
                    if j == 0:
                        pe.wait_ge(s["ctx_lo"], b + 1)
                    if j == 1:
                        pe.wait_ge(s["x1_lo"], b + 1)
                    if j == 2 and c is not None:
                        pe.wait_ge(s["oc_out"], 2 * c + 2)
                        pe.wait_ge(s["os_out"], 2 * c + 2)
                    src = (c_s, a_s)[j % 2]
                    for k in range(KD):
                        m = mm3(pe, ps[:, 4 + j, :], lambda l: w[:, 1 - j % 2, l, k, blk * P:(blk + 1) * P],
                                lambda l: src[:, l, k, :], k == 0, k == KD - 1)
                    m.then_inc(s["qk2_ps"], 1)
                    if j == 0:
                        if c is not None:
                            pe.wait_ge(s["augT_out"], c + 2)
                        rows_of(2, c_s, w, 2, "v2_ps")
                pe.wait_ge(s["v2_out"], 2 * b + 2)
                if c is not None:
                    pe.wait_ge(s["qk2_lo"], 4 * b + 1)
                    turn_out(c)
                if g is not None:
                    gates(g)
                    pe.wait_ge(s["lgT_out"], g + 1)
                pe.wait_ge(s["qk2_lo"], 4 * b + 4)

            def half(a, c, ha, hc, full):
                def pv_local(m):
                    g, i = m // NT, m % NT
                    pe.wait_ge(s["b_exp"], UNITS * c + 2 * m + 2)
                    if i == 0 and (full or g):
                        pe.wait_ge(s["oc_out"], 2 * c + g)
                    for j in range(4):
                        nc.tensor.matmul(ps[32 * j:32 * j + 32, 6, i * P:(i + 1) * P],
                                         v_aug[:, i, hc * HALF + 4 * g + j, :],
                                         pT[:, m % 2, j // 2, (j % 2) * P:(j % 2 + 1) * P],
                                         start=True, stop=True, skip_group_check=True)

                def pv_sides(m):
                    g, i = m // NT, m % NT
                    sides = side_blocks(i)
                    if i == 0 and (full or g):
                        pe.wait_ge(s["os_out"], 2 * c + g)
                    w = len(sides) * P
                    for j in range(4):
                        out = ps[32 * j:32 * j + 32, 7, :].rearrange("p (n q) -> p n q", q=P)[:, sides[0]:sides[-1] + 1:2, :]
                        last = nc.tensor.matmul(
                            out, v_aug[:, i, hc * HALF + 4 * g + j, :],
                            pT[:, m % 2, j // 2, 2 * P + (j % 2) * w:2 * P + (j % 2 + 1) * w].rearrange("p (n q) -> p n q", q=P),
                            start=i == 0, stop=True, skip_group_check=True)
                    last.then_inc(s["pv_done"], 1)

                if c is not None:
                    pe.wait_ge(s["aug_in"], 64 * (c + 1))
                for u in range(UNITS):
                    if a is not None:
                        p, n = u // NT, u % NT
                        k0, nb = max(n - 1, 0), 3 if 0 < n < NT - 1 else 2
                        if n == 0:
                            pe.wait_ge(stacked[p], 16 * PAIR_DMAS * (a + 1))
                        if u >= 2:
                            pe.wait_ge(s["a_red"], UNITS * a + u - 1)
                        for j in range(2):
                            m = nc.tensor.matmul(ps[:, 2 * (u % 2) + j, 0:nb * P],
                                                 q_stack[0:96, ha * HALF + 2 * p + j, n * P:(n + 1) * P],
                                                 k_stack[0:96, ha * (HALF // 2) + p, k0 * P:(k0 + nb) * P],
                                                 start=True, stop=True)
                        m.then_inc(s["a_ps"], 1)
                    if c is not None:
                        g, i, p = u // 8, (u // 2) % NT, hc * (HALF // 2) + 2 * (u // 8) + u % 2
                        if full or u:
                            pe.wait_ge(s["b_exp"], UNITS * c + u)
                        sides = side_blocks(i)
                        qv = q_stack[:, 2 * p:2 * p + 2, :]
                        nc.tensor.matmul(ps[:, 4, 256:512].rearrange("p (h q) -> p h q", h=2),
                                         k_stack[0:100, p, i * P:(i + 1) * P], qv[0:100, :, i * P:(i + 1) * P],
                                         start=True, stop=True)
                        w = 2 * len(sides) * P
                        nc.tensor.matmul(ps[:, 5, 0:w].rearrange("p (h n q) -> p h n q", h=2, q=P),
                                         k_stack[0:98, p, i * P:(i + 1) * P],
                                         qv[0:98, :, :].rearrange("p h (n q) -> p h n q", q=P)[:, :, sides[0]:sides[-1] + 1:2, :],
                                         start=True, stop=True).then_inc(s["b_ps"], 1)
                        if u >= 2:
                            (pv_local, pv_sides)[u % 2](u // 2 - 1)
                if c is not None:
                    pv_local(UNITS // 2 - 1)
                    pv_sides(UNITS // 2 - 1)
                if a is not None:
                    pe.wait_ge(s["aug_ready"], a + 1)
                    for n in range(NT):
                        m = nc.tensor.transpose(ps[0:4 * HALF, 2, n * P:(n + 1) * P],
                                                aug[:, n, :, :].rearrange("p r h -> p (r h)").bitcast(F), ident[:, :])
                    m.then_inc(s["augT_ps"], 1)

            def turn_out(c):
                pe.wait_ge(s["oc_out"], 2 * c + 2)
                pe.wait_ge(s["os_out"], 2 * c + 2)
                for n in range(NT):
                    for k in range(2):
                        for g in range(2):
                            m = nc.tensor.transpose(ps[:, n, (2 * k + g) * P:(2 * k + g + 1) * P],
                                                    oT[:, g, k, n * P:(n + 1) * P], ident[:, :])
                m.then_inc(s["cb_ps"], 1)

            def body(b, first, last):
                half(2 * b, None if first else 2 * b - 1, 0, 1, not first)
                pe.wait_ge(s["augT_out"], 2 * b + 1)
                glue_and_attention1(None if first else b - 1, None if last else b + 1, 2 * b, 2 * b + 1)
                pe.wait_ge(s["v_set"], b + 1)
                half(2 * b + 1, 2 * b, 1, 0, not first)
                if not last:
                    project2(b + 1, 2 * b + 1, 2 * b, None if first else b - 1)
                else:
                    gates(b - 1)
                    pe.wait_ge(s["augT_out"], 2 * b + 2)
                    turn_out(2 * b)
                    pe.wait_ge(s["lgT_out"], b)
                pe.wait_ge(s["cb_out"], 2 * b + 1)

            glue_and_attention1(None, 0, None, 0)
            project2(0, 0, None, None)
            body(0, True, False)
            with pe.Fori(1, B - 1) as b:
                body(b, False, False)
            body(B - 1, False, True)
            half(None, 2 * B - 1, 0, 1, True)
            glue_and_attention1(B - 1, None, 2 * B - 1, None)
            gates(B - 1)

            pe.wait_ge(s["consts2"], 12)
            pe.wait_ge(s["r_exp_in"], 2)
            mask = R["mask"][:, :, :].rearrange("p t e -> p (t e)")
            nc.tensor.matmul(ps[:, 1, 0:128], upper[:, :], mask, start=True, stop=True).then_inc(s["r_ps"], 1)
            nc.tensor.matmul(ps[:, 1, 128:256], ones[:, :], mask, start=True, stop=True).then_inc(s["r_ps"], 1)

            def expert_tiles(base, n, table_expert, w):
                def turn_x(t, q):
                    pe.wait_ge(xs_in[q], 8 * (base + t - q) + 16)
                    if base or not (isinstance(t, int) and t < 2):
                        pe.wait_ge(s["xT_out"], base + t - 1)
                    for k in range(KD):
                        m = nc.tensor.transpose(ps[:, 7 * q, k * P:(k + 1) * P],
                                                xs[:, q, k * P:(k + 1) * P], ident[:, :])
                    m.then_inc(s["xT_ps"], 1)

                def hidden(t, q):
                    e = table_expert(t)
                    pe.wait_ge(s["xT_out"], base + t + 1)
                    if base or not (isinstance(t, int) and t == 0):
                        pe.wait_ge(s["h_out"], base + t)
                    for c in range(2):
                        for k in range(KD):
                            m = nc.tensor.matmul(
                                ps[:, 2 + c, :], xT[:, q, k, :],
                                w[:, bass.ds(e, 1), k * HID + c * 512:k * HID + (c + 1) * 512].rearrange("p o n -> p (o n)"),
                                start=k == 0, stop=k == KD - 1)
                    m.then_inc(s["h_ps"], 1)

                def turn_h(t):
                    pe.wait_ge(s["h_out"], base + t + 1)
                    if base or not (isinstance(t, int) and t == 0):
                        pe.wait_ge(s["hT_out"], base + t)
                    for c in range(NH):
                        m = nc.tensor.transpose(ps[:, 4 + c // 4, (c % 4) * P:(c % 4 + 1) * P],
                                                hp[:, c * P:(c + 1) * P], ident[:, :])
                    m.then_inc(s["hT_ps"], 1)

                def output(t):
                    e = table_expert(t)
                    pe.wait_ge(s["hT_out"], base + t + 1)
                    if base or not (isinstance(t, int) and t == 0):
                        pe.wait_ge(s["y_sum"], base + t)
                    for c in range(NH):
                        m = nc.tensor.matmul(
                            ps[:, 6, 0:D], hT[:, c, :],
                            w[:, bass.ds(e, 1), KD * HID + c * D:KD * HID + (c + 1) * D].rearrange("p o n -> p (o n)"),
                            start=c == 0, stop=c == NH - 1)
                    m.then_inc(s["y_ps"], 1)

                turn_x(0, 0)
                turn_x(1, 1)
                hidden(0, 0)
                turn_h(0)
                hidden(1, 1)
                output(0)
                turn_x(2, 0)
                turn_h(1)
                hidden(2, 0)
                output(1)
                turn_x(3, 1)
                turn_h(2)
                with pe.Fori(1, n // 2 - 1) as i:
                    t = 2 * i
                    hidden(t + 1, 1)
                    output(t)
                    turn_x(t + 2, 0)
                    turn_h(t + 1)
                    hidden(t + 2, 0)
                    output(t + 1)
                    turn_x(t + 3, 1)
                    turn_h(t + 2)
                hidden(n - 1, 1)
                output(n - 2)
                turn_h(n - 1)
                output(n - 1)

            pe.wait_ge(s["x_kept"], 2 * B)
            pe.wait_ge(s["ws_in"], 32)
            expert_tiles(0, T // P, lambda t: 0, ws)
            pe.wait_ge(s["we_in"], 32 * E)
            pe.wait_ge(s["table_ready"], 1)
            expert_tiles(T // P, TILES,
                         lambda t: pe.value_load(table[0:1, bass.ds(t, 1)], min_val=0, max_val=E - 1), we)


_WEIGHTS = ["L0_attn_Wq", "L0_attn_Wk", "L0_attn_Wv", "L0_attn_Wo",
            "L0_xattn_Wq", "L0_xattn_Wk", "L0_xattn_Wv", "L0_xattn_Wo"]


def kernel(**inputs):
    import numpy as np
    import concourse.bacc as bacc
    from concourse.bass_utils import run_bass_kernel_spmd

    a = {n: np.asarray(v) for n, v in inputs.items()}
    lay = {"x": a["x"].reshape(T, D), "xT": a["x"].reshape(T, D).T, "cT": a["ctx_1024"].reshape(T, D).T}
    for n in _WEIGHTS:
        lay[n] = a[n].T if "xattn" in n else a[n]
    lay["brow"] = np.stack([a["L0_attn_bo"], a["L0_xattn_bv"], a["L0_xattn_bo"]])
    lay["bcol"] = np.stack([a[n] for n in ("L0_attn_bq", "L0_attn_bk", "L0_attn_bv", "L0_xattn_bq", "L0_xattn_bk")])
    lay["bcol"] = lay["bcol"].reshape(5 * KD, P).T
    lay["gate_w"], lay["gate_b"] = a["L0_ffn_gate_w"], a["L0_ffn_gate_b"]
    lay["w1"], lay["w2"], lay["b2"] = a["L0_ffn_w1"], a["L0_ffn_w2"], a["L0_ffn_b2"]
    lay["b1T"] = a["L0_ffn_b1"].reshape(E * NH, P).T
    lay["ws1"], lay["ws2"], lay["bs2"] = a["L0_ffn_ws1"], a["L0_ffn_ws2"], a["L0_ffn_bs2"]
    lay["bs1T"] = a["L0_ffn_bs1"].reshape(NH, P).T
    arrays = {f"in_{n}": np.ascontiguousarray(v) for n, v in lay.items()}

    nc = bacc.Bacc("TRN2", target_bir_lowering=False, num_devices=1)
    t = {n: nc.dram_tensor(f"in_{n}", arrays[f"in_{n}"].shape, F, kind="ExternalInput").ap() for n in lay}
    out = nc.dram_tensor("out", (T, D), F, kind="ExternalOutput").ap()
    build(nc, t["x"], t["xT"], t["cT"], [t[n] for n in _WEIGHTS], t["brow"], t["bcol"], t["gate_w"], t["gate_b"],
          t["w1"], t["b1T"], t["w2"], t["b2"], t["ws1"], t["bs1T"], t["ws2"], t["bs2"], out)
    r = run_bass_kernel_spmd(nc, [arrays], core_ids=[0])
    return r.results[0]["out"].reshape(B, S, D)
```

```python
from contextlib import ExitStack

import concourse.bass as bass
from concourse import mybir

F = mybir.dt.float32
FR = mybir.dt.float32r
I32 = mybir.dt.int32
ACT = mybir.ActivationFunctionType
ALU = mybir.AluOpType
AX = mybir.AxisListType.X

P = 128
B, S, D = 4, 512, 256
T = B * S
NT = S // P
KD = D // P
E, HID = 8, 1024
NH = HID // P
HEADS, DH = 16, 16
HALF = HEADS // 2
PT_BANK = (0, 1, 4, 5)
UNITS = 16
SCALE1 = 1.0 / 16.0
SCALE2 = 0.25
NEG = -3.0e38
EPS = 1e-5
TILES = (2 * T + (P - 1) * E) // P
LOOPS = (TILES - 4) // 2
REST = 2 + 2 * LOOPS
SLOTS = TILES * P
CT = 2 * P
CHUNKS = T // CT
EARLY = 4
WARM = 24
WARM_B = 16
WARM_E = 20
ROW = D + 2
PARTS = ((0, 0), (0, 1), (1, 0))
PAIRS = HALF // 2
PAIR_DMAS = 3 + 2 * 3


def side_blocks(i):
    return [n for n in (i - 1, i + 1) if 0 <= n < NT]


def build(nc, x_d, xT_d, cT_d, w_d, brow_d, bcol_d, gate_w_d, gate_b_d,
          w1_d, b1T_d, w2_d, b2_d, ws1_d, bs1T_d, ws2_d, bs2_d, out_d):
    ctx = ExitStack()
    with ctx:
        def sb(name, shape, dt=F, stack=ctx):
            return stack.enter_context(nc.sbuf_tensor(name, shape, dt))

        def sem(name):
            return ctx.enter_context(nc.semaphore(name))

        slot_rows = nc.dram_tensor("slot_rows", (SLOTS, ROW), F, kind="Internal").ap()
        pair_out = nc.dram_tensor("pair_out", (2 * T + SLOTS, D), F, kind="Internal").ap()

        X = sb("X", [P, B * NT, D])
        ident = sb("ident", [P, P])
        zero = sb("zero", [P, 1, 1])
        causal = sb("causal", [P, P])
        brow = sb("brow", [P, 3, D])
        bcol = sb("bcol", [P, 5, KD])
        logits = sb("logits", [P, B * NT, E])
        half_pow = sb("half_pow", [P, NT])
        stats = sb("stats", [P, NT, 6])
        mv = sb("mv", [P, NT, 2])
        rstd = sb("rstd", [P, NT])
        var_eps = sb("var_eps", [P, NT])
        gate_w = sb("gate_w", [P, KD, E])
        gate_b = sb("gate_b", [E, 1])
        pad_no = sb("pad_no", [P, TILES], I32)
        pad_end = sb("pad_end", [P, TILES, 2])

        att = ExitStack()
        W_s = [sb("w1_s", [P, 4, 2, KD, D], FR, att)]
        q_stack = sb("q_stack", [P, HEADS, S], FR, att)
        W_s.append(sb("w2_s", [P, 4, 2, KD, D], FR, att))
        k_stack = sb("k_stack", [P, HEADS // 2, S], FR, att)
        a_s = sb("a_s", [P, 2, KD, S], FR, att)
        c_s = sb("c_s", [P, 2, KD, S], FR, att)
        q_s = sb("q_s", [P, KD, 2, S], FR, att)
        k_s = sb("k_s", [P, KD, 2, S], FR, att)
        v_s = sb("v_s", [P, 2, NT, D], FR, att)
        pT_s = sb("pT_s", [P, 2, NT, S], FR, att)
        aug = sb("aug", [P, NT, 4, HALF], FR, att)
        augT = sb("augT", [4 * HALF, S], FR, att)
        x_raw = sb("x_raw", [P, KD, S], F, att)
        c_raw = sb("c_raw", [P, KD, S], F, att)
        v_wait = c_raw[:, :, :].rearrange("p k t -> p (k t)").rearrange("p (n d) -> p n d", n=NT)
        res = sb("res", [P, NT, D], F, att)
        v_aug = sb("v_aug", [P, NT, HEADS, 32], F, att)
        pT = sb("pT", [P, 2, 2, 768], F, att)
        probs = pT[:, :, :, :].rearrange("p a b c -> p (a b c)")[:, 0:NT * S].rearrange(
            "p (n k) -> p n k", n=NT)
        raw2 = v_aug[:, :, :, :].rearrange("p a b c -> p (a b c)").rearrange(
            "p (w k n) -> p w k n", w=4, k=KD)
        attn = sb("attn", [P, NT, D], F, att)
        lgT = attn[:, :, :].rearrange("p n d -> p (n d)")[0:E, 0:S]
        mx = sb("mx", [P, NT, HALF, 3], F, att)
        ncross = sb("ncross", [P, NT, HALF], F, att)
        dloc = sb("dloc", [P, 2, NT, HALF], F, att)
        wloc = sb("wloc", [P, NT, HALF], F, att)
        cw = sb("cw", [P, 4, NT, HALF], F, att)
        cmb = sb("cmb", [P, NT, HALF, DH], F, att)
        nmax = sb("nmax", [P, 2, NT], F, att)
        den = sb("den", [P, 2, NT], F, att)
        turned = ExitStack()
        oT = sb("oT", [P, 2, 2, S], F, turned)
        oT_flat = oT[:, :, :, :].rearrange("p a b c -> p (a b c)")
        x2T = oT_flat[:, 0:KD * S].rearrange("p (k t) -> p k t", k=KD)
        raw1 = oT_flat[:, 0:4 * KD * D].rearrange("p (w k n) -> p w k n", w=4, k=KD)
        turned.close()
        q1_s = sb("q1_s", [P, 2, KD, S], FR, att)
        att.close()

        EW = 2 * KD * HID
        mo = ExitStack()
        ws = sb("ws", [P, EW], F, mo)
        we = sb("we", [P, E, EW], F, mo)
        b1T = sb("b1T", [P, (E + 1) * NH], F, mo)
        b2b = sb("b2b", [P, E + 1, D], F, mo)
        xs = sb("xs", [P, 2, D], F, mo)
        meta = sb("meta", [P, TILES, 2], F, mo)
        xT = sb("xT", [P, 2, KD, P], F, mo)
        hp = sb("hp", [P, HID], F, mo)
        hT = sb("hT", [P, NH, P], F, mo)
        ysum = sb("ysum", [P, 2, D], F, mo)
        yw = sb("yw", [P, 2, D], F, mo)
        shared_y = ws[:, :].rearrange("p (t d) -> p t d", d=D)
        stage = sb("stage", [P, 2, 2, ROW], F, mo)
        yidx = sb("yidx", [P, 2, 1], I32, mo)
        sidx = sb("sidx", [P, 2, 2, 1], I32, mo)
        slot_tab = sb("slot_tab", [P, B * NT, 2], I32, mo)
        meta_tab = sb("meta_tab", [P, B * NT, 2, 2], F, mo)
        upper = sb("upper", [P, P], F, mo)
        ones = sb("ones", [P, P], F, mo)
        desc8 = sb("desc8", [P, E], F, mo)
        step128 = sb("step128", [P, 16], F, mo)
        tile_no = sb("tile_no", [P, TILES], F, mo)
        R = {n: sb("r_" + n, [P, B * NT, E], F, mo) for n in
             ("t0", "oh1", "oh2", "lg2", "mask", "c0", "c1", "pos")}
        r1 = {n: sb("r1_" + n, [P, B * NT], F, mo) for n in ("m1", "i1", "m2", "i2", "e2", "g1", "g2", "s1", "s2")}
        cmp = sb("cmp", [P, E, 16], F, mo)
        cmpt = sb("cmpt", [P, TILES, E], F, mo)
        nt_e = sb("nt_e", [P, E], F, mo)
        end_e = sb("end_e", [P, E], F, mo)
        beg_e = sb("beg_e", [P, E], F, mo)
        one_e = sb("one_e", [P, E], F, mo)
        tab_f = sb("tab_f", [P, TILES], F, mo)
        table = sb("table", [P, TILES], I32, mo)
        mo.close()
        sh = ExitStack()
        sb("early", [P, (1 + EARLY) * EW], F, sh)
        ws_s = sb("ws_s", [P, 2, EW], FR, sh)
        h_s = sb("h_s", [P, 2, NH, CT], FR, sh)
        xT_s = sb("xT_s", [P, 2, KD, CT], FR, sh)
        h_full = sb("h_full", [P, NH, CT], F, sh)
        xT_full = sb("xT_full", [P, KD, CT], F, sh)
        sh.close()
        fin = ExitStack()
        sb("kept", [P, EW], F, fin)
        yl = sb("yl", [P, B, NT, 2, D], F, fin)
        stats_f = sb("stats_f", [P, B, NT, 6], F, fin)
        mean_f = sb("mean_f", [P, B, NT, 2], F, fin)
        var_f, rstd_f, bias_f = (sb(n, [P, B, NT], F, fin) for n in ("var_f", "rstd_f", "bias_f"))
        fo = sb("fo", [P, B, NT, D], F, fin)
        fin.close()

        ps = ctx.enter_context(nc.psum_tensor("ps", [P, 8, 512], F))

        names = """x_in w1_in w2_in w1_hi w1_lo b_in x_raw_in c_raw_in wsplit wsplit_hi consts consts2 masks xbo pad_set pad_out
          xa_hi xa_lo qk1_ps qk1_hi qk1_lo v1_ps v1_hi v1_lo s1_ps s1_step s1_max s1_exp p1_step p1_norm
          pt_ps pt_hi pt_lo o1_ps o1_hi o1_lo w1_ps ln_step ln_pow ln_out x_kept zeroed pT_zero k_ones
          x1_ps x1_hi x1_lo ctx_hi ctx_lo qk2_ps qk2_hi qk2_lo aug_in v_set
          a_ps a_red aug_step aug_ready augT_ps augT_out b_ps b_exp pv_done oc_out os_out
          cb_ps w_exp cb_step cb_out v2_ps v2_out at_ps at_hi at_lo w2_ps
          g_ps g_out lg_ps lg_out lgT_ps lgT_out
          ws_in we_in eb_in r_step r_exp r_exp_in r_ps table_ready slots_ready
          ws_hi ws1_lo ws2_lo sx_out sxT_ps sxT_out sx_hi sx_lo sh_ps sh_out sh_hi sh_lo sy_ps sy_out x_sum
          xT_ps xT_out meta_in h_ps h_out hT_ps hT_out y_ps y_sum y_out y_idx
          f_x f_x0 f_step f_var f_pow f_bias f_out o_sent
          """.split()
        s = {n: sem("s_" + n) for n in names}
        xs_in, yw_sent, st_step, st_sent = ([sem(f"s_{n}{q}") for q in range(2)]
                                            for n in ("xs_in", "yw_sent", "st_step", "st_sent"))
        stacked = [sem(f"s_stacked{p}") for p in range(PAIRS)]
        yl_in = [sem(f"s_yl_in{b}") for b in range(B)]

        block = ctx.enter_context(nc.Block())

        def mm3(pe, out, lhs, rhs, first=True, last=True, check=False):
            for n, (a, b) in enumerate(PARTS):
                m = nc.tensor.matmul(out, lhs(a), rhs(b), start=first and n == 0,
                                     stop=last and n == 2, skip_group_check=check)
            return m

        @block.sync
        def _(sp):
            for i in range(4):
                sp.dma_start(raw1[:, i, :, :], w_d[i].rearrange("(k p) n -> p k n", p=P)).then_inc(s["w1_in"], 16)
            sp.dma_start(x_raw[:, :, :], xT_d[:, 0:S].rearrange("(k p) t -> p k t", p=P)).then_inc(s["x_raw_in"], 16)
            sp.dma_start(bcol[:, :, :].rearrange("p i k -> p (i k)"), bcol_d).then_inc(s["b_in"], 16)
            sp.dma_start(brow[:, :, :], brow_d.partition_broadcast(P)).then_inc(s["b_in"], 16)
            sp.dma_start(gate_w[:, :, :], gate_w_d.rearrange("(k p) e -> p k e", p=P)).then_inc(s["b_in"], 16)
            sp.dma_start(gate_b[:, :], gate_b_d.rearrange("(e o) -> e o", o=1)).then_inc(s["b_in"], 16)
            for i in range(4):
                sp.dma_start(raw2[:, i, :, :], w_d[4 + i].rearrange("(k p) n -> p k n", p=P)).then_inc(s["w2_in"], 16)
            for b in range(B):
                sp.dma_start(X[:, NT * b:NT * b + NT, :],
                             x_d[b * S:(b + 1) * S, :].rearrange("(n p) d -> p n d", p=P)).then_inc(s["x_in"], 16)
            sp.dma_start(c_raw[:, :, :], cT_d[:, 0:S].rearrange("(k p) t -> p k t", p=P)).then_inc(s["c_raw_in"], 16)

            sp.wait_ge(s["pad_set"], 4)
            sp.dma_start(slot_rows[:, 0:D].rearrange("(i p) d -> p i d", p=P),
                         attn[:, 0:1, :].broadcast_to([P, TILES, D])).then_inc(s["pad_out"], 16)
            sp.dma_start(slot_rows[:, D:].rearrange("(i p) d -> p i d", p=P), pad_end[:, :, :]).then_inc(s["pad_out"], 16)

            def stack(h):
                for g in range(PAIRS):
                    for sec, part in enumerate((0, 1, 0)):
                        sp.dma_start(k_stack[32 * sec:32 * sec + 32, h * PAIRS + g, :].bitcast(F),
                                     k_s[32 * g:32 * g + 32, h, part, :].bitcast(F)).then_inc(stacked[g], 16)
                    for head in (2 * g, 2 * g + 1):
                        for sec, part in enumerate((0, 0, 1)):
                            r = 32 * sec + 16 * (head % 2)
                            sp.dma_start(q_stack[r:r + 16, h * HALF + head, :].bitcast(F),
                                         q_s[16 * head:16 * head + 16, h, part, :].bitcast(F)).then_inc(stacked[g], 16)

            def aug_rows(b, h):
                sp.wait_ge(s["augT_out"], 2 * b + h + 1)
                for r in range(4):
                    sp.dma_start(q_stack[96 + r:97 + r, h * HALF:(h + 1) * HALF, :].bitcast(F),
                                 augT[r * HALF:(r + 1) * HALF, :].bitcast(F)).then_inc(s["aug_in"], 16)

            def body(b, first, last):
                nb = (b + 1) % B
                sp.wait_ge(s["qk2_lo"], 4 * b + 2)
                if first:
                    sp.wait_ge(s["masks"], 1)
                else:
                    sp.wait_ge(s["b_ps"], 2 * UNITS * (2 * b - 1))
                stack(0)
                if not last:
                    sp.wait_ge(s["xa_lo"], b + 1)
                    sp.dma_start(x_raw[:, :, :], xT_d[:, bass.ts(nb, S)].rearrange("(k p) t -> p k t", p=P))\
                        .then_inc(s["x_raw_in"], 16)
                aug_rows(b, 0)
                if not first:
                    sp.wait_ge(s["b_ps"], 2 * UNITS * (2 * b))
                stack(1)
                if not last:
                    sp.wait_ge(s["v_set"], b + 1)
                    sp.dma_start(c_raw[:, :, :], cT_d[:, bass.ts(nb, S)].rearrange("(k p) t -> p k t", p=P))\
                        .then_inc(s["c_raw_in"], 16)
                aug_rows(b, 1)

            body(0, True, False)
            with sp.Fori(1, B - 1) as b:
                body(b, False, False)
            sp.wait_ge(s["w1_ps"], 2 * B)
            sp.dma_start(ws[:, 0:KD * HID].rearrange("p (k n) -> p k n", k=KD),
                         ws1_d.rearrange("(k p) n -> p k n", p=P)).then_inc(s["ws_in"], 16)
            sp.dma_start(ws[:, KD * HID:].rearrange("p (k n) -> p k n", k=NH),
                         ws2_d.rearrange("(k p) n -> p k n", p=P)).then_inc(s["ws_in"], 16)
            body(B - 1, False, True)

            sp.wait_ge(s["lgT_out"], B)
            sp.wait_ge(s["x_kept"], 2 * B)
            sp.wait_ge(s["pad_out"], 32)
            sp.dma_start(b1T[:, 0:NH], bs1T_d).then_inc(s["eb_in"], 16)
            sp.dma_start(b1T[:, NH:], b1T_d).then_inc(s["eb_in"], 16)
            sp.dma_start(b2b[:, 0, :], bs2_d.partition_broadcast(P)).then_inc(s["eb_in"], 16)
            sp.dma_start(b2b[:, 1:, :], b2_d.partition_broadcast(P)).then_inc(s["eb_in"], 16)
            def load_expert(e):
                sp.dma_start(we[:, e, 0:KD * HID].rearrange("p (k n) -> p k n", k=KD),
                             w1_d[e].rearrange("(k p) n -> p k n", p=P)).then_inc(s["we_in"], 16)
                sp.dma_start(we[:, e, KD * HID:].rearrange("p (k n) -> p k n", k=NH),
                             w2_d[e].rearrange("(k p) n -> p k n", p=P)).then_inc(s["we_in"], 16)

            for e in range(EARLY):
                load_expert(e)
            for q in range(2):
                sp.wait_ge(st_sent[q], 16 * 2 * T // P // 2)
            sp.wait_ge(s["sxT_ps"], CHUNKS)
            for q in range(2):
                sp.dma_start(xs[:, q, :], slot_rows[q * P:(q + 1) * P, 0:D]).then_inc(xs_in[q], 16)
            sp.dma_start(meta[:, :, :], slot_rows[:, D:].rearrange("(i p) m -> p i m", p=P)).then_inc(s["meta_in"], 16)
            def rows_ahead(i, q):
                t = 2 * i + q
                sp.wait_ge(s["xT_ps"], t + 1)
                sp.dma_start(xs[:, q, :], slot_rows[bass.ts(t + 2, P), 0:D]).then_inc(xs_in[q], 16)

            sp.wait_ge(s["we_in"], 32 * EARLY)
            sp.wait_ge(s["sy_ps"], CHUNKS)
            for i in range(E - EARLY):
                load_expert(EARLY + i)
                rows_ahead(i, 0)
                rows_ahead(i, 1)
            with sp.Fori(E - EARLY, TILES // 2 - 1) as i:
                rows_ahead(i, 0)
                rows_ahead(i, 1)
            for t in range(TILES // 2 * 2 - 2, TILES - 2):
                rows_ahead(t // 2, 0)
            for q in range(2):
                sp.wait_ge(yw_sent[q], 16 * ((TILES + 1 - q) // 2))
            sp.wait_ge(s["y_ps"], TILES)
            for b in range(B):
                sp.dma_start(yl[:, b, :, :, :],
                             pair_out[2 * b * S:2 * (b + 1) * S, :].rearrange("(n p k) d -> p n k d", p=P, k=2))\
                    .then_inc(yl_in[b], 16)
            for b in range(B):
                sp.wait_ge(s["f_out"], b + 1)
                sp.dma_start(out_d[b * S:(b + 1) * S, :].rearrange("(n p) d -> p n d", p=P),
                             fo[:, b, :, :]).then_inc(s["o_sent"], 16)
            sp.wait_ge(s["o_sent"], 16 * B)

        @block.gpsimd
        def _(pool):
            def split(dst, src, free, hi, lo, n):
                for sem_, value in free:
                    pool.wait_ge(s[sem_], value)
                nc.gpsimd.tensor_tensor(dst[:, 0, :, :], src[:, :, :], zero[:, :, :].broadcast_to([P, KD, S]), ALU.add)\
                    .then_inc(s[hi], 1)
                pool.wait_ge(s[hi], n + 1)
                nc.gpsimd.tensor_tensor(dst[:, 1, :, :], src[:, :, :], dst[:, 0, :, :].bitcast(F), ALU.subtract)\
                    .then_inc(s[lo], 1)

            nc.gpsimd.memset(zero[:, :, :], 0.0).then_inc(s["zeroed"], 1)
            pool.wait_ge(s["zeroed"], 1)
            split(a_s, x_raw, (("x_raw_in", 16),), "xa_hi", "xa_lo", 0)
            nc.gpsimd.memset(ident[:, :], 0.0).then_inc(s["consts"], 1)
            nc.gpsimd.memset(causal[:, :], 0.0).then_inc(s["consts"], 1)
            nc.gpsimd.memset(half_pow[:, :], -0.5).then_inc(s["consts"], 1)
            pool.wait_ge(s["consts"], 3)
            nc.gpsimd.affine_select(out=ident[:, :], in_=ident[:, :], compare_op=ALU.not_equal, fill=1.0,
                                    base=0, pattern=[[-1, P]], channel_multiplier=1).then_inc(s["consts"], 1)
            nc.gpsimd.affine_select(out=causal[:, :], in_=causal[:, :], compare_op=ALU.is_ge, fill=NEG,
                                    base=0, pattern=[[-1, P]], channel_multiplier=1).then_inc(s["consts"], 1)
            nc.gpsimd.memset(attn[:, 0, :], 0.0).then_inc(s["pad_set"], 1)
            nc.gpsimd.memset(pad_end[:, :, :], 0.0).then_inc(s["pad_set"], 1)
            nc.gpsimd.iota(pad_no[:, :], pattern=[[P, TILES]], base=2 * T, channel_multiplier=1).then_inc(s["pad_set"], 1)
            pool.wait_ge(s["pad_set"], 3)
            nc.gpsimd.tensor_copy(pad_end[:, :, 0], pad_no[:, :]).then_inc(s["pad_set"], 1)
            pool.wait_ge(s["w2_in"], 16 * 4)
            for i in range(4):
                nc.gpsimd.tensor_copy(W_s[1][:, i, 0, :, :], raw2[:, i, :, :]).then_inc(s["wsplit_hi"], 1)
            for i in range(4):
                pool.wait_ge(s["wsplit_hi"], i + 1)
                nc.gpsimd.tensor_tensor(W_s[1][:, i, 1, :, :], raw2[:, i, :, :],
                                        W_s[1][:, i, 0, :, :].bitcast(F), ALU.subtract).then_inc(s["wsplit"], 1)
            pool.wait_ge(s["b_in"], 64)
            pool.wait_ge(s["x_in"], 16 * B)
            for b in range(B):
                Xb = X[:, NT * b:NT * b + NT, :]
                nc.gpsimd.tensor_tensor(Xb, Xb, brow[:, 0:1, :].broadcast_to([P, NT, D]), ALU.add)\
                    .then_inc(s["xbo"], 1)
            nc.gpsimd.memset(q_stack[:, :, :].bitcast(F), 0.0).then_inc(s["masks"], 1)
            nc.gpsimd.memset(mx[:, :, :, :], -NEG).then_inc(s["masks"], 1)
            pool.wait_ge(s["wsplit"], 4)
            nc.gpsimd.memset(v_aug[:, :, :, :], 0.0).then_inc(s["masks"], 1)
            pool.wait_ge(s["masks"], 3)
            nc.gpsimd.memset(v_aug[:, :, :, DH:DH + 1], 1.0).then_inc(s["masks"], 1)
            def norm_pow(c):
                pool.wait_ge(s["ln_step"], 4 * c + 4)
                nc.gpsimd.tensor_tensor(rstd[:, :], var_eps[:, :], half_pow[:, :], ALU.pow).then_inc(s["ln_pow"], 1)

            def keep(b, c, bias):
                pool.wait_ge(s["ln_out"], c + 1)
                Xb = X[:, bass.ts(b, NT), :]
                if bias:
                    nc.gpsimd.tensor_tensor(Xb, res[:, :, :], brow[:, 2:3, :].broadcast_to([P, NT, D]), ALU.add)\
                        .then_inc(s["x_kept"], 1)
                else:
                    nc.gpsimd.tensor_copy(Xb, res[:, :, :]).then_inc(s["x_kept"], 1)

            def body(b, first, last):
                if not last:
                    split(a_s, x_raw, (("x_raw_in", 16 * b + 32), ("qk2_ps", 4 * b + 4)), "xa_hi", "xa_lo", b + 1)
                if not first:
                    pool.wait_ge(s["pv_done"], 8 * 2 * b)
                pool.wait_ge(s["v2_out"], 2 * b + 2)
                nc.gpsimd.tensor_tensor(v_aug[:, :, :, 0:DH], v_wait.rearrange("p n (h d) -> p n h d", d=DH),
                                        brow[:, 1:2, :].rearrange("p o (h d) -> p o h d", d=DH)
                                        .broadcast_to([P, NT, HEADS, DH]), ALU.add)\
                    .then_inc(s["v_set"], 1)
                if not first:
                    norm_pow(2 * b)
                    keep(b - 1, 2 * b, False)
                if not last:
                    norm_pow(2 * b + 1)
                    keep(b + 1, 2 * b + 1, True)
                    split(c_s, c_raw, (("w1_ps", 2 * b + 4), ("c_raw_in", 16 * b + 32)), "ctx_hi", "ctx_lo", b + 1)

            norm_pow(0)
            split(c_s, c_raw, (("w1_ps", 2), ("c_raw_in", 16)), "ctx_hi", "ctx_lo", 0)
            keep(0, 0, True)
            pool.wait_ge(s["masks"], 4)
            body(0, True, False)
            with pool.Fori(1, B - 1) as b:
                body(b, False, False)
            body(B - 1, False, True)
            norm_pow(2 * B - 1)
            keep(B - 1, 2 * B - 1, False)

            pool.wait_ge(s["lgT_out"], B)
            pool.wait_ge(s["x_kept"], 2 * B)
            nc.gpsimd.memset(upper[:, :], 1.0).then_inc(s["consts2"], 1)
            nc.gpsimd.memset(ones[:, :], 1.0).then_inc(s["consts2"], 1)
            nc.gpsimd.memset(one_e[:, :], 1.0).then_inc(s["consts2"], 1)
            nc.gpsimd.iota(R["t0"][:, 0:1, :].bitcast(I32), pattern=[[0, 1], [-1, E]], base=E, channel_multiplier=0)\
                .then_inc(s["consts2"], 1)
            nc.gpsimd.iota(R["lg2"][:, 0:2, :].bitcast(I32), pattern=[[P * E, 2], [P, E]], base=0, channel_multiplier=0)\
                .then_inc(s["consts2"], 1)
            nc.gpsimd.iota(table[:, :], pattern=[[1, TILES]], base=0, channel_multiplier=0).then_inc(s["consts2"], 1)
            nc.gpsimd.iota(R["mask"][:, 0:4, :].bitcast(I32).rearrange("p (k a) e -> p k (a e)", k=2),
                           pattern=[[1, 2], [2 * P, B * NT]], base=0, channel_multiplier=2).then_inc(s["consts2"], 1)
            pool.wait_ge(s["consts2"], 7)
            nc.gpsimd.affine_select(out=upper[:, :], in_=upper[:, :], compare_op=ALU.is_ge, fill=0.0,
                                    base=-1, pattern=[[1, P]], channel_multiplier=-1).then_inc(s["consts2"], 1)
            nc.gpsimd.tensor_copy(desc8[:, :], R["t0"][:, 0, :].bitcast(I32)).then_inc(s["consts2"], 1)
            nc.gpsimd.tensor_copy(step128[:, :].rearrange("p (a b) -> p a b", a=2), R["lg2"][:, 0:2, :].bitcast(I32))\
                .then_inc(s["consts2"], 1)
            nc.gpsimd.tensor_copy(tile_no[:, :], table[:, :]).then_inc(s["consts2"], 1)
            nc.gpsimd.tensor_copy(meta_tab[:, :, :, 0].rearrange("p t k -> p k t"),
                                  R["mask"][:, 0:4, :].bitcast(I32).rearrange("p (k a) e -> p k (a e)", k=2))\
                .then_inc(s["consts2"], 1)

            pool.wait_ge(s["ws_hi"], 2)
            nc.gpsimd.tensor_tensor(ws_s[:, 1, KD * HID:], ws[:, KD * HID:], ws_s[:, 0, KD * HID:].bitcast(F),
                                    ALU.subtract).then_inc(s["ws2_lo"], 1)
            pool.wait_ge(s["consts2"], 12)
            pool.wait_ge(s["pad_out"], 32)
            pool.wait_ge(s["slots_ready"], 1)
            def scatter(v, q, first):
                t = 2 * v + (q - 2)
                if not first:
                    pool.wait_ge(st_sent[q], 32 * (v - 1))
                nc.gpsimd.tensor_copy(stage[:, q, :, 0:D], X[:, bass.ds(t, 1), :].broadcast_to([P, 2, D]))
                nc.gpsimd.tensor_copy(stage[:, q, :, D:], meta_tab[:, bass.ds(t, 1), :, :].rearrange("p o k m -> p (o k) m"))
                nc.gpsimd.tensor_copy(sidx[:, q, :, 0], slot_tab[:, bass.ds(t, 1), :].rearrange("p o k -> p (o k)"))\
                    .then_inc(st_step[q], 1)
                pool.wait_ge(s["slots_ready"], 1)
                pool.wait_ge(st_step[q], v)
                for k in range(2):
                    pool.indirect_dma_start(
                        out=slot_rows, out_offset=bass.IndirectOffsetOnAxis(ap=sidx[:, q, k, :], axis=0),
                        in_=stage[:, q, k, :], in_offset=None).then_inc(st_sent[q], 16)

            scatter(1, 0, True)
            scatter(1, 1, True)
            with pool.Fori(2, T // P // 2 + 1) as v:
                scatter(v, 0, False)
                scatter(v, 1, False)

            pool.wait_ge(s["sy_out"], CHUNKS)
            for q in range(2):
                pool.wait_ge(st_sent[q], 16 * T // P)
            for b in range(B):
                Xb = X[:, NT * b:NT * b + NT, :]
                nc.gpsimd.tensor_tensor(Xb, Xb, shared_y[:, NT * b:NT * b + NT, :], ALU.add).then_inc(s["x_sum"], 1)

            pool.wait_ge(s["meta_in"], 16)
            def rows_out(t, q):
                pool.wait_ge(s["y_out"], t + 1)
                nc.gpsimd.tensor_copy(yidx[:, q, :], meta[:, bass.ds(t, 1), 0]).then_inc(s["y_idx"], 1)
                pool.wait_ge(s["meta_in"], 16)
                pool.wait_ge(s["y_idx"], t + 1)
                pool.indirect_dma_start(
                    out=pair_out, out_offset=bass.IndirectOffsetOnAxis(ap=yidx[:, q, :], axis=0),
                    in_=yw[:, q, :], in_offset=None).then_inc(yw_sent[q], 16)

            with pool.Fori(0, TILES // 2) as i:
                rows_out(2 * i, 0)
                rows_out(2 * i + 1, 1)
            for t in range(TILES // 2 * 2, TILES):
                rows_out(t, 0)
            for b in range(B):
                if b + 1 < B:
                    y = yl[:, b + 1, :, 0, :]
                    pool.wait_ge(yl_in[b + 1], 16)
                    nc.gpsimd.tensor_tensor(y, y, X[:, NT * (b + 1):NT * (b + 2), :], ALU.add).then_inc(s["f_x"], 1)
                pool.wait_ge(s["f_var"], b + 1)
                nc.gpsimd.tensor_tensor(rstd_f[:, b, :], var_f[:, b, :], half_pow[:, :], ALU.pow).then_inc(s["f_pow"], 1)

        @block.scalar
        def _(act):
            def copy(out, in_, name):
                nc.scalar.activation(out, in_, ACT.Copy).then_inc(s[name], 1)

            def copy_bias(out, in_, bias, name):
                nc.scalar.activation(out, in_, ACT.Identity, bias=bias).then_inc(s[name], 1)

            def glue_and_attention1(g, n):
                if g is not None:
                    act.wait_ge(s["cb_out"], 2 * g + 1)
                    local_weight(2 * g + 1, 1)
                if n is not None:
                    for j in range(4):
                        act.wait_ge(s["qk1_ps"], 4 * n + j + 1)
                        copy_bias((q1_s, c_s)[j // 2][:, 0, j % 2, :], ps[:, 4 + j, :],
                                  bcol[:, j // 2, j % 2:j % 2 + 1], "qk1_hi")
                    for j in range(2):
                        act.wait_ge(s["v1_ps"], 2 * n + j + 1)
                        copy(v_s[:, 0, 2 * j:2 * j + 2, :], ps[:, j, :].rearrange("p (n d) -> p n d", n=2), "v1_hi")
                if g is not None:
                    act.wait_ge(s["at_ps"], g + 1)
                    copy(a_s[:, 0, :, :], ps[:, 2:4, :], "at_hi")

                def expo(i):
                    act.wait_ge(s["s1_max"], NT * n + i + 1)
                    w = (i + 1) * P
                    nc.scalar.activation(probs[:, i, 0:w], ps[:, 4 + i, 0:w], ACT.Exp, bias=nmax[:, 1, i:i + 1],
                                         scale=SCALE1, accum_out=den[:, 0, i:i + 1]).then_inc(s["s1_exp"], 1)

                def turned(i):
                    act.wait_ge(s["pt_ps"], NT * n + i + 1)
                    copy(pT_s[:, 0, 0:i + 1, i * P:(i + 1) * P],
                         ps[:, PT_BANK[i], 0:(i + 1) * P].rearrange("p (j q) -> p j q", q=P), "pt_hi")

                if n is not None:
                    if isinstance(n, int) and n == 0:
                        act.wait_ge(s["pT_zero"], 1)
                    expo(0)
                    expo(1)
                    turned(0)
                    expo(2)
                    turned(1)
                    expo(3)
                    turned(2)
                    turned(3)
                    for j in range(2):
                        act.wait_ge(s["o1_ps"], 2 * n + j + 1)
                        copy_bias(c_s[:, 0, j, :], ps[:, 6 + j, :], bcol[:, 2, j:j + 1], "o1_hi")
                if g is not None:
                    act.wait_ge(s["g_ps"], g + 1)
                    copy(x2T, ps[:, 2:4, :], "g_out")

            def project2(b, first):
                act.wait_ge(s["x1_ps"], b + 1)
                copy(a_s[:, 0, :, :], ps[:, 4:6, :], "x1_hi")
                if not first:
                    for p in range(PAIRS):
                        act.wait_ge(stacked[p], 16 * PAIR_DMAS * 2 * b)
                for j, (dst, blk) in enumerate(((k_s, 0), (q_s, 0), (k_s, 1), (q_s, 1))):
                    act.wait_ge(s["qk2_ps"], 4 * b + j + 1)
                    copy_bias(dst[:, blk, 0, :], ps[:, 7 - j % 2, :], bcol[:, 4 - j % 2, blk:blk + 1], "qk2_hi")
                    if j == 1:
                        act.wait_ge(s["ctx_lo"], b + 1)
                        for i in range(2):
                            act.wait_ge(s["v2_ps"], 2 * b + i + 1)
                            copy(v_wait[:, 2 * i:2 * i + 2, :], ps[:, 4 + i, :].rearrange("p (n d) -> p n d", n=2), "v2_out")

            def half(a, c, free):
                if c is not None:
                    for u in range(UNITS):
                        m, i = u // 2, (u // 2) % NT
                        w = 2 * P * len(side_blocks(i))
                        bank = 2 if a is None and u % 2 else 4
                        at = 2 * UNITS * c + 2 * u
                        act.wait_ge(s["b_ps"], at + 1)
                        if m >= 2:
                            act.wait_ge(s["pv_done"], 8 * c + m - 1)
                        nc.scalar.activation(pT[:, m % 2, u % 2, 0:2 * P], ps[:, bank, 256:512], ACT.Exp, scale=SCALE2)\
                            .then_inc(s["b_exp"], 1)
                        act.wait_ge(s["b_ps"], at + 2)
                        nc.scalar.activation(pT[:, m % 2, u % 2, 2 * P:2 * P + w], ps[:, bank + 1, 0:w], ACT.Exp,
                                             scale=SCALE2).then_inc(s["b_exp"], 1)
                        if u == 9:
                            out_local(c, 0)
                    out_local(c, 1)
                if a is not None:
                    if free:
                        act.wait_ge(s["aug_in"], 64 * a)
                    act.wait_ge(s["augT_ps"], a + 1)
                    copy(augT[:, :], ps[0:4 * HALF, 2, :], "augT_out")

            def out_local(c, g):
                act.wait_ge(s["pv_done"], 8 * c + 4 * g + 4)
                copy(oT[:, g, 0, :], ps[:, 6, :], "oc_out")

            def local_weight(c, h):
                nc.scalar.activation(wloc[:, :, :], dloc[:, h, :, :], ACT.Exp, scale=-SCALE2).then_inc(s["w_exp"], 1)

            def body(b, first, last):
                half(2 * b, None if first else 2 * b - 1, not first)
                glue_and_attention1(None if first else b - 1, None if last else b + 1)
                half(2 * b + 1, 2 * b, True)
                if not first:
                    act.wait_ge(s["cb_out"], 2 * b)
                local_weight(2 * b, 0)
                if not last:
                    project2(b + 1, False)

            act.wait_ge(s["b_in"], 64)
            glue_and_attention1(None, 0)
            project2(0, True)
            body(0, True, False)
            with act.Fori(1, B - 1) as b:
                body(b, False, False)
            body(B - 1, False, True)
            half(None, 2 * B - 1, True)
            glue_and_attention1(B - 1, None)

            def x_rows(c):
                nc.scalar.activation(xs[:, :, :], X[:, bass.ds(2 * c, 2), :], ACT.Copy).then_inc(s["sx_out"], 1)

            def x_turned(c, first=False):
                act.wait_ge(s["sxT_ps"], c + 1)
                if not first:
                    act.wait_ge(s["sx_lo"], c)
                copy(xT_full[:, :, :], ps[:, 7, :].rearrange("p (k t) -> p k t", k=KD), "sxT_out")

            def shared_gelu(c, first=False):
                for j in range(NH // 2):
                    act.wait_ge(s["sh_ps"], 4 * c + j + 1)
                    if not first:
                        act.wait_ge(s["sh_lo"], 2 * c + (j // 2 - 1))
                    for i in range(2):
                        last = nc.scalar.activation(h_full[:, 2 * j + i, :], ps[:, j, i * CT:(i + 1) * CT], ACT.Gelu,
                                                    bias=b1T[:, 2 * j + i:2 * j + i + 1])
                    last.then_inc(s["sh_out"], 1)

            act.wait_ge(s["lgT_out"], B)
            act.wait_ge(s["x_kept"], 2 * B)
            x_rows(0)
            act.wait_ge(s["ws_in"], 32)
            for i in range(2):
                copy(ws_s[:, 0, i * KD * HID:(i + 1) * KD * HID], ws[:, i * KD * HID:(i + 1) * KD * HID], "ws_hi")
            x_turned(0, True)
            x_rows(1)
            act.wait_ge(s["eb_in"], 64)
            shared_gelu(0, True)
            x_turned(1)
            x_rows(2)
            act.wait_ge(s["r_exp_in"], 1)
            nc.scalar.activation(r1["e2"][:, :], r1["e2"][:, :], ACT.Exp).then_inc(s["r_exp"], 1)
            with act.Fori(1, CHUNKS - 2) as c:
                shared_gelu(c)
                x_turned(c + 1)
                x_rows(c + 2)
            shared_gelu(CHUNKS - 2)
            x_turned(CHUNKS - 1)
            shared_gelu(CHUNKS - 1)


            def expert_tiles(table_expert):
                def x_out(t, q, reused=True):
                    if reused:
                        act.wait_ge(s["h_ps"], t - 1)
                    act.wait_ge(s["xT_ps"], t + 1)
                    copy(xT[:, q, :, :], ps[:, 7 * q, 0:KD * P].rearrange("p (k t) -> p k t", k=KD), "xT_out")

                def gelu(t, q):
                    e = table_expert(t)
                    act.wait_ge(s["hT_ps"], t + 1)
                    for c in range(NH):
                        last = nc.scalar.activation(hT[:, c, :], ps[:, 4 + c // 4, (c % 4) * P:(c % 4 + 1) * P],
                                                    ACT.Gelu, bias=b1T[:, bass.ds(e * NH + c, 1)])
                    last.then_inc(s["hT_out"], 1)

                def weight(t, q):
                    act.wait_ge(s["meta_in"], 16)
                    act.wait_ge(s["y_sum"], t + 1)
                    if not (isinstance(t, int) and t < 2):
                        act.wait_ge(yw_sent[q], 8 * (t - q))
                    nc.scalar.activation(yw[:, q, :], ysum[:, q, :], ACT.Copy, scale=meta[:, bass.ds(t, 1), 1])\
                        .then_inc(s["y_out"], 1)

                def step(t, q):
                    if not isinstance(t, int) or t + 2 < TILES:
                        x_out(t + 2, q)
                    if not isinstance(t, int) or t + 1 < TILES:
                        gelu(t + 1, 1 - q)
                    weight(t, q)

                x_out(0, 0, False)
                x_out(1, 1, False)
                gelu(0, 0)
                step(0, 0)
                step(1, 1)
                with act.Fori(1, 1 + LOOPS) as i:
                    step(2 * i, 0)
                    step(2 * i + 1, 1)
                for t in range(REST, TILES):
                    step(t, t % 2)

            act.wait_ge(s["table_ready"], 1)
            expert_tiles(lambda t: act.value_load(table[0:1, bass.ds(t, 1)], min_val=0, max_val=E - 1) + 1)

            for b in range(B):
                act.wait_ge(s["f_bias"], b + 1)
                for n in range(NT):
                    last = nc.scalar.activation(fo[:, b, n, :], fo[:, b, n, :], ACT.Identity,
                                                scale=rstd_f[:, b, n:n + 1], bias=bias_f[:, b, n:n + 1])
                last.then_inc(s["f_out"], 1)

        @block.vector
        def _(dve):
            def lo_of(out, full, hi, name):
                nc.vector.tensor_tensor(out, full, hi.bitcast(F), ALU.subtract).then_inc(s[name], 1)

            def lo_of_bias(out, full, bias, hi, name):
                nc.vector.scalar_tensor_tensor(out=out, in0=full, scalar=bias, in1=hi.bitcast(F),
                                               op0=ALU.add, op1=ALU.subtract).then_inc(s[name], 1)

            dve.wait_ge(s["w1_in"], 64)
            nc.vector.tensor_copy(W_s[0][:, :, 0, :, :].rearrange("p w k n -> p w (k n)"),
                                  raw1[:, :, :, :].rearrange("p w k n -> p w (k n)")).then_inc(s["w1_hi"], 1)
            dve.wait_ge(s["w1_hi"], 1)
            nc.vector.tensor_tensor(W_s[0][:, :, 1, :, :].rearrange("p w k n -> p w (k n)"),
                                    raw1[:, :, :, :].rearrange("p w k n -> p w (k n)"),
                                    W_s[0][:, :, 0, :, :].rearrange("p w k n -> p w (k n)").bitcast(F),
                                    ALU.subtract).then_inc(s["w1_lo"], 1)
            nc.vector.memset(pT_s[:, :, :, :].bitcast(F), 0.0).then_inc(s["pT_zero"], 1)
            nc.vector.memset(k_stack[96:P, :, :].bitcast(F), 1.0).then_inc(s["k_ones"], 1)

            def norm_stats(c):
                at = 4 * c
                dve.wait_ge(s["ln_step"], at + 1)
                for n in range(NT):
                    last = nc.vector.bn_stats(stats[:, n, :], res[:, n, :])
                last.then_inc(s["ln_step"], 1)
                dve.wait_ge(s["ln_step"], at + 2)
                nc.vector.memset(var_eps[:, :], 0.0)
                for n in range(NT):
                    last = nc.vector.bn_aggr(mv[:, n, :], stats[:, n, :])
                last.then_inc(s["ln_step"], 1)
                dve.wait_ge(s["ln_step"], at + 3)
                nc.vector.tensor_scalar(var_eps[:, :], mv[:, :, 1], EPS, None, ALU.add).then_inc(s["ln_step"], 1)

            def norm_apply(c):
                dve.wait_ge(s["ln_pow"], c + 1)
                for n in range(NT):
                    last = nc.vector.tensor_scalar(res[:, n, :], res[:, n, :], mv[:, n, 0:1], rstd[:, n:n + 1],
                                                   ALU.subtract, ALU.mult)
                last.then_inc(s["ln_out"], 1)

            def residual(b, banks, name):
                for j in range(2):
                    dve.wait_ge(s[name], 2 * b + j + 1)
                    last = nc.vector.tensor_tensor(res[:, 2 * j:2 * j + 2, :],
                                                   ps[:, banks + j, :].rearrange("p (n d) -> p n d", n=2),
                                                   X[:, bass.ds(NT * b + 2 * j, 2), :], ALU.add)
                last.then_inc(s["ln_step"], 1)

            def glue_and_attention1(g, n, cg, cn):
                first = isinstance(n, int) and n == 0
                if g is not None:
                    combine(2 * g + 1, 1)
                if n is not None:
                    for j in range(4):
                        dve.wait_ge(s["qk1_hi"], 4 * n + j + 1)
                        t = (q1_s, c_s)[j // 2]
                        lo_of_bias(t[:, 1, j % 2, :], ps[:, 4 + j, :], bcol[:, j // 2, j % 2:j % 2 + 1],
                                   t[:, 0, j % 2, :], "qk1_lo")
                    for j in range(2):
                        dve.wait_ge(s["v1_hi"], 2 * n + j + 1)
                        lo_of(v_s[:, 1, 2 * j:2 * j + 2, :], ps[:, j, :].rearrange("p (n d) -> p n d", n=2),
                              v_s[:, 0, 2 * j:2 * j + 2, :], "v1_lo")
                if g is not None:
                    dve.wait_ge(s["at_hi"], g + 1)
                    lo_of(a_s[:, 1, :, :], ps[:, 2:4, :], a_s[:, 0, :, :], "at_lo")

                def maximum(i):
                    dve.wait_ge(s["s1_ps"], NT * n + i + 1)
                    diag = ps[:, 4 + i, i * P:(i + 1) * P]
                    nc.vector.tensor_tensor(diag, diag, causal[:, :], ALU.add).then_inc(s["s1_step"], 1)
                    dve.wait_ge(s["s1_step"], 2 * (NT * n + i) + 1)
                    nc.vector.tensor_reduce(nmax[:, 0, i:i + 1], ps[:, 4 + i, 0:(i + 1) * P], AX, ALU.max, negate=True)\
                        .then_inc(s["s1_step"], 1)
                    dve.wait_ge(s["s1_step"], 2 * (NT * n + i) + 2)
                    nc.vector.tensor_scalar(nmax[:, 1, i:i + 1], nmax[:, 0, i:i + 1], SCALE1, None, ALU.mult)\
                        .then_inc(s["s1_max"], 1)

                def normalise(i):
                    dve.wait_ge(s["s1_exp"], NT * n + i + 1)
                    nc.vector.reciprocal(den[:, 1, i:i + 1], den[:, 0, i:i + 1]).then_inc(s["p1_step"], 1)
                    dve.wait_ge(s["p1_step"], NT * n + i + 1)
                    w = (i + 1) * P
                    nc.vector.tensor_scalar(probs[:, i, 0:w], probs[:, i, 0:w], den[:, 1, i:i + 1], None, ALU.mult)\
                        .then_inc(s["p1_norm"], 1)

                def turned(i):
                    dve.wait_ge(s["pt_hi"], NT * n + i + 1)
                    lo_of(pT_s[:, 1, 0:i + 1, i * P:(i + 1) * P],
                          ps[:, PT_BANK[i], 0:(i + 1) * P].rearrange("p (j q) -> p j q", q=P),
                          pT_s[:, 0, 0:i + 1, i * P:(i + 1) * P], "pt_lo")

                if n is not None:
                    if first:
                        dve.wait_ge(s["consts"], 5)
                    maximum(0)
                    maximum(1)
                    normalise(0)
                    maximum(2)
                    normalise(1)
                    turned(0)
                    maximum(3)
                    normalise(2)
                    turned(1)
                    normalise(3)
                    turned(2)
                    turned(3)
                if g is not None:
                    dve.wait_ge(s["x_kept"], cg)
                    residual(g, 2, "w2_ps")
                    norm_stats(cg)
                    norm_apply(cg)
                if n is not None:
                    for j in range(2):
                        dve.wait_ge(s["o1_hi"], 2 * n + j + 1)
                        lo_of_bias(c_s[:, 1, j, :], ps[:, 6 + j, :], bcol[:, 2, j:j + 1], c_s[:, 0, j, :], "o1_lo")
                    if first:
                        dve.wait_ge(s["xbo"], B)
                    else:
                        dve.wait_ge(s["x_kept"], cn)
                    if g is not None:
                        dve.wait_ge(s["g_ps"], g + 1)
                    residual(n, 0, "w1_ps")
                if g is not None:
                    dve.wait_ge(s["lg_ps"], g + 1)
                    nc.vector.tensor_scalar(lgT, ps[0:E, 4, :], gate_b[:, 0:1], None, ALU.add).then_inc(s["lg_out"], 1)

            def gates(b):
                dve.wait_ge(s["lgT_ps"], b + 1)
                nc.vector.tensor_copy(logits[:, bass.ts(b, NT), :],
                                      ps[:, 6, 0:NT * E].rearrange("p (n e) -> p n e", e=E)).then_inc(s["lgT_out"], 1)

            def project2(b, g, c):
                dve.wait_ge(s["x1_hi"], b + 1)
                lo_of(a_s[:, 1, :, :], ps[:, 4:6, :], a_s[:, 0, :, :], "x1_lo")
                if g is not None:
                    gates(g)
                for j, (t, blk) in enumerate(((k_s, 0), (q_s, 0), (k_s, 1), (q_s, 1))):
                    dve.wait_ge(s["qk2_hi"], 4 * b + j + 1)
                    lo_of_bias(t[:, blk, 1, :], ps[:, 7 - j % 2, :], bcol[:, 4 - j % 2, blk:blk + 1], t[:, blk, 0, :], "qk2_lo")
                    if j == 1 and c is not None:
                        if g is None:
                            dve.wait_ge(s["pad_out"], 32)
                        combine(c, 0)

            def out_cross(c, g):
                dve.wait_ge(s["pv_done"], 8 * c + 4 * g + 4)
                nc.vector.tensor_copy(oT[:, g, 1, :], ps[:, 7, :]).then_inc(s["os_out"], 1)

            def half(a, c, h, norm=None):
                if a is not None:
                    for u in range(UNITS):
                        p, n = u // NT, u % NT
                        k0, nb = max(n - 1, 0), 3 if 0 < n < NT - 1 else 2
                        r0 = k0 - n + 1
                        dve.wait_ge(s["a_ps"], UNITS * a + u + 1)
                        nc.vector.tensor_reduce(mx[:, n, 2 * p:2 * p + 2, r0:r0 + nb],
                                                ps[:, 2 * (u % 2):2 * (u % 2) + 2, 0:nb * P].rearrange("p h (b k) -> p h b k", k=P),
                                                AX, ALU.max, negate=True).then_inc(s["a_red"], 1)
                        if u == 1 and norm is not None:
                            norm_stats(norm)
                        if u == 3 and norm is not None:
                            norm_apply(norm)
                        if u == 9 and c is not None:
                            out_cross(c, 0)
                    at = 3 * a
                    dve.wait_ge(s["a_red"], UNITS * a + UNITS)
                    nc.vector.tensor_reduce(ncross[:, :, :], mx[:, :, :, :], AX, ALU.min).then_inc(s["aug_step"], 1)
                    dve.wait_ge(s["aug_step"], at + 1)
                    nc.vector.tensor_tensor(dloc[:, h, :, :], mx[:, :, :, 1], ncross[:, :, :], ALU.subtract)
                    nc.vector.tensor_copy(aug[:, :, 0, :], ncross[:, :, :]).then_inc(s["aug_step"], 1)
                    dve.wait_ge(s["aug_step"], at + 2)
                    nc.vector.tensor_tensor(aug[:, :, 1, :], ncross[:, :, :], aug[:, :, 0, :].bitcast(F), ALU.subtract)
                    nc.vector.tensor_copy(aug[:, :, 2, :], dloc[:, h, :, :]).then_inc(s["aug_step"], 1)
                    dve.wait_ge(s["aug_step"], at + 3)
                    nc.vector.tensor_tensor(aug[:, :, 3, :], dloc[:, h, :, :], aug[:, :, 2, :].bitcast(F), ALU.subtract)\
                        .then_inc(s["aug_ready"], 1)
                elif c is not None:
                    out_cross(c, 0)
                if c is not None:
                    out_cross(c, 1)

            def combine(c, h):
                def part(k, lo, hi):
                    x = ps[:, 0:NT, :].rearrange("p n (c g j d) -> p n c (g j) d", c=2, g=2, j=4)
                    return x[:, :, k, :, lo:hi]

                l_loc = part(0, DH, DH + 1).rearrange("p n j o -> p n (j o)")
                l_side = part(1, DH, DH + 1).rearrange("p n j o -> p n (j o)")
                at = 6 * c
                k = [0]

                def link(ins):
                    k[0] += 1
                    ins.then_inc(s["cb_step"], 1)
                    dve.wait_ge(s["cb_step"], at + k[0])

                dve.wait_ge(s["w_exp"], c + 1)
                dve.wait_ge(s["cb_ps"], c + 1)
                nc.vector.reciprocal(cw[:, 3, :, :], l_loc)
                link(nc.vector.tensor_tensor(cw[:, 0, :, :], wloc[:, :, :], l_loc, ALU.mult))
                link(nc.vector.tensor_tensor(cw[:, 1, :, :], cw[:, 0, :, :], l_side, ALU.add))
                link(nc.vector.reciprocal(cw[:, 2, :, :], cw[:, 1, :, :]))
                link(nc.vector.tensor_tensor(cw[:, 0, :, :], wloc[:, :, :], cw[:, 2, :, :], ALU.mult))
                nc.vector.tensor_tensor(cmb[:, :, :, :], part(1, 0, DH),
                                        cw[:, 2, :, :].unsqueeze(3).broadcast_to([P, NT, HALF, DH]), ALU.mult)
                link(nc.vector.tensor_tensor(cw[:, 1, :, :], cw[:, 0, :, :], cw[:, 3, :, :], ALU.add))
                av = attn[:, :, h * P:(h + 1) * P].rearrange("p n (j d) -> p n j d", d=DH)
                link(nc.vector.tensor_tensor(av, part(0, 0, DH),
                                             cw[:, 1, :, :].unsqueeze(3).broadcast_to([P, NT, HALF, DH]), ALU.mult))
                nc.vector.tensor_tensor(av, av, cmb[:, :, :, :], ALU.add).then_inc(s["cb_out"], 1)

            def body(b, first, last):
                half(2 * b, None if first else 2 * b - 1, 0)
                glue_and_attention1(None if first else b - 1, None if last else b + 1, 2 * b, 2 * b + 1)
                half(2 * b + 1, 2 * b, 1, None if last else 2 * b + 1)
                if not last:
                    project2(b + 1, None if first else b - 1, 2 * b)
                else:
                    gates(b - 1)
                    combine(2 * b, 0)

            glue_and_attention1(None, 0, None, 0)
            norm_stats(0)
            norm_apply(0)
            project2(0, None, None)
            dve.wait_ge(s["masks"], 2)
            body(0, True, False)
            with dve.Fori(1, B - 1) as b:
                body(b, False, False)
            body(B - 1, False, True)
            half(None, 2 * B - 1, 1)
            glue_and_attention1(B - 1, None, 2 * B - 1, None)
            gates(B - 1)

            k = [0]

            def link(ins):
                k[0] += 1
                ins.then_inc(s["r_step"], 1)
                dve.wait_ge(s["r_step"], k[0])

            def bc(x):
                return x[:, :].unsqueeze(2).broadcast_to([P, B * NT, E])

            def tt(out, a, b_, op):
                return nc.vector.tensor_tensor(out, a, b_, op)

            def x_split(c, first=False):
                dve.wait_ge(s["sxT_out"], c + 1)
                if not first:
                    dve.wait_ge(s["sh_ps"], 4 * c)
                nc.vector.tensor_copy(xT_s[:, 0, :, :], xT_full[:, :, :]).then_inc(s["sx_hi"], 1)
                dve.wait_ge(s["sx_hi"], c + 1)
                lo_of(xT_s[:, 1, :, :], xT_full[:, :, :], xT_s[:, 0, :, :], "sx_lo")

            def h_split(c, first=False):
                for i in range(2):
                    h = slice(i * NH // 2, (i + 1) * NH // 2)
                    dve.wait_ge(s["sh_out"], 4 * c + 2 * i + 2)
                    if not first:
                        dve.wait_ge(s["sy_ps"], c)
                    nc.vector.tensor_copy(h_s[:, 0, h, :], h_full[:, h, :]).then_inc(s["sh_hi"], 1)
                    dve.wait_ge(s["sh_hi"], 2 * c + i + 1)
                    lo_of(h_s[:, 1, h, :], h_full[:, h, :], h_s[:, 0, h, :], "sh_lo")

            def y_out(c):
                dve.wait_ge(s["sy_ps"], c + 1)
                nc.vector.tensor_tensor(shared_y[:, bass.ds(2 * c, 2), :], ps[:, 4:6, 0:D],
                                        b2b[:, 0:1, :].broadcast_to([P, 2, D]), ALU.add).then_inc(s["sy_out"], 1)

            dve.wait_ge(s["lgT_out"], B)
            dve.wait_ge(s["ws_hi"], 1)
            lo_of(ws_s[:, 1, 0:KD * HID], ws[:, 0:KD * HID], ws_s[:, 0, 0:KD * HID], "ws1_lo")
            x_split(0, True)
            desc = desc8[:, :].unsqueeze(1).broadcast_to([P, B * NT, E])
            dve.wait_ge(s["consts2"], 12)
            dve.wait_ge(s["lgT_out"], B)
            for src, m, i, oh in ((logits, "m1", "i1", "oh1"), (R["lg2"], "m2", "i2", "oh2")):
                link(nc.vector.tensor_reduce(r1[m][:, :], src[:, :, :], AX, ALU.max))
                link(tt(R["t0"][:, :, :], src[:, :, :], bc(r1[m]), ALU.is_equal))
                link(tt(R["t0"][:, :, :], R["t0"][:, :, :], desc, ALU.mult))
                link(nc.vector.tensor_reduce(r1[i][:, :], R["t0"][:, :, :], AX, ALU.max))
                link(tt(R[oh][:, :, :], desc, bc(r1[i]), ALU.is_equal))
                if m == "m1":
                    link(nc.vector.scalar_tensor_tensor(out=R["lg2"][:, :, :], in0=R["oh1"][:, :, :], scalar=NEG,
                                                        in1=logits[:, :, :], op0=ALU.mult, op1=ALU.add))
            tt(r1["e2"][:, :], r1["m2"][:, :], r1["m1"][:, :], ALU.subtract).then_inc(s["r_exp_in"], 1)
            tt(R["mask"][:, :, :], R["oh1"][:, :, :], R["oh2"][:, :, :], ALU.add).then_inc(s["r_exp_in"], 1)
            x_split(1)
            h_split(0, True)
            dve.wait_ge(s["r_ps"], 2)
            link(nc.vector.tensor_copy(R["c0"][:, :, :], ps[:, 6, 128:256].rearrange("p (t e) -> p t e", e=E)))
            a, b_ = R["c0"], R["c1"]
            for sh in (1, 2, 4, 8):
                nc.vector.tensor_copy(b_[:, 0:sh, :], a[:, 0:sh, :])
                link(tt(b_[:, sh:, :], a[:, sh:, :], a[:, 0:B * NT - sh, :], ALU.add))
                a, b_ = b_, a
            link(tt(cmp[:, :, :], a[:, B * NT - 1, :].unsqueeze(2).broadcast_to([P, E, 16]),
                    step128[:, :].unsqueeze(1).broadcast_to([P, E, 16]), ALU.is_gt))
            link(nc.vector.tensor_reduce(nt_e[:, :], cmp[:, :, :], AX, ALU.add))
            link(nc.vector.tensor_tensor_scan(end_e[:, :], one_e[:, :], nt_e[:, :], 0.0, ALU.mult, ALU.add))
            link(tt(beg_e[:, :], end_e[:, :], nt_e[:, :], ALU.subtract))
            link(nc.vector.tensor_scalar(beg_e[:, :], beg_e[:, :], float(P), None, ALU.mult))
            link(tt(R["pos"][:, :, :], a[:, :, :], ps[:, 6, 128:256].rearrange("p (t e) -> p t e", e=E), ALU.subtract))
            link(tt(R["pos"][:, :, :], R["pos"][:, :, :], ps[:, 6, 0:128].rearrange("p (t e) -> p t e", e=E), ALU.add))
            link(tt(R["pos"][:, :, :], R["pos"][:, :, :], beg_e[:, :].unsqueeze(1).broadcast_to([P, B * NT, E]), ALU.add))
            for oh, sl in (("oh1", "s1"), ("oh2", "s2")):
                link(tt(R["t0"][:, :, :], R[oh][:, :, :], R["pos"][:, :, :], ALU.mult))
                link(nc.vector.tensor_reduce(r1[sl][:, :], R["t0"][:, :, :], AX, ALU.add))
            link(tt(cmpt[:, :, :], tile_no[:, :].unsqueeze(2).broadcast_to([P, TILES, E]),
                    end_e[:, :].unsqueeze(1).broadcast_to([P, TILES, E]), ALU.is_ge))
            link(nc.vector.tensor_reduce(tab_f[:, :], cmpt[:, :, :], AX, ALU.add))
            link(nc.vector.tensor_scalar(table[:, :], tab_f[:, :], float(E - 1), None, ALU.min))
            dve.wait_ge(s["r_exp"], 1)
            link(nc.vector.tensor_scalar(r1["m1"][:, :], r1["e2"][:, :], 1.0, None, ALU.add))
            link(nc.vector.reciprocal(r1["g1"][:, :], r1["m1"][:, :]))
            link(tt(r1["g2"][:, :], r1["e2"][:, :], r1["g1"][:, :], ALU.mult))
            for k, (g, sl) in enumerate((("g1", "s1"), ("g2", "s2"))):
                nc.vector.tensor_copy(slot_tab[:, :, k], r1[sl][:, :])
                last = nc.vector.tensor_copy(meta_tab[:, :, k, 1], r1[g][:, :])
            last.then_inc(s["slots_ready"], 1)
            nc.vector.tensor_copy(r1["m2"][:, :], r1["g1"][:, :]).then_inc(s["table_ready"], 1)
            dve.wait_ge(s["eb_in"], 64)
            dve.wait_ge(s["ws2_lo"], 1)
            x_split(2)
            h_split(1)
            y_out(0)
            with dve.Fori(1, CHUNKS - 2) as c:
                x_split(c + 2)
                h_split(c + 1)
                y_out(c)
            h_split(CHUNKS - 1)
            y_out(CHUNKS - 2)
            y_out(CHUNKS - 1)

            def expert_tiles(table_expert):
                def h_out(t):
                    dve.wait_ge(s["h_ps"], t + 1)
                    if not (isinstance(t, int) and t == 0):
                        dve.wait_ge(s["hT_ps"], t)
                    for c in range(2):
                        last = nc.vector.tensor_copy(hp[:, c * 512:(c + 1) * 512], ps[:, 2 + c, :])
                    last.then_inc(s["h_out"], 1)

                def y_sum(t, q, free):
                    e = table_expert(t)
                    dve.wait_ge(s["y_ps"], t + 1)
                    if free:
                        dve.wait_ge(s["y_out"], t - 1)
                    nc.vector.tensor_tensor(ysum[:, q, :], ps[:, 6, 0:D],
                                            b2b[:, bass.ds(e, 1), :].rearrange("p o d -> p (o d)"), ALU.add)\
                        .then_inc(s["y_sum"], 1)

                h_out(0)
                for t in range(2):
                    h_out(t + 1)
                    y_sum(t, t, False)
                with dve.Fori(1, 1 + LOOPS) as i:
                    for q in range(2):
                        h_out(2 * i + q + 1)
                        y_sum(2 * i + q, q, True)
                for t in range(REST, TILES):
                    if t + 1 < TILES:
                        h_out(t + 1)
                    y_sum(t, t % 2, True)

            expert_tiles(lambda t: dve.value_load(table[0:1, bass.ds(t, 1)], min_val=0, max_val=E - 1) + 1)

            def sums(b):
                dve.wait_ge(yl_in[b], 16)
                if b:
                    dve.wait_ge(s["f_x"], b)
                else:
                    dve.wait_ge(s["x_sum"], B)
                    nc.vector.tensor_tensor(yl[:, b, :, 0, :], yl[:, b, :, 0, :], X[:, 0:NT, :], ALU.add)\
                        .then_inc(s["f_x0"], 1)
                    dve.wait_ge(s["f_x0"], 1)
                nc.vector.tensor_tensor(fo[:, b, :, :], yl[:, b, :, 0, :], yl[:, b, :, 1, :], ALU.add).then_inc(s["f_step"], 1)
                dve.wait_ge(s["f_step"], 3 * b + 1)
                for n in range(NT):
                    last = nc.vector.bn_stats(stats_f[:, b, n, :], fo[:, b, n, :])
                last.then_inc(s["f_step"], 1)
                dve.wait_ge(s["f_step"], 3 * b + 2)
                for n in range(NT):
                    last = nc.vector.bn_aggr(mean_f[:, b, n, :], stats_f[:, b, n, :])
                last.then_inc(s["f_step"], 1)
                dve.wait_ge(s["f_step"], 3 * b + 3)
                nc.vector.tensor_scalar(var_f[:, b, :], mean_f[:, b, :, 1], EPS, None, ALU.add).then_inc(s["f_var"], 1)

            def bias(b):
                dve.wait_ge(s["f_pow"], b + 1)
                nc.vector.scalar_tensor_tensor(out=bias_f[:, b, :], in0=mean_f[:, b, :, 0], scalar=-1.0,
                                               in1=rstd_f[:, b, :], op0=ALU.mult, op1=ALU.mult).then_inc(s["f_bias"], 1)

            sums(0)
            for b in range(1, B):
                sums(b)
                bias(b - 1)
            bias(B - 1)

        @block.tensor
        def _(pe):
            def keep_clock(n, w=None, bank=5):
                w = W_s[1][:, 0, 0, :, :].rearrange("p k n -> p (k n)") if w is None else w
                for _ in range(n):
                    nc.tensor.matmul(ps[:, bank, :], w[:, 0:P], w, start=True, stop=True)

            def turn(bank, src, name):
                for n in range(NT):
                    for k in range(KD):
                        m = nc.tensor.transpose(ps[:, bank + k, n * P:(n + 1) * P], src[:, n, k * P:(k + 1) * P], ident[:, :])
                m.then_inc(s[name], 1)

            def rows_of(bank, src, w, i, name):
                for n in range(NT):
                    for k in range(KD):
                        m = mm3(pe, ps[:, bank + n // 2, (n % 2) * D:(n % 2 + 1) * D],
                                lambda l: src[:, l, k, n * P:(n + 1) * P], lambda l: w[:, i, l, k, :],
                                k == 0, k == KD - 1)
                    if n % 2:
                        m.then_inc(s[name], 1)

            def glue_and_attention1(g, n, cg, cn):
                w = W_s[0]
                if g is not None:
                    turn_out(2 * g + 1)
                    if n is None:
                        keep_clock(WARM)
                if n is not None:
                    pe.wait_ge(s["xa_lo"], n + 1)
                    if isinstance(n, int) and n == 0:
                        pe.wait_ge(s["w1_lo"], 1)
                    for j in range(4):
                        for k in range(KD):
                            m = mm3(pe, ps[:, 4 + j, :], lambda l: w[:, j // 2, l, k, (j % 2) * P:(j % 2 + 1) * P],
                                    lambda l: a_s[:, l, k, :], k == 0, k == KD - 1)
                        m.then_inc(s["qk1_ps"], 1)
                if g is not None:
                    pe.wait_ge(s["cb_out"], 2 * g + 2)
                if n is not None:
                    rows_of(0, a_s, w, 2, "v1_ps")
                if g is not None:
                    turn(2, attn, "at_ps")
                    if n is None:
                        keep_clock(WARM // 2)
                if n is not None:
                    pe.wait_ge(s["qk1_lo"], 4 * n + 4)
                    for i in range(NT):
                        wd = max(i + 1, 2) * P
                        for k in range(KD):
                            m = mm3(pe, ps[:, 4 + i, 0:wd], lambda l: q1_s[:, l, k, i * P:(i + 1) * P],
                                    lambda l: c_s[:, l, k, 0:wd], k == 0, k == KD - 1)
                        m.then_inc(s["s1_ps"], 1)
                if g is not None:
                    pe.wait_ge(s["at_lo"], g + 1)
                    rows_of(2, a_s, W_s[1], 3, "w2_ps")
                    if n is None:
                        keep_clock(WARM)
                if n is not None:
                    if isinstance(n, int) and n == 0:
                        pe.wait_ge(s["consts"], 5)
                    pe.wait_ge(s["v1_lo"], 2 * n + 2)
                    for i in range(NT):
                        pe.wait_ge(s["p1_norm"], NT * n + i + 1)
                        for j in range(i + 1):
                            m = nc.tensor.transpose(ps[:, PT_BANK[i], j * P:(j + 1) * P], probs[:, i, j * P:(j + 1) * P],
                                                    ident[:, :])
                        m.then_inc(s["pt_ps"], 1)
                    pe.wait_ge(s["pt_lo"], NT * n + NT)
                    for d in range(KD):
                        for j in range(NT):
                            q0 = min(j, NT - 2) * P
                            m = mm3(pe, ps[:, 6 + d, q0:S], lambda l: v_s[:, l, j, d * P:(d + 1) * P],
                                    lambda l: pT_s[:, l, j, q0:S], j == 0, j == NT - 1, True)
                        m.then_inc(s["o1_ps"], 1)
                if g is not None:
                    pe.wait_ge(s["ln_out"], cg + 1)
                    turn(2, res, "g_ps")
                if n is not None:
                    pe.wait_ge(s["o1_lo"], 2 * n + 2)
                    rows_of(0, c_s, w, 3, "w1_ps")
                    if g is None:
                        keep_clock(WARM, w[:, 0, 0, :, :].rearrange("p k n -> p (k n)"))
                if g is not None:
                    pe.wait_ge(s["g_out"], g + 1)
                    for k in range(KD):
                        m = nc.tensor.matmul(ps[0:E, 4, :], gate_w[:, k, :], x2T[:, k, :], start=k == 0, stop=k == KD - 1)
                    m.then_inc(s["lg_ps"], 1)
                if n is not None:
                    pe.wait_ge(s["ln_step"], 4 * cn + 1)
                if g is not None:
                    pe.wait_ge(s["lg_out"], g + 1)

            def gates(b):
                for i in range(NT):
                    m = nc.tensor.transpose(ps[:, 6, i * E:(i + 1) * E], lgT[:, i * P:(i + 1) * P], ident[0:E, 0:E])
                m.then_inc(s["lgT_ps"], 1)

            def project2(b, cn, c, g):
                w = W_s[1]
                if c is None:
                    pe.wait_ge(s["wsplit"], 4)
                else:
                    pe.wait_ge(s["oc_out"], 2 * c + 2)
                    pe.wait_ge(s["os_out"], 2 * c + 2)
                pe.wait_ge(s["ln_out"], cn + 1)
                turn(4, res, "x1_ps")
                if g is not None:
                    gates(g)
                for j, blk in enumerate((0, 0, 1, 1)):
                    if j == 0:
                        pe.wait_ge(s["ctx_lo"], b + 1)
                    if j == 1:
                        pe.wait_ge(s["x1_lo"], b + 1)
                        if g is not None:
                            pe.wait_ge(s["lgT_out"], g + 1)
                    if j >= 2:
                        pe.wait_ge(s["qk2_lo"], 4 * b + j - 1)
                    src = (c_s, a_s)[j % 2]
                    for k in range(KD):
                        m = mm3(pe, ps[:, 7 - j % 2, :], lambda l: w[:, 1 - j % 2, l, k, blk * P:(blk + 1) * P],
                                lambda l: src[:, l, k, :], k == 0, k == KD - 1)
                    m.then_inc(s["qk2_ps"], 1)
                    if j == 0 and c is not None:
                        pe.wait_ge(s["augT_out"], c + 2)
                        turn_out(c)
                    if j == 1:
                        rows_of(4, c_s, w, 2, "v2_ps")
                pe.wait_ge(s["v2_out"], 2 * b + 2)
                keep_clock(WARM)
                pe.wait_ge(s["qk2_lo"], 4 * b + 4)

            def half(a, c, ha, hc, full):
                def pv_local(m):
                    g, i = m // NT, m % NT
                    pe.wait_ge(s["b_exp"], 2 * (UNITS * c + 2 * m + 2) - 1)
                    if i == 0 and (full or g):
                        pe.wait_ge(s["oc_out"], 2 * c + g)
                    for j in range(4):
                        nc.tensor.matmul(ps[32 * j:32 * j + 32, 6, i * P:(i + 1) * P],
                                         v_aug[:, i, hc * HALF + 4 * g + j, :],
                                         pT[:, m % 2, j // 2, (j % 2) * P:(j % 2 + 1) * P],
                                         start=True, stop=True, skip_group_check=True)

                def pv_sides(m):
                    g, i = m // NT, m % NT
                    sides = side_blocks(i)
                    pe.wait_ge(s["b_exp"], 2 * (UNITS * c + 2 * m + 2))
                    if i == 0 and (full or g):
                        pe.wait_ge(s["os_out"], 2 * c + g)
                    w = len(sides) * P
                    for j in range(4):
                        out = ps[32 * j:32 * j + 32, 7, :].rearrange("p (n q) -> p n q", q=P)[:, sides[0]:sides[-1] + 1:2, :]
                        last = nc.tensor.matmul(
                            out, v_aug[:, i, hc * HALF + 4 * g + j, :],
                            pT[:, m % 2, j // 2, 2 * P + (j % 2) * w:2 * P + (j % 2 + 1) * w].rearrange("p (n q) -> p n q", q=P),
                            start=i == 0, stop=True, skip_group_check=True)
                    last.then_inc(s["pv_done"], 1)

                if c is not None:
                    pe.wait_ge(s["k_ones"], 1)
                    pe.wait_ge(s["aug_in"], 64 * (c + 1))
                for u in range(UNITS):
                    if a is not None:
                        p, n = u // NT, u % NT
                        k0, nb = max(n - 1, 0), 3 if 0 < n < NT - 1 else 2
                        if n == 0:
                            pe.wait_ge(stacked[p], 16 * PAIR_DMAS * (a + 1))
                        if u >= 2:
                            pe.wait_ge(s["a_red"], UNITS * a + u - 1)
                        for j in range(2):
                            m = nc.tensor.matmul(ps[:, 2 * (u % 2) + j, 0:nb * P],
                                                 q_stack[0:96, ha * HALF + 2 * p + j, n * P:(n + 1) * P],
                                                 k_stack[0:96, ha * (HALF // 2) + p, k0 * P:(k0 + nb) * P],
                                                 start=True, stop=True)
                        m.then_inc(s["a_ps"], 1)
                    if c is not None:
                        g, i, p = u // 8, (u // 2) % NT, hc * (HALF // 2) + 2 * (u // 8) + u % 2
                        bank = 2 if a is None and u % 2 else 4
                        old = u - 1 if a is not None else u - 2
                        waits = old >= 0 or (a is not None and full)
                        if waits:
                            pe.wait_ge(s["b_exp"], 2 * (UNITS * c + old) + 1)
                        sides = side_blocks(i)
                        qv = q_stack[:, 2 * p:2 * p + 2, :]
                        nc.tensor.matmul(ps[:, bank, 256:512].rearrange("p (h q) -> p h q", h=2),
                                         k_stack[0:100, p, i * P:(i + 1) * P], qv[0:100, :, i * P:(i + 1) * P],
                                         start=True, stop=True).then_inc(s["b_ps"], 1)
                        if waits:
                            pe.wait_ge(s["b_exp"], 2 * (UNITS * c + old) + 2)
                        w = 2 * len(sides) * P
                        nc.tensor.matmul(ps[:, bank + 1, 0:w].rearrange("p (h n q) -> p h n q", h=2, q=P),
                                         k_stack[0:98, p, i * P:(i + 1) * P],
                                         qv[0:98, :, :].rearrange("p h (n q) -> p h n q", q=P)[:, :, sides[0]:sides[-1] + 1:2, :],
                                         start=True, stop=True).then_inc(s["b_ps"], 1)
                        if u >= 2:
                            (pv_local, pv_sides)[u % 2](u // 2 - 1)
                if c is not None:
                    pv_local(UNITS // 2 - 1)
                    pv_sides(UNITS // 2 - 1)
                if a is not None:
                    pe.wait_ge(s["aug_ready"], a + 1)
                    for n in range(NT):
                        m = nc.tensor.transpose(ps[0:4 * HALF, 2, n * P:(n + 1) * P],
                                                aug[:, n, :, :].rearrange("p r h -> p (r h)").bitcast(F), ident[:, :])
                    m.then_inc(s["augT_ps"], 1)

            def turn_out(c):
                pe.wait_ge(s["oc_out"], 2 * c + 2)
                pe.wait_ge(s["os_out"], 2 * c + 2)
                for n in range(NT):
                    for k in range(2):
                        for g in range(2):
                            m = nc.tensor.transpose(ps[:, n, (2 * k + g) * P:(2 * k + g + 1) * P],
                                                    oT[:, g, k, n * P:(n + 1) * P], ident[:, :])
                m.then_inc(s["cb_ps"], 1)

            def body(b, first, last):
                half(2 * b, None if first else 2 * b - 1, 0, 1, not first)
                pe.wait_ge(s["augT_out"], 2 * b + 1)
                glue_and_attention1(None if first else b - 1, None if last else b + 1, 2 * b, 2 * b + 1)
                pe.wait_ge(s["v_set"], b + 1)
                half(2 * b + 1, 2 * b, 1, 0, not first)
                if not last:
                    project2(b + 1, 2 * b + 1, 2 * b, None if first else b - 1)
                else:
                    pe.wait_ge(s["oc_out"], 4 * b + 2)
                    gates(b - 1)
                    pe.wait_ge(s["augT_out"], 2 * b + 2)
                    turn_out(2 * b)
                    keep_clock(WARM_B)
                    pe.wait_ge(s["lgT_out"], b)
                pe.wait_ge(s["cb_out"], 2 * b + 1)

            glue_and_attention1(None, 0, None, 0)
            project2(0, 0, None, None)
            body(0, True, False)
            with pe.Fori(1, B - 1) as b:
                body(b, False, False)
            body(B - 1, False, True)
            half(None, 2 * B - 1, 0, 1, True)
            glue_and_attention1(B - 1, None, 2 * B - 1, None)
            gates(B - 1)

            def turn_chunk(c, first=False):
                pe.wait_ge(s["sx_out"], c + 1)
                if not first:
                    pe.wait_ge(s["sxT_out"], c)
                for k in range(KD):
                    for n in range(2):
                        m = nc.tensor.transpose(ps[:, 7, k * CT + n * P:k * CT + (n + 1) * P],
                                                xs[:, n, k * P:(k + 1) * P], ident[:, :])
                m.then_inc(s["sxT_ps"], 1)

            def shared_hidden(c, first=False):
                pe.wait_ge(s["sx_lo"], c + 1)
                for j in range(NH // 2):
                    if not first:
                        pe.wait_ge(s["sh_out"], 4 * c + j - 3)
                    for i in range(2):
                        for k in range(KD):
                            at = k * HID + (2 * j + i) * P
                            m = mm3(pe, ps[:, j, i * CT:(i + 1) * CT], lambda l: ws_s[:, l, at:at + P],
                                    lambda l: xT_s[:, l, k, :], k == 0, k == KD - 1)
                    m.then_inc(s["sh_ps"], 1)

            def shared_output(c, first=False):
                if not first:
                    pe.wait_ge(s["sy_out"], c)
                for h in range(NH):
                    if h % (NH // 2) == 0:
                        pe.wait_ge(s["sh_lo"], 2 * c + h // (NH // 2) + 1)
                    at = KD * HID + h * D
                    for n in range(2):
                        m = mm3(pe, ps[:, 4 + n, 0:D], lambda l: h_s[:, l, h, n * P:(n + 1) * P],
                                lambda l: ws_s[:, l, at:at + D], h == 0, h == NH - 1)
                m.then_inc(s["sy_ps"], 1)

            turn_chunk(0, True)
            pe.wait_ge(s["ws1_lo"], 1)
            shared_hidden(0, True)
            turn_chunk(1)
            pe.wait_ge(s["consts2"], 12)
            pe.wait_ge(s["r_exp_in"], 2)
            mask = R["mask"][:, :, :].rearrange("p t e -> p (t e)")
            nc.tensor.matmul(ps[:, 6, 0:128], upper[:, :], mask, start=True, stop=True).then_inc(s["r_ps"], 1)
            nc.tensor.matmul(ps[:, 6, 128:256], ones[:, :], mask, start=True, stop=True).then_inc(s["r_ps"], 1)
            pe.wait_ge(s["ws2_lo"], 1)
            shared_hidden(1)
            turn_chunk(2)
            shared_output(0, True)
            with pe.Fori(1, CHUNKS - 2) as c:
                shared_hidden(c + 1)
                turn_chunk(c + 2)
                shared_output(c)
            shared_hidden(CHUNKS - 1)
            shared_output(CHUNKS - 2)
            keep_clock(WARM_E, ws_s[:, 0, 0:512], 6)
            shared_output(CHUNKS - 1)
            pe.wait_ge(s["sy_out"], CHUNKS)
            pe.wait_ge(s["sh_out"], 4 * CHUNKS)
            pe.wait_ge(s["sxT_out"], CHUNKS)


            def expert_tiles(w):
                def turn_x(t, q):
                    pe.wait_ge(xs_in[q], 8 * (t - q) + 16)
                    if not (isinstance(t, int) and t < 2):
                        pe.wait_ge(s["xT_out"], t - 1)
                    for k in range(KD):
                        m = nc.tensor.transpose(ps[:, 7 * q, k * P:(k + 1) * P],
                                                xs[:, q, k * P:(k + 1) * P], ident[:, :])
                    m.then_inc(s["xT_ps"], 1)

                def expert(t):
                    return pe.value_load(table[0:1, bass.ds(t, 1)], min_val=0, max_val=E - 1)

                def weights(e):
                    pe.wait_ge(s["we_in"], (e // EARLY) * (32 * EARLY) + 32 * EARLY)

                def hidden(t, q, e):
                    pe.wait_ge(s["xT_out"], t + 1)
                    if not (isinstance(t, int) and t == 0):
                        pe.wait_ge(s["h_out"], t)
                    for c in range(2):
                        for k in range(KD):
                            m = nc.tensor.matmul(
                                ps[:, 2 + c, :], xT[:, q, k, :],
                                w[:, bass.ds(e, 1), k * HID + c * 512:k * HID + (c + 1) * 512].rearrange("p o n -> p (o n)"),
                                start=k == 0, stop=k == KD - 1)
                    m.then_inc(s["h_ps"], 1)

                def turn_h(t):
                    pe.wait_ge(s["h_out"], t + 1)
                    if not (isinstance(t, int) and t == 0):
                        pe.wait_ge(s["hT_out"], t)
                    for c in range(NH):
                        m = nc.tensor.transpose(ps[:, 4 + c // 4, (c % 4) * P:(c % 4 + 1) * P],
                                                hp[:, c * P:(c + 1) * P], ident[:, :])
                    m.then_inc(s["hT_ps"], 1)

                def output(t, e):
                    pe.wait_ge(s["hT_out"], t + 1)
                    if not (isinstance(t, int) and t == 0):
                        pe.wait_ge(s["y_sum"], t)
                    for c in range(NH):
                        m = nc.tensor.matmul(
                            ps[:, 6, 0:D], hT[:, c, :],
                            w[:, bass.ds(e, 1), KD * HID + c * D:KD * HID + (c + 1) * D].rearrange("p o n -> p (o n)"),
                            start=c == 0, stop=c == NH - 1)
                    m.then_inc(s["y_ps"], 1)

                turn_x(0, 0)
                turn_x(1, 1)
                pe.wait_ge(s["table_ready"], 1)
                e0, e1, e2 = expert(0), expert(1), expert(2)
                weights(e2)
                hidden(0, 0, e0)
                turn_h(0)
                hidden(1, 1, e1)
                output(0, e0)
                turn_x(2, 0)
                turn_h(1)
                hidden(2, 0, e2)
                output(1, e1)
                turn_x(3, 1)
                turn_h(2)
                with pe.Fori(1, 1 + LOOPS) as i:
                    t = 2 * i
                    e1 = expert(t + 1)
                    weights(e1)
                    hidden(t + 1, 1, e1)
                    output(t, expert(t))
                    e2 = expert(t + 2)
                    turn_x(t + 2, 0)
                    weights(e2)
                    turn_h(t + 1)
                    hidden(t + 2, 0, e2)
                    output(t + 1, e1)
                    turn_x(t + 3, 1)
                    turn_h(t + 2)
                for t in range(REST, TILES):
                    if t + 1 < TILES:
                        e1 = expert(t + 1)
                        weights(e1)
                        hidden(t + 1, (t + 1) % 2, e1)
                    output(t, expert(t))
                    if t + 2 < TILES:
                        turn_x(t + 2, t % 2)
                    if t + 1 < TILES:
                        turn_h(t + 1)

            expert_tiles(we)


_WEIGHTS = ["L0_attn_Wq", "L0_attn_Wk", "L0_attn_Wv", "L0_attn_Wo",
            "L0_xattn_Wq", "L0_xattn_Wk", "L0_xattn_Wv", "L0_xattn_Wo"]


def kernel(**inputs):
    import numpy as np
    import concourse.bacc as bacc
    from concourse.bass_utils import run_bass_kernel_spmd

    a = {n: np.asarray(v) for n, v in inputs.items()}
    lay = {"x": a["x"].reshape(T, D), "xT": a["x"].reshape(T, D).T, "cT": a["ctx_1024"].reshape(T, D).T}
    for n in _WEIGHTS:
        lay[n] = a[n].T if "xattn" in n else a[n]
    lay["brow"] = np.stack([a["L0_attn_bo"], a["L0_xattn_bv"], a["L0_xattn_bo"]])
    lay["bcol"] = np.stack([a[n] for n in ("L0_attn_bq", "L0_attn_bk", "L0_attn_bv", "L0_xattn_bq", "L0_xattn_bk")])
    lay["bcol"] = lay["bcol"].reshape(5 * KD, P).T
    lay["gate_w"], lay["gate_b"] = a["L0_ffn_gate_w"], a["L0_ffn_gate_b"]
    lay["w1"], lay["w2"], lay["b2"] = a["L0_ffn_w1"], a["L0_ffn_w2"], a["L0_ffn_b2"]
    lay["b1T"] = a["L0_ffn_b1"].reshape(E * NH, P).T
    lay["ws1"], lay["ws2"], lay["bs2"] = a["L0_ffn_ws1"], a["L0_ffn_ws2"], a["L0_ffn_bs2"]
    lay["bs1T"] = a["L0_ffn_bs1"].reshape(NH, P).T
    arrays = {f"in_{n}": np.ascontiguousarray(v) for n, v in lay.items()}

    nc = bacc.Bacc("TRN2", target_bir_lowering=False, num_devices=1)
    t = {n: nc.dram_tensor(f"in_{n}", arrays[f"in_{n}"].shape, F, kind="ExternalInput").ap() for n in lay}
    out = nc.dram_tensor("out", (T, D), F, kind="ExternalOutput").ap()
    build(nc, t["x"], t["xT"], t["cT"], [t[n] for n in _WEIGHTS], t["brow"], t["bcol"], t["gate_w"], t["gate_b"],
          t["w1"], t["b1T"], t["w2"], t["b2"], t["ws1"], t["bs1T"], t["ws2"], t["bs2"], out)
    r = run_bass_kernel_spmd(nc, [arrays], core_ids=[0])
    return r.results[0]["out"].reshape(B, S, D)
```
